# Optimizing a Trainium2 kernel written in Bass

```python
import numpy as np
import jax
import jax.numpy as jnp

def _softmax(x, axis=-1):
    return jax.nn.softmax(x, axis=axis)

def _gelu(x):
    return jax.nn.gelu(x, approximate=True)

def _silu(x):
    return jax.nn.silu(x)

def _sigmoid(x):
    return jax.nn.sigmoid(x)

def _layernorm(x, axis=-1, eps=1e-05):
    m = jnp.mean(x, axis=axis, keepdims=True)
    v = jnp.var(x, axis=axis, keepdims=True)
    return (x - m) / jnp.sqrt(v + eps)

def _scatter_add(tgt, idx, src, axis=0):
    return tgt.at[idx].add(src)

def _segment_sum(src, seg, n):
    return jax.ops.segment_sum(src, seg, n)
kernel_name = 'mk_flamingo_gated_d1_seqx_r2_dac643'

def setup_inputs(seed: int=0):
    np.random.seed(seed)
    _w = jnp.asarray

    def _rec_inputs():
        import jax
        import jax.numpy as jnp
        _rk = jax.random.key(seed)
        x = -0.0002928 + 1 * jax.random.normal(jax.random.fold_in(_rk, 1), (4, 1024, 512), jnp.float32)
        _lenS = 1024 - jax.random.randint(jax.random.fold_in(_rk, 7), (4,), 0, max(1, 1024 // 4) + 1, jnp.int32)
        _lenS2 = 1024 - jax.random.randint(jax.random.fold_in(_rk, 8), (4,), 0, max(1, 1024 // 4) + 1, jnp.int32)
        _ctx_1024P = jax.random.normal(jax.random.fold_in(_rk, 11), (4, 16, 512), jnp.float32)
        _ctx_1024c = jax.random.dirichlet(jax.random.fold_in(_rk, 511), 0.3 * jnp.ones((16,), jnp.float32), (4, 1024))
        _ctx_1024t = jnp.einsum('bsk,bkd->bsd', _ctx_1024c, _ctx_1024P)
        _ctx_1024t = _ctx_1024t * jax.lax.rsqrt(jnp.mean(jnp.square(_ctx_1024t)) + 1e-12) * 0.953939
        ctx_1024 = 4.13588e-05 + 0.999923 * (_ctx_1024t + 0.3 * jax.random.normal(jax.random.fold_in(_rk, 611), (4, 1024, 512), jnp.float32))
        itok_BxS_8_8191 = jax.random.randint(jax.random.fold_in(_rk, 12), (4, 1024), 8, 4096, jnp.int32)
        itok_BxS2_1_8191 = jax.random.randint(jax.random.fold_in(_rk, 13), (4, 1024), 1, 4096, jnp.int32)
        _validS = jnp.arange(1024)[None, :] < _lenS[:, None]
        _validS2 = jnp.arange(1024)[None, :] < _lenS2[:, None]
        _causal = jnp.tril(jnp.ones((1024, 1024), dtype=bool))
        mask_BxSxS2_if1 = jnp.where(jnp.ones((4, 1024, 1024), dtype=bool), 1, 0).astype(jnp.int32)
        _g = jax.random.normal(jax.random.fold_in(_rk, 9001), (2, 1), jnp.float32)
        _g = jnp.sign(_g) * jnp.maximum(jnp.abs(_g), 1.0) + (_g == 0) * 1.0
        g_xattn = _g[0]
        g_ffn = _g[1]
        return (x, ctx_1024, itok_BxS_8_8191, itok_BxS2_1_8191, mask_BxSxS2_if1, g_xattn, g_ffn)
    x, ctx_1024, itok_BxS_8_8191, itok_BxS2_1_8191, mask_BxSxS2_if1, g_xattn, g_ffn = _rec_inputs()

    def _L0_xattn_setup():
        import jax, jax.numpy as jnp
        import numpy as np
        DIM = 512
        NUM_HEADS = 16
        HEAD_DIM = DIM // NUM_HEADS

        def _slopes(num_heads):
            ratio = 2.0 ** (-8.0 / num_heads)
            return jnp.asarray([ratio ** i for i in range(1, num_heads + 1)], dtype=jnp.float32)
        key = jax.random.key(seed)
        ks = jax.random.split(key, 10)
        b, q_len, k_len = (2, 1024, 2048)
        query = jax.random.normal(ks[0], (b, q_len, DIM), dtype=jnp.float32)
        keys = jax.random.normal(ks[1], (b, k_len, DIM), dtype=jnp.float32)
        values = jax.random.normal(ks[2], (b, k_len, DIM), dtype=jnp.float32)
        query_pos = jnp.sort(jax.random.randint(ks[3], (b, q_len), 0, 4096), axis=-1)
        key_pos = jnp.sort(jax.random.randint(ks[4], (b, k_len), 0, 4096), axis=-1)
        mask = jnp.ones((b, q_len, k_len), dtype=jnp.int32)
        lim = float(np.sqrt(6.0 / (DIM + DIM)))
        W_q = jax.random.uniform(ks[5], (DIM, DIM), minval=-lim, maxval=lim, dtype=jnp.float32)
        W_k = jax.random.uniform(ks[6], (DIM, DIM), minval=-lim, maxval=lim, dtype=jnp.float32)
        W_v = jax.random.uniform(ks[7], (DIM, DIM), minval=-lim, maxval=lim, dtype=jnp.float32)
        W_o = jax.random.uniform(ks[8], (DIM, DIM), minval=-lim, maxval=lim, dtype=jnp.float32)
        return {'query': query, 'keys': keys, 'values': values, 'W_q': W_q, 'W_k': W_k, 'W_v': W_v, 'W_o': W_o, 'query_pos': query_pos, 'key_pos': key_pos, 'mask': mask}
    _L0_xattn_all = _L0_xattn_setup()
    _L0_xattn_in = {k: v for k, v in _L0_xattn_all.items() if k in ('W_q', 'W_k', 'W_v', 'W_o')}
    del _L0_xattn_all

    def _L0_ffn_setup():
        import jax, jax.numpy as jnp
        import numpy as np
        B, N, D = (4, 4096, 512)
        HEADS, DH = (8, 64)
        HID = HEADS * DH
        WIN = 128
        NQ, NKV = (512, 1024)
        EPS, N_ITERS, FETCH_K = (1.0, 50, 9.0 / 8.0)
        SCALE = DH ** (-0.5)

        def rmsnorm(x, gamma):
            norm = jnp.maximum(jnp.linalg.norm(x, axis=-1, keepdims=True), 1e-12)
            return x / norm * x.shape[-1] ** 0.5 * gamma

        def coor_descent(s, k):
            logk = jnp.log(jnp.asarray(k, s.dtype))

            def body(_, ab):
                a, b = ab
                a = EPS * (logk - jax.nn.logsumexp((s + b) / EPS, axis=-1, keepdims=True))
                b = -jax.nn.relu(s + a)
                return (a, b)
            a, b = jax.lax.fori_loop(0, N_ITERS, body, (jnp.zeros_like(s[..., :1]), -s))
            return jnp.exp((s + a + b) / EPS)

        def route(x, routing_token, num_tokens):
            s = jnp.einsum('bnd,d->bn', x, routing_token)
            k = min(num_tokens * FETCH_K, x.shape[1])
            scores = coor_descent(s, k)
            sel_scores, sel_idx = jax.lax.top_k(scores, num_tokens)
            sel_scores = sel_scores + jax.lax.stop_gradient(1.0 - sel_scores)
            return (sel_scores, sel_idx)

        def light_local_attn(x, gamma, wq, wkv, wo):
            b, n, d = x.shape
            xn = rmsnorm(x, gamma)
            q = xn @ wq
            k, v = jnp.split(xn @ wkv, 2, axis=-1)

            def win(t):
                return t.reshape(b, n // WIN, WIN, HEADS, DH).transpose(0, 1, 3, 2, 4)
            q, k, v = (win(q) * SCALE, win(k), win(v))
            attn = jax.nn.softmax(jnp.einsum('bwhid,bwhjd->bwhij', q, k), axis=-1)
            out = jnp.einsum('bwhij,bwhjd->bwhid', attn, v)
            out = out.transpose(0, 1, 3, 2, 4).reshape(b, n, HID)
            return out @ wo

        def heavy_attn(xq, context, scores_kv, gamma, wq, wkv_t, wo):
            b, nq, d = xq.shape
            nkv = context.shape[1]
            xqn = rmsnorm(xq, gamma)
            ctx = rmsnorm(context, gamma)[:, None]
            q = (xqn @ wq).reshape(b, nq, HEADS, DH).transpose(0, 2, 1, 3) * SCALE
            kvw = wkv_t.reshape(1, HEADS, 2 * DH, d)
            kv = jnp.einsum('rhdi,brni->brhnd', kvw, ctx)
            k, v = jnp.split(kv, 2, axis=-1)
            v = v * scores_kv[:, None, None, :, None]
            k = k.reshape(b, HEADS, nkv, DH)
            v = v.reshape(b, HEADS, nkv, DH)
            attn = jax.nn.softmax(jnp.einsum('bhid,bhjd->bhij', q, k), axis=-1)
            out = jnp.einsum('bhij,bhjd->bhid', attn, v)
            out = out.transpose(0, 2, 1, 3).reshape(b, nq, HID)
            return out @ wo
        key = jax.random.key(seed)
        ks = jax.random.split(key, 10)
        lin = lambda k, shape, fan: jax.random.normal(k, shape, jnp.float32) * fan ** (-0.5)
        return dict(x=jax.random.normal(ks[0], (B, N, D), jnp.float32), gamma_light=jnp.ones((D,), jnp.float32), wq_light=lin(ks[1], (D, HID), D), wkv_light=lin(ks[2], (D, 2 * HID), D), wo_light=lin(ks[3], (HID, D), HID), q_routing_token=jax.random.normal(ks[4], (D,), jnp.float32), kv_routing_token=jax.random.normal(ks[5], (D,), jnp.float32), gamma_heavy=jnp.ones((D,), jnp.float32), wq_heavy=lin(ks[6], (D, HID), D), wkv_heavy=lin(ks[7], (2 * HID, D), D), wo_heavy=lin(ks[8], (HID, D), HID))
    _L0_ffn_all = _L0_ffn_setup()
    _L0_ffn_in = {k: v for k, v in _L0_ffn_all.items() if k in ('gamma_light', 'wq_light', 'wkv_light', 'wo_light', 'q_routing_token', 'kv_routing_token', 'gamma_heavy', 'wq_heavy', 'wkv_heavy', 'wo_heavy')}
    del _L0_ffn_all
    return {'x': x, 'ctx_1024': ctx_1024, 'itok_BxS_8_8191': itok_BxS_8_8191, 'itok_BxS2_1_8191': itok_BxS2_1_8191, 'mask_BxSxS2_if1': mask_BxSxS2_if1, 'g_xattn': g_xattn, 'g_ffn': g_ffn, 'L0_xattn_W_q': _L0_xattn_in['W_q'], 'L0_xattn_W_k': _L0_xattn_in['W_k'], 'L0_xattn_W_v': _L0_xattn_in['W_v'], 'L0_xattn_W_o': _L0_xattn_in['W_o'], 'L0_ffn_gamma_light': _L0_ffn_in['gamma_light'], 'L0_ffn_wq_light': _L0_ffn_in['wq_light'], 'L0_ffn_wkv_light': _L0_ffn_in['wkv_light'], 'L0_ffn_wo_light': _L0_ffn_in['wo_light'], 'L0_ffn_q_routing_token': _L0_ffn_in['q_routing_token'], 'L0_ffn_kv_routing_token': _L0_ffn_in['kv_routing_token'], 'L0_ffn_gamma_heavy': _L0_ffn_in['gamma_heavy'], 'L0_ffn_wq_heavy': _L0_ffn_in['wq_heavy'], 'L0_ffn_wkv_heavy': _L0_ffn_in['wkv_heavy'], 'L0_ffn_wo_heavy': _L0_ffn_in['wo_heavy']}

def reference(x, ctx_1024, itok_BxS_8_8191, itok_BxS2_1_8191, mask_BxSxS2_if1, g_xattn, g_ffn, L0_xattn_W_q, L0_xattn_W_k, L0_xattn_W_v, L0_xattn_W_o, L0_ffn_gamma_light, L0_ffn_wq_light, L0_ffn_wkv_light, L0_ffn_wo_light, L0_ffn_q_routing_token, L0_ffn_kv_routing_token, L0_ffn_gamma_heavy, L0_ffn_wq_heavy, L0_ffn_wkv_heavy, L0_ffn_wo_heavy):
    import jax
    import jax.numpy as jnp

    def _L0_xattn_ref(query, keys, values, W_q, W_k, W_v, W_o, query_pos, key_pos, mask):
        import jax, jax.numpy as jnp
        import numpy as np
        DIM = 512
        NUM_HEADS = 16
        HEAD_DIM = DIM // NUM_HEADS

        def _slopes(num_heads):
            ratio = 2.0 ** (-8.0 / num_heads)
            return jnp.asarray([ratio ** i for i in range(1, num_heads + 1)], dtype=jnp.float32)
        b, q_len, _ = query.shape
        k_len = keys.shape[1]
        scale = 1.0 / np.sqrt(HEAD_DIM)
        Q = (query @ W_q.T).reshape(b, q_len, NUM_HEADS, HEAD_DIM).transpose(0, 2, 1, 3)
        K = (keys @ W_k.T).reshape(b, k_len, NUM_HEADS, HEAD_DIM).transpose(0, 2, 1, 3)
        V = (values @ W_v.T).reshape(b, k_len, NUM_HEADS, HEAD_DIM).transpose(0, 2, 1, 3)
        scores = jnp.einsum('bhqd,bhkd->bhqk', Q, K) * scale
        dist = (query_pos[:, :, None] - key_pos[:, None, :]).astype(scores.dtype)
        bias = -_slopes(NUM_HEADS)[None, :, None, None] * dist[:, None, :, :]
        scores = scores + bias
        scores = jnp.where(mask[:, None, :, :] == 0, -jnp.inf, scores)
        m = jnp.max(scores, axis=-1, keepdims=True)
        e = jnp.exp(scores - m)
        attn = e / (1.0 + jnp.sum(e, axis=-1, keepdims=True))
        out = jnp.einsum('bhqk,bhkd->bhqd', attn, V)
        out = out.transpose(0, 2, 1, 3).reshape(b, q_len, DIM)
        return out @ W_o.T

    def _L0_ffn_ref(x, gamma_light, wq_light, wkv_light, wo_light, q_routing_token, kv_routing_token, gamma_heavy, wq_heavy, wkv_heavy, wo_heavy):
        import jax, jax.numpy as jnp
        import numpy as np
        B, N, D = (4, 4096, 512)
        HEADS, DH = (8, 64)
        HID = HEADS * DH
        WIN = 128
        NQ, NKV = (512, 1024)
        EPS, N_ITERS, FETCH_K = (1.0, 50, 9.0 / 8.0)
        SCALE = DH ** (-0.5)

        def rmsnorm(x, gamma):
            norm = jnp.maximum(jnp.linalg.norm(x, axis=-1, keepdims=True), 1e-12)
            return x / norm * x.shape[-1] ** 0.5 * gamma

        def coor_descent(s, k):
            logk = jnp.log(jnp.asarray(k, s.dtype))

            def body(_, ab):
                a, b = ab
                a = EPS * (logk - jax.nn.logsumexp((s + b) / EPS, axis=-1, keepdims=True))
                b = -jax.nn.relu(s + a)
                return (a, b)
            a, b = jax.lax.fori_loop(0, N_ITERS, body, (jnp.zeros_like(s[..., :1]), -s))
            return jnp.exp((s + a + b) / EPS)

        def route(x, routing_token, num_tokens):
            s = jnp.einsum('bnd,d->bn', x, routing_token)
            k = min(num_tokens * FETCH_K, x.shape[1])
            scores = coor_descent(s, k)
            sel_scores, sel_idx = jax.lax.top_k(scores, num_tokens)
            sel_scores = sel_scores + jax.lax.stop_gradient(1.0 - sel_scores)
            return (sel_scores, sel_idx)

        def light_local_attn(x, gamma, wq, wkv, wo):
            b, n, d = x.shape
            xn = rmsnorm(x, gamma)
            q = xn @ wq
            k, v = jnp.split(xn @ wkv, 2, axis=-1)

            def win(t):
                return t.reshape(b, n // WIN, WIN, HEADS, DH).transpose(0, 1, 3, 2, 4)
            q, k, v = (win(q) * SCALE, win(k), win(v))
            attn = jax.nn.softmax(jnp.einsum('bwhid,bwhjd->bwhij', q, k), axis=-1)
            out = jnp.einsum('bwhij,bwhjd->bwhid', attn, v)
            out = out.transpose(0, 1, 3, 2, 4).reshape(b, n, HID)
            return out @ wo

        def heavy_attn(xq, context, scores_kv, gamma, wq, wkv_t, wo):
            b, nq, d = xq.shape
            nkv = context.shape[1]
            xqn = rmsnorm(xq, gamma)
            ctx = rmsnorm(context, gamma)[:, None]
            q = (xqn @ wq).reshape(b, nq, HEADS, DH).transpose(0, 2, 1, 3) * SCALE
            kvw = wkv_t.reshape(1, HEADS, 2 * DH, d)
            kv = jnp.einsum('rhdi,brni->brhnd', kvw, ctx)
            k, v = jnp.split(kv, 2, axis=-1)
            v = v * scores_kv[:, None, None, :, None]
            k = k.reshape(b, HEADS, nkv, DH)
            v = v.reshape(b, HEADS, nkv, DH)
            attn = jax.nn.softmax(jnp.einsum('bhid,bhjd->bhij', q, k), axis=-1)
            out = jnp.einsum('bhij,bhjd->bhid', attn, v)
            out = out.transpose(0, 2, 1, 3).reshape(b, nq, HID)
            return out @ wo
        b = x.shape[0]
        light_out = light_local_attn(x, gamma_light, wq_light, wkv_light, wo_light)
        scores_q, idx_q = route(x, q_routing_token, NQ)
        scores_kv, idx_kv = route(x, kv_routing_token, NKV)
        routed_q = jnp.take_along_axis(x, idx_q[..., None], axis=1)
        routed_kv = jnp.take_along_axis(x, idx_kv[..., None], axis=1)
        routed_out = heavy_attn(routed_q, routed_kv, scores_kv, gamma_heavy, wq_heavy, wkv_heavy, wo_heavy)
        routed_out = routed_out * scores_q[..., None]
        heavy_out = jnp.zeros_like(x).at[jnp.arange(b)[:, None], idx_q].set(routed_out)
        return light_out + heavy_out
    x = x + jnp.tanh(g_xattn[0]) * _L0_xattn_ref(_layernorm(x, axis=-1), ctx_1024, ctx_1024, L0_xattn_W_q, L0_xattn_W_k, L0_xattn_W_v, L0_xattn_W_o, itok_BxS_8_8191, itok_BxS2_1_8191, mask_BxSxS2_if1)
    x = x + jnp.tanh(g_ffn[0]) * _L0_ffn_ref(_layernorm(x, axis=-1), L0_ffn_gamma_light, L0_ffn_wq_light, L0_ffn_wkv_light, L0_ffn_wo_light, L0_ffn_q_routing_token, L0_ffn_kv_routing_token, L0_ffn_gamma_heavy, L0_ffn_wq_heavy, L0_ffn_wkv_heavy, L0_ffn_wo_heavy)
    return x

_drawn_inputs = setup_inputs


def setup_inputs(seed=0):
    import zlib

    import numpy as np

    out = dict(_drawn_inputs(seed))
    spreads = {'L0_ffn_gamma_light': (1.0, 0.2), 'L0_ffn_gamma_heavy': (1.0, 0.2)}
    factors = {}
    for name, (base, spread) in spreads.items():
        noise = np.random.default_rng([zlib.crc32(name.encode()), seed]).standard_normal(out[name].shape)
        drawn = base * np.exp(spread * noise) if base else spread * noise
        out[name] = jnp.asarray(drawn.astype(out[name].dtype))
    for name, factor in factors.items():
        out[name] = (out[name] * factor).astype(out[name].dtype)
    return out
```

```python
from contextlib import ExitStack

import numpy as np

import concourse.bass as bass
from concourse import mybir

F32 = mybir.dt.float32
F16 = mybir.dt.float16
I32 = mybir.dt.int32
ALU = mybir.AluOpType
ACT = mybir.ActivationFunctionType
AX = mybir.AxisListType

P = 128
B, S, D = 4, 1024, 512
NT = S // P
KT = D // P
XH, XD = 16, D // 16
GH = P // XD
NG = XH // GH
FH, FD = 8, D // 8
HP = FH // 2
NQ = 512
LN_EPS = 1e-5
MASKED = 1e30
ITERS = 50
LOG_KQ = float(np.log(np.float32(min(NQ * 9.0 / 8.0, S))))
LOG_KKV = float(np.log(np.float32(min(S * 9.0 / 8.0, S))))
OUT_OF_RANGE = 1 << 20


def slope(h):
    return float(np.float32(2.0 ** (-8.0 / XH)) ** (h + 1))


class Memory:

    def __init__(self, nc, ctx, phase):
        self.nc, self.ctx, self.phase = nc, ctx, phase

    def sb(self, name, shape, dt=F32):
        return self.ctx.enter_context(self.nc.sbuf_tensor(f"{self.phase}_{name}", shape, dt))

    def ps(self, name, shape, dt=F32):
        return self.ctx.enter_context(self.nc.psum_tensor(f"{self.phase}_{name}", shape, dt))

    def sem(self, name):
        return self.ctx.enter_context(self.nc.semaphore(f"{self.phase}_{name}"))


def prime(eng, *sems):
    for sem in sems:
        eng.sem_inc(sem, 1)


def after(eng, sem, count):
    eng.wait_ge(sem, count + 1)


def alone(eng, passed):
    eng.sem_inc(passed, 1)


class Chain:

    def __init__(self, eng, sem, base=0):
        self.eng, self.sem, self.base, self.n = eng, sem, base, 0

    def mark(self, ins):
        ins.then_inc(self.sem, 1)
        self.n += 1
        return self.base + self.n

    def wait(self):
        self.eng.wait_ge(self.sem, self.base + self.n)


def prepare_weights(nc, t, keep):
    with ExitStack() as ctx:
        m = Memory(nc, ctx, "w")
        natural = m.sb("natural", [P, 6, KT, D])
        turned = m.sb("turned", [P, 5, KT, D])
        q_scale = m.sb("q_scale", [P, KT])
        wqh = m.sb("wqh", [P, KT, D])
        light_w = m.sb("light_w", [P, 3, KT, D])
        gam = m.sb("gam", [P, 2, KT])
        gate_in = m.sb("gate_in", [P, 2])
        tp = m.ps("tp", [P, 2, KT, P])
        loaded = m.sem("loaded")
        small_loaded = m.sem("small_loaded")
        ident_made = m.sem("ident_made")
        consts_made = m.sem("consts_made")
        scaled = m.sem("scaled")
        transposed = m.sem("transposed")
        copied = m.sem("copied")
        stored = m.sem("stored")
        gated = m.sem("gated")
        block = ctx.enter_context(nc.Block())
        N_TURN = 6 * KT

        @block.sync
        def _(sp):
            for i, w in enumerate(("L0_xattn_W_q", "L0_xattn_W_k", "L0_xattn_W_v", "L0_xattn_W_o")):
                sp.dma_start(natural[:, i], t[w].rearrange("(o p) d -> p o d", p=P)).then_inc(loaded, 16)
            for i in range(2):
                sp.dma_start(natural[:, 4 + i],
                             t["L0_ffn_wkv_heavy"][i * D:(i + 1) * D, :].rearrange("(o p) d -> p o d", p=P)
                             ).then_inc(loaded, 16)
            sp.dma_start(wqh[:], t["L0_ffn_wq_heavy"].rearrange("(k p) o -> p k o", p=P)).then_inc(loaded, 16)
            sp.dma_start(light_w[:, 0], t["L0_ffn_wq_light"].rearrange("(k p) o -> p k o", p=P)).then_inc(loaded, 16)
            for i in range(2):
                sp.dma_start(light_w[:, 1 + i],
                             t["L0_ffn_wkv_light"][:, i * D:(i + 1) * D].rearrange("(k p) o -> p k o", p=P)
                             ).then_inc(loaded, 16)
            sp.wait_ge(copied, N_TURN)
            for i in range(3):
                for g in range(NG):
                    sp.dma_start(t["xattn_wt"][g, i], turned[:, i, :, g * P:(g + 1) * P]).then_inc(stored, 16)
            for hp in range(HP):
                half, at = hp // 2, (hp % 2) * 2 * P
                cols = turned[:, 3 + half, :, at:at + 2 * P].rearrange("p k (h s d) -> p k h s d", h=2, s=2)
                for s in range(2):
                    for h in range(2):
                        sp.dma_start(t["heavy_wt"][hp, 1 + s, :, :, h * FD:(h + 1) * FD],
                                     cols[:, :, h, s]).then_inc(stored, 16)
            sp.wait_ge(scaled, 1 + KT * 5)
            for hp in range(HP):
                sp.dma_start(t["heavy_wt"][hp, 0], wqh[:, :, hp * P:(hp + 1) * P]).then_inc(stored, 16)
            sp.dma_start(t["light_wt"].rearrange("i p k o -> p i k o"), light_w[:]).then_inc(stored, 16)
            sp.wait_ge(stored, 16 * (3 * NG + HP * 4 + HP + 1))

        @block.gpsimd
        def _(pool):
            nc.gpsimd.memset(keep["ident"][:], 0.0).then_inc(ident_made, 1)
            pool.wait_ge(ident_made, 1)
            nc.gpsimd.affine_select(out=keep["ident"][:], in_=keep["ident"][:], compare_op=ALU.not_equal, fill=1.0,
                                    base=0, pattern=[[-1, P]], channel_multiplier=1).then_inc(ident_made, 1)
            nc.gpsimd.memset(keep["ones"][:], 1.0).then_inc(consts_made, 1)
            nc.gpsimd.memset(keep["minus_half"][:], -0.5).then_inc(consts_made, 1)
            for h in range(XH):
                nc.gpsimd.memset(keep["slopes"][:, h:h + 1], slope(h)).then_inc(consts_made, 1)
            nc.gpsimd.memset(keep["before"][:], 1.0).then_inc(consts_made, 1)
            nc.gpsimd.memset(keep["after"][:], 1.0).then_inc(consts_made, 1)
            pool.wait_ge(consts_made, XH + 4)
            nc.gpsimd.affine_select(out=keep["before"][:], in_=keep["before"][:], compare_op=ALU.is_gt, fill=0.0,
                                    base=0, pattern=[[-1, P]], channel_multiplier=1).then_inc(consts_made, 1)
            nc.gpsimd.affine_select(out=keep["after"][:], in_=keep["after"][:], compare_op=ALU.is_gt, fill=0.0,
                                    base=0, pattern=[[1, P]], channel_multiplier=-1).then_inc(consts_made, 1)

        @block.scalar
        def _(act):
            for i, n in enumerate(("g_xattn", "g_ffn")):
                act.dma_start(gate_in[:, i:i + 1], t[n].rearrange("(a n) -> a n", a=1).to_broadcast([P, 1])
                              ).then_inc(small_loaded, 16)
            for i, n in enumerate(("L0_ffn_gamma_light", "L0_ffn_gamma_heavy")):
                act.dma_start(gam[:, i], t[n].rearrange("(k p) -> p k", p=P),
                              allow_slow_non_contiguous=True).then_inc(small_loaded, 16)
            for i, n in enumerate(("L0_ffn_q_routing_token", "L0_ffn_kv_routing_token")):
                act.dma_start(keep["tokens"][:, i], t[n].rearrange("(a n) -> a n", a=1).to_broadcast([P, D])
                              ).then_inc(small_loaded, 16)
            act.wait_ge(small_loaded, 96)
            act.activation(keep["gates"][:], gate_in[:], ACT.Tanh).then_inc(gated, 1)
            for n in range(N_TURN):
                which, kt = divmod(n, KT)
                act.wait_ge(transposed, n + 1)
                dst = keep["wo_t"][:, kt] if which == 3 else turned[:, which - (which > 3), kt]
                if which >= 4:
                    act.activation(dst, tp[:, n % 2].rearrange("p o c -> p (o c)"), ACT.Copy,
                                   scale=gam[:, 1, kt:kt + 1]).then_inc(copied, 1)
                else:
                    act.activation(dst, tp[:, n % 2].rearrange("p o c -> p (o c)"), ACT.Copy).then_inc(copied, 1)

        @block.vector
        def _(dve):
            for o in range(KT):
                for j in range(GH):
                    ins = dve.memset(q_scale[j * XD:(j + 1) * XD, o:o + 1],
                                     -(1.0 / np.sqrt(XD)) / slope(o * GH + j))
            ins.then_inc(scaled, 1)
            dve.wait_ge(scaled, 1)
            dve.wait_ge(loaded, 160)
            for o in range(KT):
                dve.tensor_scalar(natural[:, 0, o], natural[:, 0, o], q_scale[:, o:o + 1], None,
                                  ALU.mult).then_inc(scaled, 1)
            dve.wait_ge(small_loaded, 96)
            for k in range(KT):
                dve.tensor_scalar(wqh[:, k], wqh[:, k], gam[:, 1, k:k + 1], -float(FD) ** -0.5,
                                  ALU.mult, ALU.mult).then_inc(scaled, 1)
                for i in range(3):
                    dve.tensor_scalar(light_w[:, i, k], light_w[:, i, k], gam[:, 0, k:k + 1], None,
                                      ALU.mult).then_inc(scaled, 1)

        @block.tensor
        def _(pe):
            pe.wait_ge(ident_made, 2)
            pe.wait_ge(loaded, 160)
            pe.wait_ge(scaled, 1 + KT)
            for n in range(N_TURN):
                which, kt = divmod(n, KT)
                if n >= 2:
                    pe.wait_ge(copied, n - 1)
                for o in range(KT):
                    ins = pe.transpose(tp[:, n % 2, o], natural[:, which, o, kt * P:(kt + 1) * P], keep["ident"][:])
                ins.then_inc(transposed, 1)




def cross_attention(nc, t, keep, batches=B):
    with ExitStack() as ctx:
        m = Memory(nc, ctx, "x")
        ctx_t = m.sb("ctx_t", [P, KT, S])
        xn_t = m.sb("xn_t", [P, KT, S])
        dist = m.sb("dist", [P, NT, S])
        prob = m.sb("prob", [P, 3, S])
        prob_t = m.sb("prob_t", [P, 2, GH, NT, 2 * P])
        attn_t = m.sb("attn_t", [P, NG, S])
        wg = m.sb("wg", [P, 3, KT, P])
        q_part = m.sb("q_part", [P, 2, S], F16)
        k_part = m.sb("k_part", [P, 2, S], F16)
        q_stack = m.sb("q_stack", [P, GH, S], F16)
        k_stack = m.sb("k_stack", [P, GH, S], F16)
        v_g = m.sb("v_g", [P, NT, P])
        neg_max = m.sb("neg_max", [P, NT * GH])
        row_sum = m.sb("row_sum", [P, NT * GH])
        den_wide = m.sb("den_wide", [P, 2, GH, XD])
        den = m.sb("den", [P, 2, GH])
        inv = m.sb("inv", [P, 2, GH])
        den_t = m.sb("den_t", [P, 2 * P])
        slope_g = m.sb("slope_g", [P, GH])
        stats = m.sb("stats", [P, NT, 6])
        mean_var = m.sb("mean_var", [P, NT, 2])
        small = m.sb("small", [P, 6, NT])
        route = m.sb("route", [P, 2, NT])
        pos_i = m.sb("pos_i", [P, NT], I32)
        pos_f = m.sb("pos_f", [P, NT])
        flat = prob_t[:].rearrange("p a b c d -> p (a b c d)")
        xs = flat[:, 0:NT * D].rearrange("p (t d) -> p t d", d=D)
        cs = flat[:, NT * D:2 * NT * D].rearrange("p (t d) -> p t d", d=D)
        mask = flat[:, 2 * NT * D:2 * NT * D + NT * S].bitcast(I32).rearrange("p (t s) -> p t s", s=S)
        junk = flat[:, 2 * NT * D:2 * NT * D + D]
        kpos_i = prob[:, 0].bitcast(I32)
        kpos_neg = prob[:, 1]

        score_ps = m.ps("score_ps", [P, 2, S])
        turn_ps = m.ps("turn_ps", [P, 2, KT, P])
        attn_ps = m.ps("attn_ps", [P, 512])
        den_ps = m.ps("den_ps", [P, 512])

        x_in, c_in, mask_in, pos_in = m.sem("x_in"), m.sem("c_in"), m.sem("mask_in"), m.sem("pos_in")
        x_again, w_in, stack_in, out_stored = m.sem("x_again"), m.sem("w_in"), m.sem("stack_in"), m.sem("out_stored")
        dve_did, pool_did = m.sem("dve_did"), m.sem("pool_did")
        turned, turned_out = m.sem("turned"), m.sem("turned_out")
        k_made, q_made, v_made = m.sem("k_made"), m.sem("q_made"), m.sem("v_made")
        high_done, low_done, v_out = m.sem("high_done"), m.sem("low_done"), m.sem("v_out")
        slope_set = m.sem("slope_set")
        scored, biased, exped = m.sem("scored"), m.sem("biased"), m.sem("exped")
        turn_a, turn_b, out_a, out_b = m.sem("turn_a"), m.sem("turn_b"), m.sem("out_a"), m.sem("out_b")
        den_made = m.sem("den_made")
        inverted = m.sem("inverted")
        widened, den_turned, den_out = m.sem("widened"), m.sem("den_turned"), m.sem("den_out")
        attended, normed = m.sem("attended"), m.sem("normed")
        projected, x1_made = m.sem("projected"), m.sem("x1_made")
        passed = m.sem("passed")
        block = ctx.enter_context(nc.Block())

        STEPS = NT * GH
        PAIRS = NT // 2
        PER_PAIR = 2 * GH
        LN_MARKS = 3 * NT + 1
        TO_END = LN_MARKS + 2 + 2 * NT
        TO_SQUARES = TO_END + LN_MARKS + NT + 1
        DVE_BATCH = TO_SQUARES + 2 * NT + 1 + NT
        POOL_BATCH = 3
        TURNS = 3 * NT

        @block.sync
        def _(sp):
            with sp.Fori(0, batches) as b:
                sp.dma_start(cs, t["ctx_1024"][bass.ds(b, 1)].rearrange("a (t p) d -> p (a t) d", p=P)).then_inc(c_in, 16)
                sp.dma_start(xs, t["x"][bass.ds(b, 1)].rearrange("a (t p) d -> p (a t) d", p=P)).then_inc(x_in, 16)
                sp.dma_start(kpos_i, t["itok_BxS2_1_8191"][bass.ds(b, 1)].to_broadcast([P, S])).then_inc(pos_in, 16)
                sp.dma_start(pos_i[:], t["itok_BxS_8_8191"][bass.ds(b, 1)].rearrange("a (t p) -> p (a t)", p=P),
                             allow_slow_non_contiguous=True).then_inc(pos_in, 16)
                sp.dma_start(mask, t["mask_BxSxS2_if1"][bass.ds(b, 1)].rearrange("a (t p) s -> p (a t) s", p=P)
                             ).then_inc(mask_in, 16)
                with sp.Fori(0, NG) as g:
                    it = b * NG + g
                    after(sp, v_made, it * NT)
                    alone(sp, passed)
                    after(sp, q_made, it * 2)
                    sp.dma_start(wg[:], t["xattn_wt"][bass.ds(g, 1)].rearrange("a i p k o -> p (a i) k o")
                                 ).then_inc(w_in, 16)
                    after(sp, scored, it * STEPS)
                    sp.wait_ge(low_done, it * 4 + 4)
                    sp.wait_ge(high_done, it * 4 + 4)
                    for r in range(4):
                        for part, stack, which in ((k_part, k_stack, r // 2), (q_part, q_stack, r % 2)):
                            for j in range(GH):
                                sp.dma_start(stack[r * XD:(r + 1) * XD, j],
                                             part[j * XD:(j + 1) * XD, which]).then_inc(stack_in, 16)
                after(sp, attended, (b + 1) * NG * PAIRS)
                sp.dma_start(xs, t["x"][bass.ds(b, 1)].rearrange("a (t p) d -> p (a t) d", p=P)).then_inc(x_again, 16)
                sp.wait_ge(dve_did, (b + 1) * DVE_BATCH)
                sp.dma_start(t["x1"][bass.ds(b, 1)].rearrange("a (t p) d -> p (a t) d", p=P), cs).then_inc(out_stored, 16)
                sp.dma_start(t["yn"][bass.ds(b, 1)].rearrange("a (t p) d -> p (a t) d", p=P), xs).then_inc(out_stored, 16)
                after(sp, turned_out, (b + 1) * TURNS)
                sp.dma_start(t["yn_t"][bass.ds(b, 1)].rearrange("a p k s -> p (a k) s"), xn_t[:]).then_inc(out_stored, 16)
                sp.wait_ge(out_stored, (b + 1) * 48)
                alone(sp, passed)

        @block.gpsimd
        def _(pool):
            prime(pool, widened)
            with pool.Fori(0, batches) as b:
                def power(slot, at):
                    pool.wait_ge(dve_did, b * DVE_BATCH + at)
                    nc.gpsimd.tensor_tensor(small[:, slot + 1], small[:, slot], keep["minus_half"][:], ALU.pow
                                            ).then_inc(pool_did, 1)
                power(0, 2 * NT + 1)
                with pool.Fori(0, NG) as g:
                    it = b * NG + g
                    for qt in range(NT):
                        pool.wait_ge(exped, it * STEPS + (qt + 1) * GH)
                        after(pool, den_turned, it * NT + max(qt - 1, 0))
                        alone(pool, passed)
                        nc.gpsimd.tensor_scalar(den[:, qt % 2], row_sum[:, qt * GH:(qt + 1) * GH], 1.0, 1.0,
                                                ALU.add, ALU.mult).then_inc(den_made, 1)
                        pool.wait_ge(inverted, it * NT + qt + 1)
                        alone(pool, passed)
                        nc.gpsimd.tensor_scalar(den_wide[:, qt % 2],
                                                inv[:, qt % 2].unsqueeze(2).to_broadcast([P, GH, XD]), 1.0, 1.0,
                                                ALU.mult, ALU.mult).then_inc(widened, 1)
                power(2, TO_END + 2 * NT + 1)
                power(4, TO_SQUARES)

        @block.scalar
        def _(act):
            prime(act, turned_out, out_a, den_out)
            with act.Fori(0, batches) as b:
                def turn_out(first, dst, b=b):
                    for i in range(NT):
                        act.wait_ge(turned, b * TURNS + first + i + 1)
                        act.activation(dst[:, :, i * P:(i + 1) * P], turn_ps[:, i % 2], ACT.Copy).then_inc(turned_out, 1)
                turn_out(0, ctx_t)
                turn_out(NT, xn_t)
                with act.Fori(0, NG) as g:
                    it = b * NG + g
                    after(act, scored, it * STEPS)
                    for n in range(4):
                        part, c = (k_part, q_part)[n // 2], n % 2
                        after(act, (k_made, q_made)[n // 2], it * 2 + c + 1)
                        act.activation(part[:, 0, c * 512:(c + 1) * 512], score_ps[:, n // 2, c * 512:(c + 1) * 512],
                                       ACT.Copy).then_inc(high_done, 1)
                    after(act, attended, it * PAIRS)
                    for c in range(2):
                        after(act, v_made, it * NT + 4 * c + 4)
                        act.activation(v_g[:, 4 * c:4 * c + 4], turn_ps[:, c], ACT.Copy).then_inc(v_out, 1)
                    def expo(s):
                        after(act, biased, it * STEPS + s + 1)
                        act.activation(prob[:, s % 3], prob[:, s % 3], ACT.Exp, scale=-1.0, bias=neg_max[:, s:s + 1],
                                       accum_out=row_sum[:, s:s + 1]).then_inc(exped, 1)

                    def inverse_out(pair):
                        after(act, den_turned, it * NT + 2 * pair + 2)
                        after(act, normed, it * PAIRS + pair)
                        act.activation(den_t[:], den_ps[:, 0:2 * P], ACT.Copy).then_inc(den_out, 1)
                    expo(0)
                    for s in range(STEPS):
                        qt, j = divmod(s, GH)
                        pair, half = divmod(qt, 2)
                        if s + 1 < STEPS:
                            expo(s + 1)
                        if s % PER_PAIR == 0:
                            after(act, attended, it * PAIRS + max(pair - 1, 0))
                        act.wait_ge(turn_a, it * STEPS + s + 1)
                        act.activation(prob_t[:, pair % 2, j, 0:4, half * P:(half + 1) * P], turn_ps[:, 0],
                                       ACT.Copy).then_inc(out_a, 1)
                        if s % PER_PAIR == 2 and pair:
                            inverse_out(pair - 1)
                    inverse_out(PAIRS - 1)
                turn_out(2 * NT, xn_t)

        @block.vector
        def _(dve):
            prime(dve, normed, biased, x1_made, out_b)
            with dve.Fori(0, batches) as b:
                done = Chain(dve, dve_did, b * DVE_BATCH)

                def layer_norm(rows, slot):
                    for i in range(NT):
                        done.mark(dve.bn_stats(stats[:, i], rows[:, i]))
                    done.wait()
                    alone(dve, passed)
                    for i in range(NT):
                        done.mark(dve.bn_aggr(mean_var[:, i], stats[:, i]))
                    done.wait()
                    done.mark(dve.tensor_scalar(small[:, slot], mean_var[:, :, 1], LN_EPS, None, ALU.add))
                    dve.wait_ge(pool_did, b * POOL_BATCH + slot // 2 + 1)
                    for i in range(NT):
                        done.mark(dve.tensor_scalar(xs[:, i], rows[:, i], mean_var[:, i, 0:1],
                                                    small[:, slot + 1, i:i + 1], ALU.subtract, ALU.mult))

                dve.wait_ge(x_in, (b + 1) * 16)
                layer_norm(xs, 0)
                dve.wait_ge(pos_in, (b + 1) * 32)
                done.mark(dve.tensor_scalar(kpos_neg, kpos_i, -1.0, None, ALU.mult))
                done.mark(dve.tensor_copy(pos_f[:], pos_i[:]))
                dve.wait_ge(mask_in, (b + 1) * 16)
                for i in range(NT):
                    done.mark(dve.tensor_scalar(dist[:, i], mask[:, i], 0.0, MASKED, ALU.is_equal, ALU.mult))
                done.wait()
                for i in range(NT):
                    done.mark(dve.scalar_tensor_tensor(dist[:, i], kpos_neg, pos_f[:, i:i + 1], dist[:, i],
                                                       ALU.add, ALU.add))
                done.wait()
                alone(dve, passed)

                with dve.Fori(0, NG) as g:
                    it = b * NG + g
                    after(dve, biased, it * STEPS)
                    dve.tensor_copy(slope_g[:], keep["slopes"][:, bass.ds(g * GH, GH)]).then_inc(slope_set, 1)
                    for n in range(4):
                        part, c = (k_part, q_part)[n // 2], n % 2
                        dve.wait_ge(high_done, it * 4 + n + 1)
                        dve.tensor_tensor(part[:, 1, c * 512:(c + 1) * 512], score_ps[:, n // 2, c * 512:(c + 1) * 512],
                                          part[:, 0, c * 512:(c + 1) * 512], ALU.subtract).then_inc(low_done, 1)
                    dve.wait_ge(slope_set, it + 1)

                    def bias(s):
                        qt, j = divmod(s, GH)
                        after(dve, scored, it * STEPS + s + 1)
                        if s >= 3:
                            dve.wait_ge(turn_b, it * STEPS + s - 2)
                        alone(dve, passed)
                        dve.tensor_tensor_reduce(out=prob[:, s % 3], in0=dist[:, qt], in1=score_ps[:, s % 2],
                                                 scale=slope_g[:, j:j + 1], scalar=3.0e38, op0=ALU.add, op1=ALU.min,
                                                 accum_out=neg_max[:, s:s + 1]).then_inc(biased, 1)

                    def invert(qt):
                        dve.wait_ge(den_made, it * NT + qt + 1)
                        after(dve, widened, it * NT + max(qt - 1, 0))
                        dve.reciprocal(inv[:, qt % 2], den[:, qt % 2]).then_inc(inverted, 1)

                    def norm(pair):
                        after(dve, attended, it * PAIRS + pair + 1)
                        after(dve, den_out, it * PAIRS + pair + 1)
                        dve.tensor_tensor(attn_t[:, bass.ds(g, 1), pair * 2 * P:(pair + 1) * 2 * P],
                                          attn_ps[:, 0:2 * P].unsqueeze(1), den_t[:].unsqueeze(1),
                                          ALU.mult).then_inc(normed, 1)
                    bias(0)
                    bias(1)
                    for s in range(STEPS):
                        qt, j = divmod(s, GH)
                        pair, half = divmod(qt, 2)
                        if s % PER_PAIR == 0:
                            after(dve, attended, it * PAIRS + max(pair - 1, 0))
                        dve.wait_ge(turn_b, it * STEPS + s + 1)
                        dve.tensor_copy(prob_t[:, pair % 2, j, 4:8, half * P:(half + 1) * P], turn_ps[:, 1]
                                        ).then_inc(out_b, 1)
                        if s + 2 < STEPS:
                            bias(s + 2)
                        if s and j == 0:
                            invert(qt - 1)
                        if s % PER_PAIR == 3 and pair:
                            norm(pair - 1)
                    invert(NT - 1)
                    norm(PAIRS - 1)

                dve.wait_ge(x_again, (b + 1) * 16)
                for i in range(NT):
                    dve.wait_ge(projected, b * NT + i + 1)
                    dve.scalar_tensor_tensor(cs[:, i], score_ps[:, i % 2, 0:D], keep["gates"][:, 0:1], xs[:, i],
                                             ALU.mult, ALU.add).then_inc(x1_made, 1)
                after(dve, x1_made, (b + 1) * NT)
                layer_norm(cs, 2)
                done.wait()
                for i in range(NT):
                    done.mark(dve.tensor_tensor_reduce(out=junk, in0=xs[:, i], in1=xs[:, i], scale=1.0, scalar=0.0,
                                                       op0=ALU.mult, op1=ALU.add, accum_out=mean_var[:, i, 0:1]))
                    done.wait()
                done.mark(dve.tensor_scalar(small[:, 4], mean_var[:, :, 0], 1e-24, 1.0 / D, ALU.max, ALU.mult))
                for w in range(2):
                    for i in range(NT):
                        done.mark(dve.tensor_tensor_reduce(out=junk, in0=xs[:, i], in1=keep["tokens"][:, w], scale=1.0,
                                                           scalar=0.0, op0=ALU.mult, op1=ALU.add,
                                                           accum_out=route[:, w, i:i + 1]))
                        done.wait()
                done.mark(dve.tensor_copy(keep["route_s"][:, :, bass.ds(b, 1), :], route[:].unsqueeze(2)))
                dve.wait_ge(pool_did, (b + 1) * POOL_BATCH)
                for i in range(NT):
                    done.mark(dve.tensor_scalar(xs[:, i], xs[:, i], small[:, 5, i:i + 1], None, ALU.mult))
                assert done.n == DVE_BATCH

        @block.tensor
        def _(pe):
            prime(pe, v_made, k_made, q_made, scored, attended, den_turned)
            with pe.Fori(0, batches) as b:
                def turn_rows(first, rows):
                    for i in range(NT):
                        if i >= 2:
                            after(pe, turned_out, b * TURNS + first + i - 1)
                        for k in range(KT):
                            ins = pe.transpose(turn_ps[:, i % 2, k], rows[:, i, k * P:(k + 1) * P], keep["ident"][:])
                        ins.then_inc(turned, 1)
                after(pe, turned_out, b * TURNS)
                pe.wait_ge(c_in, (b + 1) * 16)
                turn_rows(0, cs)
                after(pe, turned_out, b * TURNS + NT)
                pe.wait_ge(dve_did, b * DVE_BATCH + 3 * NT + 1)
                turn_rows(NT, xs)
                after(pe, turned_out, b * TURNS + 2 * NT)
                alone(pe, passed)
                with pe.Fori(0, NG) as g:
                    it = b * NG + g
                    pe.wait_ge(w_in, (it + 1) * 16)
                    after(pe, biased, it * STEPS)
                    after(pe, x1_made, b * NT)
                    for n in range(4):
                        w, src, made = ((1, ctx_t, k_made), (0, xn_t, q_made))[n // 2]
                        c = n % 2
                        for k in range(KT):
                            ins = pe.matmul(score_ps[:, n // 2, c * 512:(c + 1) * 512], wg[:, w, k],
                                            src[:, k, c * 512:(c + 1) * 512], start=k == 0, stop=k == KT - 1)
                        ins.then_inc(made, 1)
                    after(pe, out_a, it * STEPS)
                    after(pe, out_b, it * STEPS)
                    for i in range(NT):
                        for k in range(KT):
                            ins = pe.matmul(turn_ps[:, i // 4, i % 4], ctx_t[:, k, i * P:(i + 1) * P], wg[:, 2, k],
                                            start=k == 0, stop=k == KT - 1)
                        ins.then_inc(v_made, 1)
                    pe.wait_ge(stack_in, (it + 1) * 512)
                    pe.wait_ge(low_done, it * 4 + 4)
                    pe.wait_ge(v_out, it * 2 + 2)

                    def score(s):
                        qt, j = divmod(s, GH)
                        if s >= 2:
                            after(pe, biased, it * STEPS + s - 1)
                        for c in range(2):
                            ins = pe.matmul(score_ps[:, s % 2, c * 512:(c + 1) * 512], q_stack[:, j, qt * P:(qt + 1) * P],
                                            k_stack[:, j, c * 512:(c + 1) * 512], start=True, stop=True)
                        ins.then_inc(scored, 1)

                    def turn_inverse(qt):
                        after(pe, widened, it * NT + qt + 1)
                        after(pe, den_out, it * PAIRS + qt // 2)
                        pe.transpose(den_ps[:, (qt % 2) * P:(qt % 2 + 1) * P],
                                     den_wide[:, qt % 2].rearrange("p h d -> p (h d)"), keep["ident"][:]
                                     ).then_inc(den_turned, 1)

                    def attend(pair):
                        after(pe, out_a, it * STEPS + (pair + 1) * PER_PAIR)
                        after(pe, out_b, it * STEPS + (pair + 1) * PER_PAIR)
                        after(pe, normed, it * PAIRS + pair)
                        for k in range(NT):
                            for j in range(GH):
                                ins = pe.matmul(attn_ps[j * XD:(j + 1) * XD, 0:2 * P], v_g[:, k, j * XD:(j + 1) * XD],
                                                prob_t[:, pair % 2, j, k], start=k == 0, stop=k == NT - 1)
                        ins.then_inc(attended, 1)

                    score(0)
                    score(1)
                    for s in range(STEPS):
                        pe.wait_ge(exped, it * STEPS + s + 1)
                        for h, (sem, out) in enumerate(((turn_a, out_a), (turn_b, out_b))):
                            after(pe, out, it * STEPS + s)
                            for k in range(4):
                                ins = pe.transpose(turn_ps[:, h, k], prob[:, s % 3, (4 * h + k) * P:(4 * h + k + 1) * P],
                                                   keep["ident"][:])
                            ins.then_inc(sem, 1)
                        if s + 2 < STEPS:
                            score(s + 2)
                        if s > GH and s % GH == 1:
                            turn_inverse(s // GH - 1)
                        if s % PER_PAIR == 0 and s:
                            attend(s // PER_PAIR - 1)
                    turn_inverse(NT - 1)
                    attend(PAIRS - 1)
                after(pe, normed, (b + 1) * NG * PAIRS)
                after(pe, biased, (b + 1) * NG * STEPS)
                for i in range(NT):
                    if i >= 2:
                        after(pe, x1_made, b * NT + i - 1)
                    for k in range(KT):
                        ins = pe.matmul(score_ps[:, i % 2, 0:D], attn_t[:, k, i * P:(i + 1) * P], keep["wo_t"][:, k],
                                        start=k == 0, stop=k == KT - 1)
                    ins.then_inc(projected, 1)
                pe.wait_ge(dve_did, (b + 1) * DVE_BATCH)
                after(pe, out_a, (b + 1) * NG * STEPS)
                after(pe, out_b, (b + 1) * NG * STEPS)
                turn_rows(2 * NT, xs)


def light_attention(nc, t, keep):
    with ExitStack() as ctx:
        m = Memory(nc, ctx, "l")
        W = D // P
        w_qkv = m.sb("w_qkv", [P, 3, KT, D])
        w_o = m.sb("w_o", [P, KT, D])
        y_t = m.sb("y_t", [P, 2, KT, D])
        x1 = m.sb("x1", [P, 2, W, D])
        qk_t = m.sb("qk_t", [P, 2, KT, D])
        v = m.sb("v", [P, W, D])
        prob = m.sb("prob", [P, 2, 2, HP, P])
        prob_t = m.sb("prob_t", [P, 2, 2, HP, P])
        attn_t = m.sb("attn_t", [P, 2, HP, P])
        top = m.sb("top", [P, 2, FH])
        total = m.sb("total", [P, 2, FH])
        inv = m.sb("inv", [P, 2, FH])
        score_ps = m.ps("score_ps", [P, 2, HP, P])
        turn_ps = m.ps("turn_ps", [P, 2, HP, P])
        attn_ps = m.ps("attn_ps", [P, HP, P])
        proj_ps = m.ps("proj_ps", [P, 2, D])
        w_in, stored, passed = m.sem("w_in"), m.sem("stored"), m.sem("passed")
        y_in = [m.sem(f"y_in{half}") for half in range(2)]
        x_in = [m.sem(f"x_in{half}") for half in range(2)]
        projected, proj_out = m.sem("projected"), m.sem("proj_out")
        scored, topped, shifted, exped = m.sem("scored"), m.sem("topped"), m.sem("shifted"), m.sem("exped")
        summed, inverted, scaled = m.sem("summed"), m.sem("inverted"), m.sem("scaled")
        turned, turned_out, attended, attn_out = m.sem("turned"), m.sem("turned_out"), m.sem("attended"), m.sem("attn_out")
        out_made, result = m.sem("out_made"), m.sem("result")
        block = ctx.enter_context(nc.Block())
        PROJ = 3 * KT
        SLOTS = PROJ + W

        def loop(eng):
            return eng.Fori(0, B)

        @block.sync
        def _(sp):
            sp.dma_start(w_qkv[:], t["light_wt"].rearrange("i p k o -> p i k o")).then_inc(w_in, 16)
            sp.dma_start(w_o[:], t["L0_ffn_wo_light"].rearrange("(k p) o -> p k o", p=P)).then_inc(w_in, 16)
            with loop(sp) as b:
                for half in range(2):
                    n = b * 2 + half
                    after(sp, projected, b * 2 * PROJ + max(half - 1, 0) * PROJ)
                    sp.dma_start(y_t[:, half], t["yn_t"][bass.ds(b, 1), :, :, half * D:(half + 1) * D]
                                 .rearrange("a p k s -> p (a k) s")).then_inc(y_in[half], 16)
                    sp.dma_start(x1[:, half], t["x1"][bass.ds(b, 1), half * D:(half + 1) * D]
                                 .rearrange("a (t p) d -> p (a t) d", p=P)).then_inc(x_in[half], 16)
                for half in range(2):
                    after(sp, result, (b * 2 + half + 1) * W)
                    sp.dma_start(t["mid"][bass.ds(b, 1), half * D:(half + 1) * D]
                                 .rearrange("a (t p) d -> p (a t) d", p=P), x1[:, half]).then_inc(stored, 16)
                sp.wait_ge(stored, (b + 1) * 32)
                alone(sp, passed)

        @block.gpsimd
        def _(pool):
            with loop(pool) as b:
                for w in range(2 * W):
                    n = b * 2 * W + w
                    pool.wait_ge(inverted, n + 1)
                    nc.gpsimd.tensor_tensor(prob[:, w % 2].rearrange("p a b c -> p (a b) c"),
                                            prob[:, w % 2].rearrange("p a b c -> p (a b) c"),
                                            inv[:, w % 2].unsqueeze(2).to_broadcast([P, FH, P]),
                                            ALU.mult).then_inc(scaled, 1)

        @block.scalar
        def _(act):
            prime(act, proj_out, turned_out, attn_out)
            with loop(act) as b:
                for half in range(2):
                    n = b * 2 + half
                    for i in range(PROJ):
                        after(act, projected, n * PROJ + i + 1)
                        dst = qk_t[:, i // KT, i % KT] if i < 2 * KT else v[:, i % KT]
                        if i == 0:
                            after(act, scored, n * W)
                            after(act, attended, n * W)
                        act.activation(dst, proj_ps[:, i % 2], ACT.Copy).then_inc(proj_out, 1)
                    for w in range(W):
                        nw = n * W + w
                        after(act, shifted, nw + 1)
                        act.activation(prob[:, w % 2], prob[:, w % 2], ACT.Exp, scale=float(FD) ** -0.5).then_inc(exped, 1)
                        after(act, turned, nw + 1)
                        act.activation(prob_t[:, w % 2], turn_ps[:], ACT.Copy).then_inc(turned_out, 1)
                        after(act, attended, nw + 1)
                        act.activation(attn_t[:, w % 2], attn_ps[:], ACT.Copy).then_inc(attn_out, 1)

        @block.vector
        def _(dve):
            prime(dve, result, shifted)
            with loop(dve) as b:
                for half in range(2):
                    n = b * 2 + half
                    for w in range(W):
                        nw = n * W + w
                        after(dve, scored, nw + 1)
                        dve.reduce_max(top[:, w % 2], score_ps[:].rearrange("p a b c -> p (a b) c"), AX.X
                                       ).then_inc(topped, 1)
                        dve.wait_ge(topped, nw + 1)
                        after(dve, turned, b * 2 * W + max(half * W + w - 1, 0))
                        dve.tensor_tensor(prob[:, w % 2].rearrange("p a b c -> p (a b) c"),
                                          score_ps[:].rearrange("p a b c -> p (a b) c"),
                                          top[:, w % 2].unsqueeze(2).to_broadcast([P, FH, P]),
                                          ALU.subtract).then_inc(shifted, 1)
                        if w:
                            finish(w - 1)
                        else:
                            def finish(w):
                                dve.wait_ge(out_made, n * W + w + 1)
                                if w == 0:
                                    dve.wait_ge(x_in[half], (b + 1) * 16)
                                dve.scalar_tensor_tensor(x1[:, half, w], proj_ps[:, w % 2], keep["gates"][:, 1:2],
                                                         x1[:, half, w], ALU.mult, ALU.add).then_inc(result, 1)
                        dve.wait_ge(exped, nw + 1)
                        dve.reduce_sum(total[:, w % 2], prob[:, w % 2].rearrange("p a b c -> p (a b) c"), AX.X
                                       ).then_inc(summed, 1)
                        dve.wait_ge(summed, nw + 1)
                        dve.reciprocal(inv[:, w % 2], total[:, w % 2]).then_inc(inverted, 1)
                    finish(W - 1)

        @block.tensor
        def _(pe):
            prime(pe, projected, scored, attended, turned)
            pe.wait_ge(w_in, 32)
            with loop(pe) as b:
                for half in range(2):
                    n = b * 2 + half
                    pe.wait_ge(y_in[half], (b + 1) * 16)
                    after(pe, result, n * W)
                    for i in range(PROJ):
                        after(pe, proj_out, n * PROJ + max(i - 1, 0))
                        for k in range(KT):
                            if i < 2 * KT:
                                lhs, rhs = w_qkv[:, i // KT, k, (i % KT) * P:(i % KT + 1) * P], y_t[:, half, k]
                            else:
                                lhs, rhs = y_t[:, half, k, (i % KT) * P:(i % KT + 1) * P], w_qkv[:, 2, k]
                            ins = pe.matmul(proj_ps[:, i % 2], lhs, rhs, start=k == 0, stop=k == KT - 1)
                        ins.then_inc(projected, 1)
                    after(pe, proj_out, (n + 1) * PROJ)
                    for w in range(W):
                        nw = n * W + w
                        cut = slice(w * P, (w + 1) * P)
                        after(pe, shifted, nw)
                        for h in range(FH):
                            row = (h % 2) * FD
                            ins = pe.matmul(score_ps[:, h % 2, h // 2], qk_t[row:row + FD, 0, h // 2, cut],
                                            qk_t[row:row + FD, 1, h // 2, cut], start=True, stop=True)
                        ins.then_inc(scored, 1)
                        if w:
                            output(w - 1)
                        else:
                            def output(w):
                                after(pe, attn_out, n * W + w + 1)
                                if w >= 2:
                                    after(pe, result, n * W + w - 1)
                                for k in range(HP):
                                    ins = pe.matmul(proj_ps[:, w % 2], attn_t[:, w % 2, k], w_o[:, k],
                                                    start=k == 0, stop=k == HP - 1)
                                ins.then_inc(out_made, 1)
                        pe.wait_ge(scaled, nw + 1)
                        after(pe, turned_out, nw)
                        for h in range(FH):
                            ins = pe.transpose(turn_ps[:, h % 2, h // 2], prob[:, w % 2, h % 2, h // 2], keep["ident"][:])
                        ins.then_inc(turned, 1)
                        after(pe, turned_out, nw + 1)
                        after(pe, attn_out, nw)
                        for h in range(FH):
                            row = (h % 2) * FD
                            ins = pe.matmul(attn_ps[row:row + FD, h // 2], v[:, w, h * FD:(h + 1) * FD],
                                            prob_t[:, w % 2, h % 2, h // 2], start=True, stop=True)
                        ins.then_inc(attended, 1)
                    output(W - 1)


def route(nc, t, keep):
    with ExitStack() as ctx:
        m = Memory(nc, ctx, "r")
        G = 2 * B
        s = keep["route_s"][:].rearrange("p w b t -> p (w b) t")
        log_k = m.sb("log_k", [P, G])
        minus_a = m.sb("minus_a", [P, G])
        part_max = m.sb("part_max", [P, G])
        s_max = m.sb("s_max", [P, G])
        most = m.sb("most", [P, G])
        most_k = m.sb("most_k", [P, G])
        x = m.sb("x", [P, G, NT])
        e = m.sb("e", [P, G, NT])
        part_sum = m.sb("part_sum", [P, G])
        log_sum = m.sb("log_sum", [P, G])
        score = m.sb("score", [P, G, NT])
        rest = m.sb("rest", [P, G, NT])
        score_rows = m.sb("score_rows", [B * NT, P])
        all_scores = m.sb("all_scores", [P, B * NT, P])
        counts = m.sb("counts", [P, B * NT, 4])
        hit = m.sb("hit", [P, S])
        hit_tile = m.sb("hit_tile", [P, P])
        rank = m.sb("rank", [P, B, NT])
        far = m.sb("far", [P, B, NT])
        rows = m.sb("rows", [P, 2, NT, D])
        sum_ps = m.ps("sum_ps", [P, 512])
        turn_ps = m.ps("turn_ps", [P, 512])
        dve_did, act_did, pe_did, pool_did = m.sem("dve_did"), m.sem("act_did"), m.sem("pe_did"), m.sem("pool_did")
        exped, summed, added, logged = m.sem("exped"), m.sem("summed"), m.sem("added"), m.sem("logged")
        step_did = m.sem("step_did")
        score_out, scores_in, rows_in, scattered = m.sem("score_out"), m.sem("scores_in"), [m.sem(f"rows_in{b}") for b in range(B)], [m.sem(f"scattered{b}") for b in range(B)]
        shifted, renewed, scored, ranked = m.sem("shifted"), m.sem("renewed"), m.sem("scored"), m.sem("ranked")
        block = ctx.enter_context(nc.Block())
        N = ITERS - 1

        def wide(a):
            return a.unsqueeze(2).to_broadcast([P, G, NT])

        @block.vector
        def _(dve):
            start = Chain(dve, dve_did)
            start.mark(dve.memset(log_k[:, 0:B], LOG_KQ))
            start.mark(dve.memset(log_k[:, B:G], LOG_KKV))
            start.mark(dve.memset(counts[:], 0.0))
            start.mark(dve.memset(minus_a[:, 0:B], float(np.log(np.float32(S))) - LOG_KQ))
            start.mark(dve.memset(minus_a[:, B:G], float(np.log(np.float32(S))) - LOG_KKV))
            start.mark(dve.reduce_max(part_max[:], s, AX.X))
            dve.wait_ge(pool_did, 1)
            start.wait()
            MARKS = 4
            with dve.Fori(0, N) as i:
                step = Chain(dve, step_did, i * MARKS)
                step.mark(dve.tensor_tensor(most[:], s_max[:], minus_a[:], ALU.min))
                step.mark(dve.tensor_tensor(x[:], s, wide(minus_a[:]), ALU.min))
                step.wait()
                step.mark(dve.tensor_tensor(x[:], x[:], wide(most[:]), ALU.subtract))
                step.mark(dve.tensor_tensor(most_k[:], most[:], log_k[:], ALU.subtract))
                dve.wait_ge(exped, i + 1)
                dve.reduce_sum(part_sum[:], e[:], AX.X).then_inc(summed, 1)
                dve.wait_ge(logged, i + 1)
                dve.tensor_tensor(minus_a[:], log_sum[:], most_k[:], ALU.add).then_inc(renewed, 1)
                dve.wait_ge(renewed, i + 1)
                assert step.n == MARKS
            dve.wait_ge(renewed, N)
            start.mark(dve.tensor_tensor(x[:], s, wide(minus_a[:]), ALU.subtract))
            start.wait()
            start.mark(dve.tensor_scalar(x[:], x[:], 0.0, None, ALU.min))
            FINAL = start.n
            assert FINAL == 8
            dve.wait_ge(scored, 1)
            start.mark(dve.tensor_scalar(rest[:], score[:], -1.0, 1.0, ALU.mult, ALU.add))
            start.wait()
            start.mark(dve.tensor_tensor(keep["factor"][:].rearrange("p w b t -> p (w b) t"), score[:], rest[:], ALU.add))
            start.wait()
            start.mark(dve.tensor_scalar(keep["q_gate"][:].rearrange("p b t -> p (b t)"),
                                         keep["factor"][:, 0].rearrange("p b t -> p (b t)"),
                                         keep["gates"][:, 1:2], None, ALU.mult))
            dve.wait_ge(pe_did, 1)
            start.mark(dve.tensor_copy(score_rows[:], turn_ps[0:B * NT, 0:P]))
            assert start.n == 12
            dve.wait_ge(scores_in, 16)
            for b in range(B):
                for i in range(NT):
                    n = b * NT + i
                    own = score[:, b, i:i + 1]
                    if i:
                        start.mark(dve.tensor_scalar(hit[:, 0:i * P],
                                                     all_scores[:, b * NT:n].rearrange("p a c -> p (a c)"), own,
                                                     None, ALU.is_ge, ALU.add, accum_out=counts[:, n, 0:1]))
                    if i < NT - 1:
                        start.mark(dve.tensor_scalar(hit[:, (i + 1) * P:S],
                                                     all_scores[:, n + 1:(b + 1) * NT].rearrange("p a c -> p (a c)"), own,
                                                     None, ALU.is_gt, ALU.add, accum_out=counts[:, n, 1:2]))
                    for c, (op, half) in enumerate(((ALU.is_ge, "before"), (ALU.is_gt, "after"))):
                        start.mark(dve.scalar_tensor_tensor(hit[:, i * P:(i + 1) * P] if c else hit_tile[:],
                                                            all_scores[:, n], own, keep[half][:],
                                                            op, ALU.mult, accum_out=counts[:, n, 2 + c:3 + c]))
                    start.wait()
            start.mark(dve.reduce_sum(rank[:].rearrange("p b t -> p (b t)"), counts[:], AX.X))
            start.wait()
            start.mark(dve.tensor_scalar(far[:], rank[:], float(NQ), float(OUT_OF_RANGE), ALU.is_ge, ALU.mult))
            start.wait()
            for b in range(B):
                start.mark(dve.scalar_tensor_tensor(far[:, b], rank[:, b], float(b * NQ), far[:, b], ALU.add, ALU.add))
            start.wait()
            dve.tensor_copy(keep["place"][:], far[:]).then_inc(ranked, 1)

        @block.scalar
        def _(act):
            with act.Fori(0, N) as i:
                act.wait_ge(step_did, i * 4 + 3)
                act.activation(e[:], x[:], ACT.Exp).then_inc(exped, 1)
                act.wait_ge(added, i + 1)
                act.activation(log_sum[:], sum_ps[:, 0:G], ACT.Ln).then_inc(logged, 1)
            act.wait_ge(dve_did, 8)
            act.activation(score[:], x[:], ACT.Exp).then_inc(scored, 1)

        @block.tensor
        def _(pe):
            with pe.Fori(0, N) as i:
                pe.wait_ge(summed, i + 1)
                pe.matmul(sum_ps[:, 0:G], keep["ones"][:], part_sum[:], start=True, stop=True).then_inc(added, 1)
            pe.wait_ge(scored, 1)
            pe.transpose(turn_ps[0:B * NT, 0:P], score[:, 0:B].rearrange("p b t -> p (b t)"), keep["ident"][:]
                         ).then_inc(pe_did, 1)

        @block.gpsimd
        def _(pool):
            pool.wait_ge(dve_did, 6)
            nc.gpsimd.partition_all_reduce(s_max[:], part_max[:], P, bass.bass_isa.ReduceOp.max).then_inc(pool_did, 1)
            pool.wait_ge(ranked, 1)
            for b in range(B):
                pool.wait_ge(rows_in[b], 16)
                for i in range(NT):
                    nc.gpsimd.indirect_dma_start(
                        t["q_rows"], bass.IndirectOffsetOnAxis(keep["place"][:, b, i:i + 1], 0),
                        rows[:, b % 2, i], None, bounds_check=B * NQ - 1, oob_is_err=False).then_inc(scattered[b], 16)
            for b in range(B):
                pool.wait_ge(scattered[b], 16 * NT)

        @block.sync
        def _(sp):
            for b in range(2):
                sp.dma_start(rows[:, b], t["yn"][b].rearrange("(t p) d -> p t d", p=P)).then_inc(rows_in[b], 16)
            sp.wait_ge(dve_did, 12)
            sp.dma_start(t["scores"], score_rows[:]).then_inc(score_out, 16)
            sp.wait_ge(score_out, 16)
            sp.dma_start(all_scores[:], t["scores"].unsqueeze(0).to_broadcast([P, B * NT, P])).then_inc(scores_in, 16)
            for b in range(2, B):
                sp.wait_ge(scattered[b - 2], 16 * NT)
                sp.dma_start(rows[:, b % 2], t["yn"][b].rearrange("(t p) d -> p t d", p=P)).then_inc(rows_in[b], 16)


def heavy_attention(nc, t, keep):
    with ExitStack() as ctx:
        m = Memory(nc, ctx, "h")
        QT = NQ // P
        y_t = m.sb("y_t", [P, KT, S])
        q_rows = m.sb("q_rows", [P, QT, D])
        xq_t = m.sb("xq_t", [P, KT, NQ])
        wg = m.sb("wg", [P, 3, KT, P])
        w_o = m.sb("w_o", [P, KT, D])
        part = m.sb("part", [P, 2, NQ + S], F16)
        q_stack = m.sb("q_stack", [P, 2, NQ], F16)
        k_stack = m.sb("k_stack", [P, 2, 2, S], F16)
        v_g = m.sb("v_g", [P, NT, P])
        factor_b = m.sb("factor_b", [P, NT])
        prob = m.sb("prob", [P, 3, S])
        prob_t = m.sb("prob_t", [P, 2, 2, NT, 2 * P])
        attn_t = m.sb("attn_t", [P, HP, NQ])
        neg_max = m.sb("neg_max", [P, QT * 2])
        row_sum = m.sb("row_sum", [P, QT * 2])
        inv = m.sb("inv", [P, QT, 2])
        inv_wide = m.sb("inv_wide", [P, 2, 2, FD])
        inv_t = m.sb("inv_t", [P, 2 * P])
        out_rows = m.sb("out_rows", [P, QT, D])
        score_ps = m.ps("score_ps", [P, 2, S])
        turn_ps = m.ps("turn_ps", [P, 2, 4, P])
        attn_ps = m.ps("attn_ps", [P, 512])
        inv_ps = m.ps("inv_ps", [P, 512])
        y_in, rows_in, w_in, wo_in, stack_in, stored = (m.sem(n) for n in
                                                        ("y_in", "rows_in", "w_in", "wo_in", "stack_in", "stored"))
        rows_turned, rows_turned_out, factor_set = m.sem("rows_turned"), m.sem("rows_turned_out"), m.sem("factor_set")
        made, v_made, high_done, low_done, v_out = (m.sem(n) for n in ("made", "v_made", "high_done", "low_done", "v_out"))
        scored, topped, exped = m.sem("scored"), m.sem("topped"), m.sem("exped")
        turn_a, turn_b, out_a, out_b = m.sem("turn_a"), m.sem("turn_b"), m.sem("out_a"), m.sem("out_b")
        inverted, widened, inv_turned, inv_out = (m.sem(n) for n in ("inverted", "widened", "inv_turned", "inv_out"))
        passed = m.sem("passed")
        attended, normed, projected, proj_out = (m.sem(n) for n in ("attended", "normed", "projected", "proj_out"))
        block = ctx.enter_context(nc.Block())
        STEPS, PAIRS, PER_PAIR = QT * 2, QT // 2, 4
        STACK = 2 * (2 + 4) * 16

        @block.sync
        def _(sp):
            sp.dma_start(w_o[:], t["L0_ffn_wo_heavy"].rearrange("(k p) o -> p k o", p=P)).then_inc(wo_in, 16)
            with sp.Fori(0, B) as b:
                after(sp, v_made, b * HP * NT)
                alone(sp, passed)
                after(sp, rows_turned, b * QT)
                sp.dma_start(q_rows[:], t["q_rows"].rearrange("(b t p) d -> b p t d", b=B, p=P)[bass.ds(b, 1)]
                             .rearrange("a p t d -> p (a t) d")).then_inc(rows_in, 16)
                sp.dma_start(y_t[:], t["yn_t"][bass.ds(b, 1)].rearrange("a p k s -> p (a k) s")).then_inc(y_in, 16)
                with sp.Fori(0, HP) as g:
                    it = b * HP + g
                    after(sp, v_made, it * NT)
                    alone(sp, passed)
                    after(sp, made, it * 3)
                    sp.dma_start(wg[:], t["heavy_wt"][bass.ds(g, 1)].rearrange("a i p k o -> p (a i) k o")
                                 ).then_inc(w_in, 16)
                    after(sp, scored, it * STEPS)
                    alone(sp, passed)
                    sp.wait_ge(low_done, it * 3 + 3)
                    sp.wait_ge(high_done, it * 3 + 3)
                    for h in range(2):
                        rows = slice(h * FD, (h + 1) * FD)
                        for half in range(2):
                            sp.dma_start(q_stack[half * FD:(half + 1) * FD, h], part[rows, half, 0:NQ]).then_inc(stack_in, 16)
                            for r in range(2):
                                sp.dma_start(k_stack[r * FD:(r + 1) * FD, half, h], part[rows, half, NQ:]
                                             ).then_inc(stack_in, 16)
                after(sp, proj_out, (b + 1) * QT)
                sp.dma_start(t["h_rows"].rearrange("(b t p) d -> b p t d", b=B, p=P)[bass.ds(b, 1)]
                             .rearrange("a p t d -> p (a t) d"), out_rows[:]).then_inc(stored, 16)
                sp.wait_ge(stored, (b + 1) * 16)
                alone(sp, passed)

        @block.gpsimd
        def _(pool):
            prime(pool, widened)
            with pool.Fori(0, B * HP) as it:
                for qt in range(QT):
                    pool.wait_ge(inverted, it * QT + qt + 1)
                    after(pool, inv_turned, it * QT + max(qt - 1, 0))
                    alone(pool, passed)
                    nc.gpsimd.tensor_scalar(inv_wide[:, qt % 2], inv[:, qt].unsqueeze(2).to_broadcast([P, 2, FD]),
                                            1.0, 1.0, ALU.mult, ALU.mult).then_inc(widened, 1)

        @block.scalar
        def _(act):
            prime(act, exped, out_a, inv_out, proj_out)
            with act.Fori(0, B) as b:
                for i in range(QT):
                    after(act, rows_turned, b * QT + i + 1)
                    act.activation(xq_t[:, :, i * P:(i + 1) * P], turn_ps[:, i % 2], ACT.Copy).then_inc(rows_turned_out, 1)
                with act.Fori(0, HP) as g:
                    it = b * HP + g
                    after(act, scored, it * STEPS)
                    for n in range(3):
                        after(act, made, it * 3 + n + 1)
                        act.activation(part[:, 0, n * 512:(n + 1) * 512], score_ps[:, n // 2, n % 2 * 512:n % 2 * 512 + 512],
                                       ACT.Copy).then_inc(high_done, 1)

                    def expo(s):
                        act.wait_ge(topped, it * STEPS + s + 1)
                        if s >= 3:
                            act.wait_ge(turn_b, it * STEPS + s - 2)
                        act.activation(prob[:, s % 3], score_ps[:, s % 2], ACT.Exp, scale=-1.0, bias=neg_max[:, s:s + 1],
                                       accum_out=row_sum[:, s:s + 1]).then_inc(exped, 1)

                    def inverse_out(pair):
                        after(act, inv_turned, it * QT + 2 * pair + 2)
                        after(act, normed, it * PAIRS + pair)
                        act.activation(inv_t[:], inv_ps[:, 0:2 * P], ACT.Copy).then_inc(inv_out, 1)
                    expo(0)
                    for s in range(STEPS):
                        pair, at = divmod(s, PER_PAIR)
                        if s + 1 < STEPS:
                            expo(s + 1)
                        if at == 0:
                            after(act, attended, it * PAIRS)
                        act.wait_ge(turn_a, it * STEPS + s + 1)
                        act.activation(prob_t[:, pair % 2, s % 2, 0:4, at // 2 * P:at // 2 * P + P], turn_ps[:, 0],
                                       ACT.Copy).then_inc(out_a, 1)
                        if at == 2 and pair:
                            inverse_out(pair - 1)
                    inverse_out(PAIRS - 1)
                for i in range(QT):
                    act.wait_ge(projected, b * QT + i + 1)
                    act.activation(out_rows[:, i], score_ps[:, i % 2, 0:D], ACT.Copy).then_inc(proj_out, 1)

        @block.vector
        def _(dve):
            prime(dve, v_out, out_b, normed)
            with dve.Fori(0, B) as b:
                after(dve, v_out, b * HP * 2)
                dve.tensor_copy(factor_b[:].unsqueeze(1), keep["factor"][:, 1, bass.ds(b, 1)]).then_inc(factor_set, 1)
                dve.wait_ge(factor_set, b + 1)
                alone(dve, passed)
                with dve.Fori(0, HP) as g:
                    it = b * HP + g
                    for n in range(3):
                        dve.wait_ge(high_done, it * 3 + n + 1)
                        dve.tensor_tensor(part[:, 1, n * 512:(n + 1) * 512], score_ps[:, n // 2, n % 2 * 512:n % 2 * 512 + 512],
                                          part[:, 0, n * 512:(n + 1) * 512], ALU.subtract).then_inc(low_done, 1)
                    after(dve, attended, it * PAIRS)
                    for c in range(2):
                        after(dve, v_made, it * NT + 4 * c + 4)
                        dve.tensor_tensor(v_g[:, 4 * c:4 * c + 4], turn_ps[:, c],
                                          factor_b[:, 4 * c:4 * c + 4].unsqueeze(2).to_broadcast([P, 4, P]),
                                          ALU.mult).then_inc(v_out, 1)

                    def least(s):
                        after(dve, scored, it * STEPS + s + 1)
                        dve.tensor_reduce(neg_max[:, s:s + 1], score_ps[:, s % 2], axis=AX.X, op=ALU.min).then_inc(topped, 1)

                    def invert(qt):
                        after(dve, exped, it * STEPS + 2 * qt + 2)
                        dve.reciprocal(inv[:, qt], row_sum[:, 2 * qt:2 * qt + 2]).then_inc(inverted, 1)

                    def norm(pair):
                        after(dve, attended, it * PAIRS + pair + 1)
                        after(dve, inv_out, it * PAIRS + pair + 1)
                        dve.tensor_tensor(attn_t[:, bass.ds(g, 1), pair * 2 * P:(pair + 1) * 2 * P],
                                          attn_ps[:, 0:2 * P].unsqueeze(1), inv_t[:].unsqueeze(1),
                                          ALU.mult).then_inc(normed, 1)
                    after(dve, widened, it * QT)
                    least(0)
                    least(1)
                    for s in range(STEPS):
                        pair, at = divmod(s, PER_PAIR)
                        if at == 0:
                            after(dve, attended, it * PAIRS)
                        dve.wait_ge(turn_b, it * STEPS + s + 1)
                        dve.tensor_copy(prob_t[:, pair % 2, s % 2, 4:8, at // 2 * P:at // 2 * P + P], turn_ps[:, 1]
                                        ).then_inc(out_b, 1)
                        if s + 2 < STEPS:
                            least(s + 2)
                        if s and s % 2 == 0:
                            invert(s // 2 - 1)
                        if at == 3 and pair:
                            norm(pair - 1)
                    invert(QT - 1)
                    norm(PAIRS - 1)

        @block.tensor
        def _(pe):
            prime(pe, v_made, made, rows_turned, scored, inv_turned, attended)
            with pe.Fori(0, B) as b:
                pe.wait_ge(rows_in, (b + 1) * 16)
                after(pe, out_a, b * HP * STEPS)
                after(pe, out_b, b * HP * STEPS)
                for i in range(QT):
                    if i >= 2:
                        pe.wait_ge(rows_turned_out, b * QT + i - 1)
                    for k in range(KT):
                        ins = pe.transpose(turn_ps[:, i % 2, k], q_rows[:, i, k * P:(k + 1) * P], keep["ident"][:])
                    ins.then_inc(rows_turned, 1)
                pe.wait_ge(y_in, (b + 1) * 16)
                pe.wait_ge(rows_turned_out, (b + 1) * QT)
                after(pe, proj_out, b * QT)
                alone(pe, passed)
                with pe.Fori(0, HP) as g:
                    it = b * HP + g
                    pe.wait_ge(w_in, (it + 1) * 16)
                    after(pe, exped, it * STEPS)
                    for n in range(3):
                        w, src = (0, xq_t[:]) if n == 0 else (1, y_t[:, :, (n - 1) * 512:n * 512])
                        for k in range(KT):
                            ins = pe.matmul(score_ps[:, n // 2, n % 2 * 512:n % 2 * 512 + 512], wg[:, w, k], src[:, k],
                                            start=k == 0, stop=k == KT - 1)
                        ins.then_inc(made, 1)
                    after(pe, out_a, it * STEPS)
                    after(pe, out_b, it * STEPS)
                    for i in range(NT):
                        for k in range(KT):
                            ins = pe.matmul(turn_ps[:, i // 4, i % 4], y_t[:, k, i * P:(i + 1) * P], wg[:, 2, k],
                                            start=k == 0, stop=k == KT - 1)
                        ins.then_inc(v_made, 1)
                    pe.wait_ge(stack_in, (it + 1) * STACK)
                    pe.wait_ge(low_done, it * 3 + 3)
                    after(pe, v_out, it * 2 + 2)

                    def score(s):
                        qt, h = divmod(s, 2)
                        if s >= 2:
                            after(pe, exped, it * STEPS + s - 1)
                        for c in range(2):
                            for half in range(2):
                                ins = pe.matmul(score_ps[:, s % 2, c * 512:(c + 1) * 512], q_stack[:, h, qt * P:(qt + 1) * P],
                                                k_stack[:, half, h, c * 512:(c + 1) * 512], start=half == 0, stop=half == 1)
                        ins.then_inc(scored, 1)

                    def turn_inverse(qt):
                        after(pe, widened, it * QT + qt + 1)
                        after(pe, inv_out, it * PAIRS + qt // 2)
                        pe.transpose(inv_ps[:, (qt % 2) * P:(qt % 2 + 1) * P],
                                     inv_wide[:, qt % 2].rearrange("p h d -> p (h d)"), keep["ident"][:]
                                     ).then_inc(inv_turned, 1)

                    def attend(pair):
                        after(pe, out_a, it * STEPS + (pair + 1) * PER_PAIR)
                        after(pe, out_b, it * STEPS + (pair + 1) * PER_PAIR)
                        after(pe, normed, it * PAIRS + pair)
                        for k in range(NT):
                            for h in range(2):
                                ins = pe.matmul(attn_ps[h * FD:(h + 1) * FD, 0:2 * P], v_g[:, k, h * FD:(h + 1) * FD],
                                                prob_t[:, pair % 2, h, k], start=k == 0, stop=k == NT - 1)
                        ins.then_inc(attended, 1)
                    score(0)
                    score(1)
                    for s in range(STEPS):
                        after(pe, exped, it * STEPS + s + 1)
                        for h, (sem, out) in enumerate(((turn_a, out_a), (turn_b, out_b))):
                            after(pe, out, it * STEPS + s)
                            for k in range(4):
                                ins = pe.transpose(turn_ps[:, h, k], prob[:, s % 3, (4 * h + k) * P:(4 * h + k + 1) * P],
                                                   keep["ident"][:])
                            ins.then_inc(sem, 1)
                        if s + 2 < STEPS:
                            score(s + 2)
                        if s > 2 and s % 2 == 1:
                            turn_inverse(s // 2 - 1)
                        if s % PER_PAIR == 0 and s:
                            attend(s // PER_PAIR - 1)
                    turn_inverse(QT - 1)
                    attend(PAIRS - 1)
                pe.wait_ge(wo_in, 16)
                after(pe, normed, (b + 1) * HP * PAIRS)
                after(pe, exped, (b + 1) * HP * STEPS)
                for i in range(QT):
                    if i >= 2:
                        after(pe, proj_out, b * QT + i - 1)
                    for k in range(HP):
                        ins = pe.matmul(score_ps[:, i % 2, 0:D], attn_t[:, k, i * P:(i + 1) * P], w_o[:, k],
                                        start=k == 0, stop=k == HP - 1)
                    ins.then_inc(projected, 1)


def combine(nc, t, keep):
    with ExitStack() as ctx:
        m = Memory(nc, ctx, "c")
        mid = m.sb("mid", [P, B, NT, D])
        routed = m.sb("routed", [P, B, NT, D])
        mid_in = [m.sem(f"mid_in{b}") for b in range(B)]
        cleared = m.sem("cleared")
        gathered = [m.sem(f"gathered{b}") for b in range(B)]
        added, stored = m.sem("added"), m.sem("stored")
        block = ctx.enter_context(nc.Block())

        @block.sync
        def _(sp):
            for b in range(B):
                sp.dma_start(mid[:, b], t["mid"][b].rearrange("(t p) d -> p t d", p=P)).then_inc(mid_in[b], 16)
            for b in range(B):
                sp.wait_ge(added, (b + 1) * NT)
                sp.dma_start(t["out"][b].rearrange("(t p) d -> p t d", p=P), mid[:, b]).then_inc(stored, 16)
            sp.wait_ge(stored, B * 16)

        @block.gpsimd
        def _(pool):
            for b in range(B):
                pool.wait_ge(cleared, b + 1)
                for i in range(NT):
                    nc.gpsimd.indirect_dma_start(
                        routed[:, b, i], None, t["h_rows"], bass.IndirectOffsetOnAxis(keep["place"][:, b, i:i + 1], 0),
                        bounds_check=B * NQ - 1, oob_is_err=False).then_inc(gathered[b], 16)

        @block.vector
        def _(dve):
            for b in range(B):
                dve.memset(routed[:, b], 0.0).then_inc(cleared, 1)
            for b in range(B):
                dve.wait_ge(mid_in[b], 16)
                dve.wait_ge(gathered[b], 16 * NT)
                for i in range(NT):
                    dve.scalar_tensor_tensor(mid[:, b, i], routed[:, b, i], keep["q_gate"][:, b, i:i + 1], mid[:, b, i],
                                             ALU.mult, ALU.add).then_inc(added, 1)


def build(nc, t, phases=9):
    def scratch(name, shape, dt=F32):
        t[name] = nc.dram_tensor(name, shape, dt, kind="Internal").ap()

    scratch("xattn_wt", [NG, 3, P, KT, P])
    scratch("heavy_wt", [HP, 3, P, KT, P])
    scratch("light_wt", [3, P, KT, D])
    for name in ("x1", "yn"):
        scratch(name, [B, S, D])
    scratch("yn_t", [B, P, KT, S])
    scratch("mid", [B, S, D])
    scratch("scores", [B * NT, P])
    scratch("q_rows", [B * NQ, D])
    scratch("h_rows", [B * NQ, D])
    with ExitStack() as ctx:
        m = Memory(nc, ctx, "keep")
        keep = {
            "ident": m.sb("ident", [P, P]), "ones": m.sb("ones", [P, P]),
            "before": m.sb("before", [P, P]), "after": m.sb("after", [P, P]),
            "minus_half": m.sb("minus_half", [P, NT]), "slopes": m.sb("slopes", [P, XH]),
            "tokens": m.sb("tokens", [P, 2, D]), "gates": m.sb("gates", [P, 2]),
            "wo_t": m.sb("wo_t", [P, KT, D]), "route_s": m.sb("route_s", [P, 2, B, NT]),
            "factor": m.sb("factor", [P, 2, B, NT]), "q_gate": m.sb("q_gate", [P, B, NT]),
            "place": m.sb("place", [P, B, NT], I32),
        }
        prepare_weights(nc, t, keep)
        if phases >= 1:
            cross_attention(nc, t, keep, B if phases > 1 else 1)
        if phases >= 2:
            light_attention(nc, t, keep)
        if phases >= 3:
            route(nc, t, keep)
        if phases >= 4:
            heavy_attention(nc, t, keep)
        if phases >= 5:
            combine(nc, t, keep)


INPUTS = ["x", "ctx_1024", "itok_BxS_8_8191", "itok_BxS2_1_8191", "mask_BxSxS2_if1", "g_xattn", "g_ffn",
          "L0_xattn_W_q", "L0_xattn_W_k", "L0_xattn_W_v", "L0_xattn_W_o", "L0_ffn_gamma_light", "L0_ffn_wq_light",
          "L0_ffn_wkv_light", "L0_ffn_wo_light", "L0_ffn_q_routing_token", "L0_ffn_kv_routing_token",
          "L0_ffn_gamma_heavy", "L0_ffn_wq_heavy", "L0_ffn_wkv_heavy", "L0_ffn_wo_heavy"]


def kernel(**inputs):
    import concourse.bacc as bacc
    from concourse.bass_utils import run_bass_kernel_spmd

    nc = bacc.Bacc("TRN2", target_bir_lowering=False, num_devices=1)
    arrays, t = {}, {}
    for name in INPUTS:
        a = np.ascontiguousarray(inputs[name])
        arrays[f"in_{name}"] = a
        t[name] = nc.dram_tensor(f"in_{name}", a.shape, mybir.dt.from_np(a.dtype), kind="ExternalInput").ap()
    t["out"] = nc.dram_tensor("out", (B, S, D), F32, kind="ExternalOutput").ap()
    build(nc, t)
    r = run_bass_kernel_spmd(nc, [arrays], core_ids=[0])
    return r.results[0]["out"]
```

```python
from contextlib import ExitStack

import numpy as np

import concourse.bass as bass
from concourse import mybir

F32 = mybir.dt.float32
F16 = mybir.dt.float16
I32 = mybir.dt.int32
ALU = mybir.AluOpType
ACT = mybir.ActivationFunctionType
AX = mybir.AxisListType

P = 128
B, S, D = 4, 1024, 512
NT = S // P
KT = D // P
XH, XD = 16, D // 16
GH = P // XD
NG = XH // GH
FH, FD = 8, D // 8
HP = FH // 2
NQ = 512
LN_EPS = 1e-5
MASKED = 1e30
ITERS = 50
LOG_KQ = float(np.log(np.float32(min(NQ * 9.0 / 8.0, S))))
LOG_KKV = float(np.log(np.float32(min(S * 9.0 / 8.0, S))))
OUT_OF_RANGE = 1 << 20


def slope(h):
    return float(np.float32(2.0 ** (-8.0 / XH)) ** (h + 1))


class Memory:

    def __init__(self, nc, ctx, phase):
        self.nc, self.ctx, self.phase = nc, ctx, phase

    def sb(self, name, shape, dt=F32):
        return self.ctx.enter_context(self.nc.sbuf_tensor(f"{self.phase}_{name}", shape, dt))

    def ps(self, name, shape, dt=F32):
        return self.ctx.enter_context(self.nc.psum_tensor(f"{self.phase}_{name}", shape, dt))

    def sem(self, name):
        return self.ctx.enter_context(self.nc.semaphore(f"{self.phase}_{name}"))


def prime(eng, *sems):
    for sem in sems:
        eng.sem_inc(sem, 1)


def after(eng, sem, count):
    eng.wait_ge(sem, count + 1)


def alone(eng, passed):
    eng.sem_inc(passed, 1)


class Chain:

    def __init__(self, eng, sem, base=0):
        self.eng, self.sem, self.base, self.n = eng, sem, base, 0

    def mark(self, ins):
        ins.then_inc(self.sem, 1)
        self.n += 1
        return self.base + self.n

    def wait(self):
        self.eng.wait_ge(self.sem, self.base + self.n)


def prepare_weights(nc, t, keep):
    with ExitStack() as ctx:
        m = Memory(nc, ctx, "w")
        natural = m.sb("natural", [P, 6, KT, D])
        turned = m.sb("turned", [P, 6, KT, D])
        q_scale = m.sb("q_scale", [P, KT])
        wqh = m.sb("wqh", [P, KT, D])
        light_w = m.sb("light_w", [P, 3, KT, D])
        gam = m.sb("gam", [P, 2, KT])
        gate_in = m.sb("gate_in", [P, 2])
        tp = m.ps("tp", [P, 2, KT, P])
        loaded = m.sem("loaded")
        small_loaded = m.sem("small_loaded")
        ident_made = m.sem("ident_made")
        consts_made = m.sem("consts_made")
        scaled = m.sem("scaled")
        transposed = m.sem("transposed")
        copied = m.sem("copied")
        stored = m.sem("stored")
        gated = m.sem("gated")
        block = ctx.enter_context(nc.Block())
        N_TURN = 6 * KT

        @block.sync
        def _(sp):
            for i, w in enumerate(("L0_xattn_W_q", "L0_xattn_W_k", "L0_xattn_W_v", "L0_xattn_W_o")):
                sp.dma_start(natural[:, i], t[w].rearrange("(o p) d -> p o d", p=P)).then_inc(loaded, 16)
            for i in range(2):
                sp.dma_start(natural[:, 4 + i],
                             t["L0_ffn_wkv_heavy"][i * D:(i + 1) * D, :].rearrange("(o p) d -> p o d", p=P)
                             ).then_inc(loaded, 16)
            sp.dma_start(wqh[:], t["L0_ffn_wq_heavy"].rearrange("(k p) o -> p k o", p=P)).then_inc(loaded, 16)
            sp.dma_start(light_w[:, 0], t["L0_ffn_wq_light"].rearrange("(k p) o -> p k o", p=P)).then_inc(loaded, 16)
            for i in range(2):
                sp.dma_start(light_w[:, 1 + i],
                             t["L0_ffn_wkv_light"][:, i * D:(i + 1) * D].rearrange("(k p) o -> p k o", p=P)
                             ).then_inc(loaded, 16)
            sp.wait_ge(copied, N_TURN)
            for i in range(3):
                for g in range(NG):
                    sp.dma_start(t["xattn_wt"][g, i], turned[:, i, :, g * P:(g + 1) * P]).then_inc(stored, 16)
            sp.dma_start(t["xattn_wo_t"], turned[:, 3]).then_inc(stored, 16)
            for hp in range(HP):
                half, at = hp // 2, (hp % 2) * 2 * P
                cols = turned[:, 4 + half, :, at:at + 2 * P].rearrange("p k (h s d) -> p k h s d", h=2, s=2)
                for s in range(2):
                    for h in range(2):
                        sp.dma_start(t["heavy_wt"][hp, 1 + s, :, :, h * FD:(h + 1) * FD],
                                     cols[:, :, h, s]).then_inc(stored, 16)
            sp.wait_ge(scaled, 1 + KT * 5)
            for hp in range(HP):
                sp.dma_start(t["heavy_wt"][hp, 0], wqh[:, :, hp * P:(hp + 1) * P]).then_inc(stored, 16)
            sp.dma_start(t["light_wt"].rearrange("i p k o -> p i k o"), light_w[:]).then_inc(stored, 16)
            sp.wait_ge(stored, 16 * (3 * NG + 1 + HP * 4 + HP + 1))

        @block.gpsimd
        def _(pool):
            nc.gpsimd.memset(keep["ident"][:], 0.0).then_inc(ident_made, 1)
            pool.wait_ge(ident_made, 1)
            nc.gpsimd.affine_select(out=keep["ident"][:], in_=keep["ident"][:], compare_op=ALU.not_equal, fill=1.0,
                                    base=0, pattern=[[-1, P]], channel_multiplier=1).then_inc(ident_made, 1)
            nc.gpsimd.memset(keep["ones"][:], 1.0).then_inc(consts_made, 1)
            nc.gpsimd.memset(keep["minus_half"][:], -0.5).then_inc(consts_made, 1)
            for h in range(XH):
                nc.gpsimd.memset(keep["slopes"][:, h:h + 1], slope(h)).then_inc(consts_made, 1)
            nc.gpsimd.memset(keep["before"][:], 1.0).then_inc(consts_made, 1)
            nc.gpsimd.memset(keep["after"][:], 1.0).then_inc(consts_made, 1)
            pool.wait_ge(consts_made, XH + 4)
            nc.gpsimd.affine_select(out=keep["before"][:], in_=keep["before"][:], compare_op=ALU.is_gt, fill=0.0,
                                    base=0, pattern=[[-1, P]], channel_multiplier=1).then_inc(consts_made, 1)
            nc.gpsimd.affine_select(out=keep["after"][:], in_=keep["after"][:], compare_op=ALU.is_gt, fill=0.0,
                                    base=0, pattern=[[1, P]], channel_multiplier=-1).then_inc(consts_made, 1)

        @block.scalar
        def _(act):
            for i, n in enumerate(("g_xattn", "g_ffn")):
                act.dma_start(gate_in[:, i:i + 1], t[n].rearrange("(a n) -> a n", a=1).to_broadcast([P, 1])
                              ).then_inc(small_loaded, 16)
            for i, n in enumerate(("L0_ffn_gamma_light", "L0_ffn_gamma_heavy")):
                act.dma_start(gam[:, i], t[n].rearrange("(k p) -> p k", p=P),
                              allow_slow_non_contiguous=True).then_inc(small_loaded, 16)
            act.wait_ge(small_loaded, 64)
            act.activation(keep["gates"][:], gate_in[:], ACT.Tanh).then_inc(gated, 1)
            for n in range(N_TURN):
                which, kt = divmod(n, KT)
                act.wait_ge(transposed, n + 1)
                dst = turned[:, which, kt]
                if which >= 4:
                    act.activation(dst, tp[:, n % 2].rearrange("p o c -> p (o c)"), ACT.Copy,
                                   scale=gam[:, 1, kt:kt + 1]).then_inc(copied, 1)
                else:
                    act.activation(dst, tp[:, n % 2].rearrange("p o c -> p (o c)"), ACT.Copy).then_inc(copied, 1)

        @block.vector
        def _(dve):
            for o in range(KT):
                for j in range(GH):
                    ins = dve.memset(q_scale[j * XD:(j + 1) * XD, o:o + 1],
                                     -(1.0 / np.sqrt(XD)) / slope(o * GH + j))
            ins.then_inc(scaled, 1)
            dve.wait_ge(scaled, 1)
            dve.wait_ge(loaded, 160)
            for o in range(KT):
                dve.tensor_scalar(natural[:, 0, o], natural[:, 0, o], q_scale[:, o:o + 1], None,
                                  ALU.mult).then_inc(scaled, 1)
            dve.wait_ge(small_loaded, 64)
            for k in range(KT):
                dve.tensor_scalar(wqh[:, k], wqh[:, k], gam[:, 1, k:k + 1], -float(FD) ** -0.5,
                                  ALU.mult, ALU.mult).then_inc(scaled, 1)
                for i in range(3):
                    dve.tensor_scalar(light_w[:, i, k], light_w[:, i, k], gam[:, 0, k:k + 1], None,
                                      ALU.mult).then_inc(scaled, 1)

        @block.tensor
        def _(pe):
            pe.wait_ge(ident_made, 2)
            pe.wait_ge(loaded, 160)
            pe.wait_ge(scaled, 1 + KT)
            for n in range(N_TURN):
                which, kt = divmod(n, KT)
                if n >= 2:
                    pe.wait_ge(copied, n - 1)
                for o in range(KT):
                    ins = pe.transpose(tp[:, n % 2, o], natural[:, which, o, kt * P:(kt + 1) * P], keep["ident"][:])
                ins.then_inc(transposed, 1)




def cross_attention(nc, t, keep, batches=B):
    with ExitStack() as ctx:
        m = Memory(nc, ctx, "x")
        ctx_t = m.sb("ctx_t", [P, KT, S])
        xn_t = m.sb("xn_t", [P, KT, S])
        dist = m.sb("dist", [P, NT, S])
        prob = m.sb("prob", [P, 3, S])
        prob_t = m.sb("prob_t", [P, 2, GH, NT, 2 * P])
        attn_t = m.sb("attn_t", [P, NG, S])
        w_qk = m.sb("w_qk", [P, 2, KT, P])
        w_v = m.sb("w_v", [P, KT, P])
        part = m.sb("part", [P, 2, S], F16)
        q_stack = m.sb("q_stack", [P, 2, GH, S], F16)
        k_stack = m.sb("k_stack", [P, 2, GH, S], F16)
        v_g = m.sb("v_g", [P, NT, P])
        neg_max = m.sb("neg_max", [P, NT * GH])
        row_sum = m.sb("row_sum", [P, NT * GH])
        den = m.sb("den", [P, 2, GH])
        inv = m.sb("inv", [P, 2, GH])
        den_wide = m.sb("den_wide", [P, 2, GH, XD])
        den_t = m.sb("den_t", [P, 2 * P])
        stats = m.sb("stats", [P, NT, 6])
        mean_var = m.sb("mean_var", [P, NT, 2])
        small = m.sb("small", [P, 6, NT])
        route = m.sb("route", [P, 2, NT])
        pos_i = m.sb("pos_i", [P, NT], I32)
        pos_f = m.sb("pos_f", [P, NT])
        flat = prob_t[:].rearrange("p a b c d -> p (a b c d)")
        xs = flat[:, 0:NT * D].rearrange("p (t d) -> p t d", d=D)
        cs = flat[:, NT * D:2 * NT * D].rearrange("p (t d) -> p t d", d=D)
        rest = flat[:, 2 * NT * D:]
        mask = rest.bitcast(I32).rearrange("p (t s) -> p t s", s=S)
        junk = rest[:, 0:D]
        tokens = rest[:, D:3 * D].rearrange("p (w d) -> p w d", d=D)
        wo_t = rest[:, 3 * D:(3 + KT) * D].rearrange("p (k d) -> p k d", d=D)
        kpos_i = prob[:, 0].bitcast(I32)
        kpos_neg = prob[:, 1]

        score_ps = m.ps("score_ps", [P, 2, S])
        turn_ps = m.ps("turn_ps", [P, 2, KT, P])
        attn_ps = m.ps("attn_ps", [P, 512])
        spare_ps = m.ps("spare_ps", [P, 512])

        x_in, c_in, mask_in, pos_in = m.sem("x_in"), m.sem("c_in"), m.sem("mask_in"), m.sem("pos_in")
        x_again, k_in, out_stored = m.sem("x_again"), m.sem("k_in"), m.sem("out_stored")
        q_in = [m.sem(f"q_in{c}") for c in range(2)]
        w_qk_in, w_v_in, w_o_in = m.sem("w_qk_in"), m.sem("w_v_in"), m.sem("w_o_in")
        dve_did, pool_did = m.sem("dve_did"), m.sem("pool_did")
        turned, turned_out = m.sem("turned"), m.sem("turned_out")
        qk_made, v_made = m.sem("qk_made"), m.sem("v_made")
        high_done, low_done, v_out = m.sem("high_done"), m.sem("low_done"), m.sem("v_out")
        scored, biased, exped = m.sem("scored"), m.sem("biased"), m.sem("exped")
        turn_a, turn_b, out_a, out_b = m.sem("turn_a"), m.sem("turn_b"), m.sem("out_a"), m.sem("out_b")
        den_made, inverted, widened = m.sem("den_made"), m.sem("inverted"), m.sem("widened")
        den_turned, den_out = m.sem("den_turned"), m.sem("den_out")
        attended, normed = m.sem("attended"), m.sem("normed")
        projected, x1_made = m.sem("projected"), m.sem("x1_made")
        passed = m.sem("passed")
        block = ctx.enter_context(nc.Block())

        STEPS = NT * GH
        ALL = NG * STEPS
        PER_PAIR = 2 * GH
        GP = STEPS // PER_PAIR
        PAIRS = ALL // PER_PAIR
        QK_PARTS = NG * 4
        V_PARTS = NG * 2
        LN_MARKS = 3 * NT + 1
        TO_END = LN_MARKS + 2 + 2 * NT
        TO_SQUARES = TO_END + LN_MARKS + NT + 1
        DVE_BATCH = TO_SQUARES + 2 * NT + 1 + NT
        POOL_BATCH = 3
        TURNS = 3 * NT
        WINDOWS = [("v", 0), ("v", 1), ("k", 0), ("k", 1), None, ("q", 0), ("q", 1), None]
        WINDOW_AT = (3, 6)
        ATTEND_AT = {1: (0, 3), 2: (3, 6), 5: (6, NT)}

        def window_of(n, stage):
            for w, at in enumerate(WINDOW_AT):
                first = n - stage
                if first >= 0 and first % PER_PAIR == at:
                    g, pair = divmod(first // PER_PAIR, GP)
                    kind = WINDOWS[2 * pair + w]
                    if kind and (kind[0] == "v" or g + 1 < NG):
                        return (g + (kind[0] != "v"), *kind)
            return None

        def qk_part(g, kind, c):
            return 4 * g + 2 * (kind == "q") + c

        @block.sync
        def _(sp):
            def load_qk(g):
                sp.dma_start(w_qk[:], t["xattn_wt"][g, 0:2].rearrange("i p k o -> p i k o")).then_inc(w_qk_in, 16)

            def load_v(g):
                sp.dma_start(w_v[:], t["xattn_wt"][g, 2]).then_inc(w_v_in, 16)

            def stack_up(b, g, kind, c):
                after(sp, low_done, b * QK_PARTS + qk_part(g, kind, c) + 1)
                cols = slice(0, S) if kind == "k" else slice(c * 512, (c + 1) * 512)
                for r in range(4):
                    for j in range(GH):
                        which = r // 2 if kind == "k" else r % 2
                        stack = k_stack if kind == "k" else q_stack
                        sp.dma_start(stack[r * XD:(r + 1) * XD, g % 2, j, cols],
                                     part[j * XD:(j + 1) * XD, which, cols]
                                     ).then_inc(k_in if kind == "k" else q_in[c], 16)

            with sp.Fori(0, batches) as b:
                load_qk(0)
                load_v(0)
                sp.dma_start(cs, t["ctx_1024"][bass.ds(b, 1)].rearrange("a (t p) d -> p (a t) d", p=P)).then_inc(c_in, 16)
                sp.dma_start(xs, t["x"][bass.ds(b, 1)].rearrange("a (t p) d -> p (a t) d", p=P)).then_inc(x_in, 16)
                sp.dma_start(kpos_i, t["itok_BxS2_1_8191"][bass.ds(b, 1)].to_broadcast([P, S])).then_inc(pos_in, 16)
                sp.dma_start(pos_i[:], t["itok_BxS_8_8191"][bass.ds(b, 1)].rearrange("a (t p) -> p (a t)", p=P),
                             allow_slow_non_contiguous=True).then_inc(pos_in, 16)
                sp.dma_start(mask, t["mask_BxSxS2_if1"][bass.ds(b, 1)].rearrange("a (t p) s -> p (a t) s", p=P)
                             ).then_inc(mask_in, 16)
                stack_up(b, 0, "k", 1)
                stack_up(b, 0, "q", 0)
                stack_up(b, 0, "q", 1)
                for g in range(NG):
                    if g + 1 < NG:
                        sp.wait_ge(qk_made, b * QK_PARTS + 4 * g + 4)
                        load_qk(g + 1)
                        sp.wait_ge(v_made, b * V_PARTS + 2 * g + 2)
                        load_v(g + 1)
                        stack_up(b, g + 1, "k", 1)
                        stack_up(b, g + 1, "q", 0)
                        stack_up(b, g + 1, "q", 1)
                after(sp, attended, (b + 1) * PAIRS)
                sp.dma_start(xs, t["x"][bass.ds(b, 1)].rearrange("a (t p) d -> p (a t) d", p=P)).then_inc(x_again, 16)
                sp.dma_start(wo_t, t["xattn_wo_t"]).then_inc(w_o_in, 16)
                for i, n in enumerate(("L0_ffn_q_routing_token", "L0_ffn_kv_routing_token")):
                    sp.dma_start(tokens[:, i], t[n].rearrange("(a n) -> a n", a=1).to_broadcast([P, D])
                                 ).then_inc(w_o_in, 16)
                sp.wait_ge(dve_did, (b + 1) * DVE_BATCH)
                sp.dma_start(t["x1"][bass.ds(b, 1)].rearrange("a (t p) d -> p (a t) d", p=P), cs).then_inc(out_stored, 16)
                sp.dma_start(t["yn"][bass.ds(b, 1)].rearrange("a (t p) d -> p (a t) d", p=P), xs).then_inc(out_stored, 16)
                after(sp, turned_out, (b + 1) * TURNS)
                sp.dma_start(t["yn_t"][bass.ds(b, 1)].rearrange("a p k s -> p (a k) s"), xn_t[:]).then_inc(out_stored, 16)
                sp.wait_ge(out_stored, (b + 1) * 48)
                alone(sp, passed)

        @block.gpsimd
        def _(pool):
            prime(pool, widened)
            with pool.Fori(0, batches) as b:
                def power(slot, at):
                    pool.wait_ge(dve_did, b * DVE_BATCH + at)
                    nc.gpsimd.tensor_tensor(small[:, slot + 1], small[:, slot], keep["minus_half"][:], ALU.pow
                                            ).then_inc(pool_did, 1)
                power(0, 2 * NT + 1)
                for q in range(NG * NT):
                    pool.wait_ge(exped, b * ALL + (q + 1) * GH)
                    alone(pool, passed)
                    cols = q % NT * GH
                    nc.gpsimd.tensor_scalar(den[:, q % 2], row_sum[:, cols:cols + GH], 1.0, 1.0,
                                            ALU.add, ALU.mult).then_inc(den_made, 1)
                    after(pool, den_turned, b * NG * NT + max(q - 1, 0))
                    pool.wait_ge(inverted, b * NG * NT + q + 1)
                    alone(pool, passed)
                    nc.gpsimd.tensor_scalar(den_wide[:, q % 2],
                                            inv[:, q % 2].unsqueeze(2).to_broadcast([P, GH, XD]), 1.0, 1.0,
                                            ALU.mult, ALU.mult).then_inc(widened, 1)
                power(2, TO_END + 2 * NT + 1)
                power(4, TO_SQUARES)

        @block.scalar
        def _(act):
            prime(act, turned_out, out_a, den_out)
            with act.Fori(0, batches) as b:
                def turn_out(first, dst):
                    for i in range(NT):
                        act.wait_ge(turned, b * TURNS + first + i + 1)
                        act.activation(dst[:, :, i * P:(i + 1) * P], turn_ps[:, i % 2], ACT.Copy).then_inc(turned_out, 1)

                def high(g, kind, c, src):
                    act.wait_ge(qk_made, b * QK_PARTS + qk_part(g, kind, c) + 1)
                    if kind == "q" and c == 0:
                        act.wait_ge(k_in, (b * NG + g + 1) * 256)
                    elif kind == "k" and c == 0:
                        if g:
                            for h in range(2):
                                act.wait_ge(q_in[h], (b * NG + g) * 256)
                        else:
                            after(act, scored, b * ALL)
                    act.activation(part[:, 0, c * 512:(c + 1) * 512], src, ACT.Copy).then_inc(high_done, 1)

                def expo(n):
                    after(act, biased, b * ALL + n + 1)
                    s = n % STEPS
                    act.activation(prob[:, n % 3], prob[:, n % 3], ACT.Exp, scale=-1.0, bias=neg_max[:, s:s + 1],
                                   accum_out=row_sum[:, s:s + 1]).then_inc(exped, 1)

                def inverse_out(pair):
                    after(act, den_turned, b * NG * NT + 2 * pair + 2)
                    after(act, normed, b * PAIRS + pair)
                    act.activation(den_t[:], spare_ps[:, 0:2 * P], ACT.Copy).then_inc(den_out, 1)

                turn_out(0, ctx_t)
                turn_out(NT, xn_t)
                for n, (kind, c) in enumerate((("k", 0), ("k", 1), ("q", 0), ("q", 1))):
                    high(0, kind, c, score_ps[:, n // 2, c * 512:(c + 1) * 512])
                expo(0)
                for n in range(ALL):
                    pair = n // PER_PAIR
                    if n + 1 < ALL:
                        expo(n + 1)
                    if n % PER_PAIR == 0:
                        after(act, attended, b * PAIRS + max(pair - 1, 0))
                    act.wait_ge(turn_a, b * ALL + n + 1)
                    half = n // GH % 2
                    act.activation(prob_t[:, pair % 2, n % GH, 0:4, half * P:(half + 1) * P], turn_ps[:, 0],
                                   ACT.Copy).then_inc(out_a, 1)
                    if n % PER_PAIR == 2 and pair:
                        inverse_out(pair - 1)
                    w = window_of(n, 2)
                    if w and w[1] == "v":
                        act.wait_ge(v_made, b * V_PARTS + 2 * w[0] + w[2] + 1)
                        after(act, attended, b * PAIRS + w[0] * GP)
                        act.activation(v_g[:, 4 * w[2]:4 * w[2] + 4], spare_ps[:].rearrange("p (i o) -> p i o", o=P),
                                       ACT.Copy).then_inc(v_out, 1)
                    elif w:
                        high(*w, spare_ps[:])
                inverse_out(PAIRS - 1)
                turn_out(2 * NT, xn_t)

        @block.vector
        def _(dve):
            prime(dve, normed, biased, x1_made, out_b, low_done)
            with dve.Fori(0, batches) as b:
                done = Chain(dve, dve_did, b * DVE_BATCH)

                def layer_norm(rows, slot):
                    for i in range(NT):
                        done.mark(dve.bn_stats(stats[:, i], rows[:, i]))
                    done.wait()
                    alone(dve, passed)
                    for i in range(NT):
                        done.mark(dve.bn_aggr(mean_var[:, i], stats[:, i]))
                    done.wait()
                    done.mark(dve.tensor_scalar(small[:, slot], mean_var[:, :, 1], LN_EPS, None, ALU.add))
                    dve.wait_ge(pool_did, b * POOL_BATCH + slot // 2 + 1)
                    for i in range(NT):
                        done.mark(dve.tensor_scalar(xs[:, i], rows[:, i], mean_var[:, i, 0:1],
                                                    small[:, slot + 1, i:i + 1], ALU.subtract, ALU.mult))

                def low(g, kind, c, src):
                    dve.wait_ge(high_done, b * QK_PARTS + qk_part(g, kind, c) + 1)
                    cols = slice(c * 512, (c + 1) * 512)
                    dve.tensor_tensor(part[:, 1, cols], src, part[:, 0, cols], ALU.subtract).then_inc(low_done, 1)

                def bias(n):
                    g, s = divmod(n, STEPS)
                    qt, j = divmod(s, GH)
                    after(dve, scored, b * ALL + n + 1)
                    if n >= 3:
                        dve.wait_ge(turn_b, b * ALL + n - 2)
                    alone(dve, passed)
                    dve.tensor_tensor_reduce(out=prob[:, n % 3], in0=dist[:, qt], in1=score_ps[:, n % 2],
                                             scale=keep["slopes"][:, g * GH + j:g * GH + j + 1], scalar=3.0e38,
                                             op0=ALU.add, op1=ALU.min,
                                             accum_out=neg_max[:, s:s + 1]).then_inc(biased, 1)

                def invert(q):
                    dve.wait_ge(den_made, b * NG * NT + q + 1)
                    after(dve, widened, b * NG * NT + max(q - 1, 0))
                    dve.reciprocal(inv[:, q % 2], den[:, q % 2]).then_inc(inverted, 1)

                def norm(pair):
                    g, at = divmod(pair, GP)
                    after(dve, attended, b * PAIRS + pair + 1)
                    after(dve, den_out, b * PAIRS + pair + 1)
                    dve.tensor_tensor(attn_t[:, g, at * 2 * P:(at + 1) * 2 * P], attn_ps[:, 0:2 * P], den_t[:],
                                      ALU.mult).then_inc(normed, 1)

                dve.wait_ge(x_in, (b + 1) * 16)
                layer_norm(xs, 0)
                dve.wait_ge(pos_in, (b + 1) * 32)
                done.mark(dve.tensor_scalar(kpos_neg, kpos_i, -1.0, None, ALU.mult))
                done.mark(dve.tensor_copy(pos_f[:], pos_i[:]))
                dve.wait_ge(mask_in, (b + 1) * 16)
                for i in range(NT):
                    done.mark(dve.tensor_scalar(dist[:, i], mask[:, i], 0.0, MASKED, ALU.is_equal, ALU.mult))
                done.wait()
                for i in range(NT):
                    done.mark(dve.scalar_tensor_tensor(dist[:, i], kpos_neg, pos_f[:, i:i + 1], dist[:, i],
                                                       ALU.add, ALU.add))
                for n, (kind, c) in enumerate((("k", 0), ("k", 1), ("q", 0), ("q", 1))):
                    low(0, kind, c, score_ps[:, n // 2, c * 512:(c + 1) * 512])
                done.wait()
                bias(0)
                bias(1)
                for n in range(ALL):
                    pair, at = divmod(n, PER_PAIR)
                    if n + 2 < ALL:
                        bias(n + 2)
                    if at == 0:
                        after(dve, attended, b * PAIRS + max(pair - 1, 0))
                    dve.wait_ge(turn_b, b * ALL + n + 1)
                    half = n // GH % 2
                    dve.tensor_copy(prob_t[:, pair % 2, n % GH, 4:8, half * P:(half + 1) * P], turn_ps[:, 1]
                                    ).then_inc(out_b, 1)
                    if n and n % GH == 0:
                        invert(n // GH - 1)
                    if at == 6 and pair:
                        norm(pair - 1)
                    w = window_of(n, 2)
                    if w and w[1] != "v":
                        low(*w, spare_ps[:])
                invert(NG * NT - 1)
                norm(PAIRS - 1)

                dve.wait_ge(x_again, (b + 1) * 16)
                for i in range(NT):
                    dve.wait_ge(projected, b * NT + i + 1)
                    dve.scalar_tensor_tensor(cs[:, i], score_ps[:, i % 2, 0:D], keep["gates"][:, 0:1], xs[:, i],
                                             ALU.mult, ALU.add).then_inc(x1_made, 1)
                after(dve, x1_made, (b + 1) * NT)
                layer_norm(cs, 2)
                done.wait()
                for i in range(NT):
                    done.mark(dve.tensor_tensor_reduce(out=junk, in0=xs[:, i], in1=xs[:, i], scale=1.0, scalar=0.0,
                                                       op0=ALU.mult, op1=ALU.add, accum_out=mean_var[:, i, 0:1]))
                    done.wait()
                done.mark(dve.tensor_scalar(small[:, 4], mean_var[:, :, 0], 1e-24, 1.0 / D, ALU.max, ALU.mult))
                dve.wait_ge(w_o_in, (b + 1) * 48)
                for w in range(2):
                    for i in range(NT):
                        done.mark(dve.tensor_tensor_reduce(out=junk, in0=xs[:, i], in1=tokens[:, w], scale=1.0,
                                                           scalar=0.0, op0=ALU.mult, op1=ALU.add,
                                                           accum_out=route[:, w, i:i + 1]))
                        done.wait()
                done.mark(dve.tensor_copy(keep["route_s"][:, :, bass.ds(b, 1), :], route[:].unsqueeze(2)))
                dve.wait_ge(pool_did, (b + 1) * POOL_BATCH)
                for i in range(NT):
                    done.mark(dve.tensor_scalar(xs[:, i], xs[:, i], small[:, 5, i:i + 1], None, ALU.mult))
                assert done.n == DVE_BATCH

        @block.tensor
        def _(pe):
            prime(pe, scored, attended, den_turned)
            with pe.Fori(0, batches) as b:
                def turn_rows(first, rows):
                    for i in range(NT):
                        if i >= 2:
                            after(pe, turned_out, b * TURNS + first + i - 1)
                        for k in range(KT):
                            ins = pe.transpose(turn_ps[:, i % 2, k], rows[:, i, k * P:(k + 1) * P], keep["ident"][:])
                        ins.then_inc(turned, 1)

                def project(g, kind, c, out, k):
                    w, src = (1, ctx_t) if kind == "k" else (0, xn_t)
                    ins = pe.matmul(out, w_qk[:, w, k], src[:, k, c * 512:(c + 1) * 512], start=k == 0, stop=k == KT - 1)
                    if k == KT - 1:
                        ins.then_inc(qk_made, 1)

                def fill(w, stage):
                    g, kind, c = w
                    if stage == 0:
                        if kind == "v":
                            after(pe, low_done, b * QK_PARTS + 4 * g + 4)
                            pe.wait_ge(w_v_in, (b * NG + g + 1) * 16)
                            if c:
                                pe.wait_ge(v_out, b * V_PARTS + 2 * g + 1)
                        else:
                            pe.wait_ge(v_out, b * V_PARTS + 2 * g)
                            after(pe, low_done, b * QK_PARTS + qk_part(g, kind, c))
                            pe.wait_ge(w_qk_in, (b * NG + g + 1) * 16)
                        after(pe, den_out, b * PAIRS + done_pairs[0])
                    if kind == "v":
                        for i in range(2):
                            i += 2 * stage
                            for k in range(KT):
                                ins = pe.matmul(spare_ps[:, i * P:(i + 1) * P], ctx_t[:, k, (4 * c + i) * P:(4 * c + i + 1) * P],
                                                w_v[:, k], start=k == 0, stop=k == KT - 1)
                        if stage:
                            ins.then_inc(v_made, 1)
                    else:
                        for k in range(2):
                            project(g, kind, c, spare_ps[:], 2 * stage + k)

                def score(n):
                    g, s = divmod(n, STEPS)
                    qt, j = divmod(s, GH)
                    if n >= 2:
                        after(pe, biased, b * ALL + n - 1)
                    if s == 0:
                        pe.wait_ge(k_in, (b * NG + g + 1) * 256)
                        pe.wait_ge(q_in[0], (b * NG + g + 1) * 256)
                    if s == STEPS // 2:
                        pe.wait_ge(q_in[1], (b * NG + g + 1) * 256)
                    for c in range(2):
                        ins = pe.matmul(score_ps[:, n % 2, c * 512:(c + 1) * 512], q_stack[:, g % 2, j, qt * P:(qt + 1) * P],
                                        k_stack[:, g % 2, j, c * 512:(c + 1) * 512], start=True, stop=True)
                    ins.then_inc(scored, 1)

                def turn_inverses(pair):
                    for q in (2 * pair, 2 * pair + 1):
                        after(pe, widened, b * NG * NT + q + 1)
                        ins = pe.transpose(spare_ps[:, (q % 2) * P:(q % 2 + 1) * P],
                                           den_wide[:, q % 2].rearrange("p h d -> p (h d)"), keep["ident"][:])
                        ins.then_inc(den_turned, 1)

                def attend(pair, first, last):
                    if first == 0:
                        after(pe, out_a, b * ALL + (pair + 1) * PER_PAIR)
                        after(pe, out_b, b * ALL + (pair + 1) * PER_PAIR)
                        after(pe, normed, b * PAIRS + pair)
                        if pair % GP == 0:
                            pe.wait_ge(v_out, b * V_PARTS + (pair // GP) * 2 + 2)
                    for k in range(first, last):
                        for j in range(GH):
                            ins = pe.matmul(attn_ps[j * XD:(j + 1) * XD, 0:2 * P], v_g[:, k, j * XD:(j + 1) * XD],
                                            prob_t[:, pair % 2, j, k], start=k == 0, stop=k == NT - 1)
                    if last == NT:
                        ins.then_inc(attended, 1)

                after(pe, turned_out, b * TURNS)
                pe.wait_ge(c_in, (b + 1) * 16)
                turn_rows(0, cs)
                after(pe, turned_out, b * TURNS + NT)
                pe.wait_ge(dve_did, b * DVE_BATCH + 3 * NT + 1)
                turn_rows(NT, xs)
                after(pe, turned_out, b * TURNS + 2 * NT)
                pe.wait_ge(w_qk_in, (b * NG + 1) * 16)
                after(pe, x1_made, b * NT)
                for n, (kind, c) in enumerate((("k", 0), ("k", 1), ("q", 0), ("q", 1))):
                    for k in range(KT):
                        project(0, kind, c, score_ps[:, n // 2, c * 512:(c + 1) * 512], k)
                after(pe, low_done, b * QK_PARTS + 4)
                score(0)
                score(1)
                done_pairs = [0]
                for n in range(ALL):
                    if n + 2 < ALL:
                        score(n + 2)
                    pe.wait_ge(exped, b * ALL + n + 1)
                    for h, (sem, out) in enumerate(((turn_a, out_a), (turn_b, out_b))):
                        after(pe, out, b * ALL + n)
                        for k in range(4):
                            ins = pe.transpose(turn_ps[:, h, k], prob[:, n % 3, (4 * h + k) * P:(4 * h + k + 1) * P],
                                               keep["ident"][:])
                        ins.then_inc(sem, 1)
                    if n % PER_PAIR == 1 and n > 1:
                        pair = n // PER_PAIR - 1
                        w = window_of(n - 1, 2)
                        if w and w[1] == "v":
                            pe.wait_ge(v_out, b * V_PARTS + 2 * w[0] + w[2] + 1)
                        elif w:
                            after(pe, low_done, b * QK_PARTS + qk_part(*w) + 1)
                        turn_inverses(pair)
                        done_pairs[0] = pair + 1
                    if n > PER_PAIR and n % PER_PAIR in ATTEND_AT:
                        attend(n // PER_PAIR - 1, *ATTEND_AT[n % PER_PAIR])
                    for stage in range(2):
                        w = window_of(n, stage)
                        if w:
                            fill(w, stage)
                attend(PAIRS - 1, 0, NT)
                turn_inverses(PAIRS - 1)
                after(pe, normed, (b + 1) * PAIRS)
                after(pe, biased, (b + 1) * ALL)
                pe.wait_ge(w_o_in, (b + 1) * 48)
                for i in range(NT):
                    if i >= 2:
                        after(pe, x1_made, b * NT + i - 1)
                    for k in range(KT):
                        ins = pe.matmul(score_ps[:, i % 2, 0:D], attn_t[:, k, i * P:(i + 1) * P], wo_t[:, k],
                                        start=k == 0, stop=k == KT - 1)
                    ins.then_inc(projected, 1)
                pe.wait_ge(dve_did, (b + 1) * DVE_BATCH)
                after(pe, out_a, (b + 1) * ALL)
                after(pe, out_b, (b + 1) * ALL)
                turn_rows(2 * NT, xs)


def light_attention(nc, t, keep):
    with ExitStack() as ctx:
        m = Memory(nc, ctx, "l")
        W = D // P
        w_qkv = m.sb("w_qkv", [P, 3, KT, D])
        w_o = m.sb("w_o", [P, KT, D])
        y_t = m.sb("y_t", [P, 2, KT, D])
        x1 = m.sb("x1", [P, 2, W, D])
        qk_t = m.sb("qk_t", [P, 2, KT, D])
        v = m.sb("v", [P, W, D])
        prob = m.sb("prob", [P, 2, 2, HP, P])
        prob_t = m.sb("prob_t", [P, 2, 2, HP, P])
        attn_t = m.sb("attn_t", [P, 2, HP, P])
        top = m.sb("top", [P, 2, FH])
        total = m.sb("total", [P, 2, FH])
        inv = m.sb("inv", [P, 2, FH])
        score_ps = m.ps("score_ps", [P, 2, HP, P])
        turn_ps = m.ps("turn_ps", [P, 2, HP, P])
        attn_ps = m.ps("attn_ps", [P, HP, P])
        proj_ps = m.ps("proj_ps", [P, 2, D])
        w_in, stored, passed = m.sem("w_in"), m.sem("stored"), m.sem("passed")
        y_in = [m.sem(f"y_in{half}") for half in range(2)]
        x_in = [m.sem(f"x_in{half}") for half in range(2)]
        projected, proj_out = m.sem("projected"), m.sem("proj_out")
        scored, topped, shifted, exped = m.sem("scored"), m.sem("topped"), m.sem("shifted"), m.sem("exped")
        summed, inverted, scaled = m.sem("summed"), m.sem("inverted"), m.sem("scaled")
        turned, turned_out, attended, attn_out = m.sem("turned"), m.sem("turned_out"), m.sem("attended"), m.sem("attn_out")
        out_made, result = m.sem("out_made"), m.sem("result")
        block = ctx.enter_context(nc.Block())
        PROJ = 3 * KT
        SLOTS = PROJ + W

        def loop(eng):
            return eng.Fori(0, B)

        @block.sync
        def _(sp):
            sp.dma_start(w_qkv[:], t["light_wt"].rearrange("i p k o -> p i k o")).then_inc(w_in, 16)
            sp.dma_start(w_o[:], t["L0_ffn_wo_light"].rearrange("(k p) o -> p k o", p=P)).then_inc(w_in, 16)
            with loop(sp) as b:
                for half in range(2):
                    n = b * 2 + half
                    after(sp, projected, b * 2 * PROJ + max(half - 1, 0) * PROJ)
                    sp.dma_start(y_t[:, half], t["yn_t"][bass.ds(b, 1), :, :, half * D:(half + 1) * D]
                                 .rearrange("a p k s -> p (a k) s")).then_inc(y_in[half], 16)
                    sp.dma_start(x1[:, half], t["x1"][bass.ds(b, 1), half * D:(half + 1) * D]
                                 .rearrange("a (t p) d -> p (a t) d", p=P)).then_inc(x_in[half], 16)
                for half in range(2):
                    after(sp, result, (b * 2 + half + 1) * W)
                    sp.dma_start(t["mid"][bass.ds(b, 1), half * D:(half + 1) * D]
                                 .rearrange("a (t p) d -> p (a t) d", p=P), x1[:, half]).then_inc(stored, 16)
                sp.wait_ge(stored, (b + 1) * 32)
                alone(sp, passed)

        @block.gpsimd
        def _(pool):
            with loop(pool) as b:
                for w in range(2 * W):
                    n = b * 2 * W + w
                    pool.wait_ge(inverted, n + 1)
                    nc.gpsimd.tensor_tensor(prob[:, w % 2].rearrange("p a b c -> p (a b) c"),
                                            prob[:, w % 2].rearrange("p a b c -> p (a b) c"),
                                            inv[:, w % 2].unsqueeze(2).to_broadcast([P, FH, P]),
                                            ALU.mult).then_inc(scaled, 1)

        @block.scalar
        def _(act):
            prime(act, proj_out, turned_out, attn_out)
            with loop(act) as b:
                for half in range(2):
                    n = b * 2 + half
                    for i in range(PROJ):
                        after(act, projected, n * PROJ + i + 1)
                        dst = qk_t[:, i // KT, i % KT] if i < 2 * KT else v[:, i % KT]
                        if i == 0:
                            after(act, scored, n * W)
                            after(act, attended, n * W)
                        act.activation(dst, proj_ps[:, i % 2], ACT.Copy).then_inc(proj_out, 1)
                    for w in range(W):
                        nw = n * W + w
                        after(act, shifted, nw + 1)
                        act.activation(prob[:, w % 2], prob[:, w % 2], ACT.Exp, scale=float(FD) ** -0.5).then_inc(exped, 1)
                        after(act, turned, nw + 1)
                        act.activation(prob_t[:, w % 2], turn_ps[:], ACT.Copy).then_inc(turned_out, 1)
                        after(act, attended, nw + 1)
                        act.activation(attn_t[:, w % 2], attn_ps[:], ACT.Copy).then_inc(attn_out, 1)

        @block.vector
        def _(dve):
            prime(dve, result, shifted)
            with loop(dve) as b:
                for half in range(2):
                    n = b * 2 + half
                    for w in range(W):
                        nw = n * W + w
                        after(dve, scored, nw + 1)
                        dve.reduce_max(top[:, w % 2], score_ps[:].rearrange("p a b c -> p (a b) c"), AX.X
                                       ).then_inc(topped, 1)
                        dve.wait_ge(topped, nw + 1)
                        after(dve, turned, b * 2 * W + max(half * W + w - 1, 0))
                        dve.tensor_tensor(prob[:, w % 2].rearrange("p a b c -> p (a b) c"),
                                          score_ps[:].rearrange("p a b c -> p (a b) c"),
                                          top[:, w % 2].unsqueeze(2).to_broadcast([P, FH, P]),
                                          ALU.subtract).then_inc(shifted, 1)
                        if w:
                            finish(w - 1)
                        else:
                            def finish(w):
                                dve.wait_ge(out_made, n * W + w + 1)
                                if w == 0:
                                    dve.wait_ge(x_in[half], (b + 1) * 16)
                                dve.scalar_tensor_tensor(x1[:, half, w], proj_ps[:, w % 2], keep["gates"][:, 1:2],
                                                         x1[:, half, w], ALU.mult, ALU.add).then_inc(result, 1)
                        dve.wait_ge(exped, nw + 1)
                        dve.reduce_sum(total[:, w % 2], prob[:, w % 2].rearrange("p a b c -> p (a b) c"), AX.X
                                       ).then_inc(summed, 1)
                        dve.wait_ge(summed, nw + 1)
                        dve.reciprocal(inv[:, w % 2], total[:, w % 2]).then_inc(inverted, 1)
                    finish(W - 1)

        @block.tensor
        def _(pe):
            prime(pe, projected, scored, attended, turned)
            pe.wait_ge(w_in, 32)
            with loop(pe) as b:
                for half in range(2):
                    n = b * 2 + half
                    pe.wait_ge(y_in[half], (b + 1) * 16)
                    after(pe, result, n * W)
                    for i in range(PROJ):
                        after(pe, proj_out, n * PROJ + max(i - 1, 0))
                        for k in range(KT):
                            if i < 2 * KT:
                                lhs, rhs = w_qkv[:, i // KT, k, (i % KT) * P:(i % KT + 1) * P], y_t[:, half, k]
                            else:
                                lhs, rhs = y_t[:, half, k, (i % KT) * P:(i % KT + 1) * P], w_qkv[:, 2, k]
                            ins = pe.matmul(proj_ps[:, i % 2], lhs, rhs, start=k == 0, stop=k == KT - 1)
                        ins.then_inc(projected, 1)
                    after(pe, proj_out, (n + 1) * PROJ)
                    for w in range(W):
                        nw = n * W + w
                        cut = slice(w * P, (w + 1) * P)
                        after(pe, shifted, nw)
                        for h in range(FH):
                            row = (h % 2) * FD
                            ins = pe.matmul(score_ps[:, h % 2, h // 2], qk_t[row:row + FD, 0, h // 2, cut],
                                            qk_t[row:row + FD, 1, h // 2, cut], start=True, stop=True)
                        ins.then_inc(scored, 1)
                        if w:
                            output(w - 1)
                        else:
                            def output(w):
                                after(pe, attn_out, n * W + w + 1)
                                if w >= 2:
                                    after(pe, result, n * W + w - 1)
                                for k in range(HP):
                                    ins = pe.matmul(proj_ps[:, w % 2], attn_t[:, w % 2, k], w_o[:, k],
                                                    start=k == 0, stop=k == HP - 1)
                                ins.then_inc(out_made, 1)
                        pe.wait_ge(scaled, nw + 1)
                        after(pe, turned_out, nw)
                        for h in range(FH):
                            ins = pe.transpose(turn_ps[:, h % 2, h // 2], prob[:, w % 2, h % 2, h // 2], keep["ident"][:])
                        ins.then_inc(turned, 1)
                        after(pe, turned_out, nw + 1)
                        after(pe, attn_out, nw)
                        for h in range(FH):
                            row = (h % 2) * FD
                            ins = pe.matmul(attn_ps[row:row + FD, h // 2], v[:, w, h * FD:(h + 1) * FD],
                                            prob_t[:, w % 2, h % 2, h // 2], start=True, stop=True)
                        ins.then_inc(attended, 1)
                    output(W - 1)


def route(nc, t, keep):
    with ExitStack() as ctx:
        m = Memory(nc, ctx, "r")
        G = 2 * B
        s = keep["route_s"][:].rearrange("p w b t -> p (w b) t")
        log_k = m.sb("log_k", [P, G])
        minus_a = m.sb("minus_a", [P, G])
        part_max = m.sb("part_max", [P, G])
        s_max = m.sb("s_max", [P, G])
        most = m.sb("most", [P, G])
        most_k = m.sb("most_k", [P, G])
        x = m.sb("x", [P, G, NT])
        e = m.sb("e", [P, G, NT])
        part_sum = m.sb("part_sum", [P, G])
        log_sum = m.sb("log_sum", [P, G])
        score = m.sb("score", [P, G, NT])
        rest = m.sb("rest", [P, G, NT])
        score_rows = m.sb("score_rows", [B * NT, P])
        all_scores = m.sb("all_scores", [P, B * NT, P])
        counts = m.sb("counts", [P, B * NT, 4])
        hit = m.sb("hit", [P, S])
        hit_tile = m.sb("hit_tile", [P, P])
        rank = m.sb("rank", [P, B, NT])
        far = m.sb("far", [P, B, NT])
        rows = m.sb("rows", [P, 2, NT, D])
        sum_ps = m.ps("sum_ps", [P, 512])
        turn_ps = m.ps("turn_ps", [P, 512])
        dve_did, act_did, pe_did, pool_did = m.sem("dve_did"), m.sem("act_did"), m.sem("pe_did"), m.sem("pool_did")
        exped, summed, added, logged = m.sem("exped"), m.sem("summed"), m.sem("added"), m.sem("logged")
        step_did = m.sem("step_did")
        score_out, scores_in, rows_in, scattered = m.sem("score_out"), m.sem("scores_in"), [m.sem(f"rows_in{b}") for b in range(B)], [m.sem(f"scattered{b}") for b in range(B)]
        shifted, renewed, scored, ranked = m.sem("shifted"), m.sem("renewed"), m.sem("scored"), m.sem("ranked")
        block = ctx.enter_context(nc.Block())
        N = ITERS - 1

        def wide(a):
            return a.unsqueeze(2).to_broadcast([P, G, NT])

        @block.vector
        def _(dve):
            start = Chain(dve, dve_did)
            start.mark(dve.memset(log_k[:, 0:B], LOG_KQ))
            start.mark(dve.memset(log_k[:, B:G], LOG_KKV))
            start.mark(dve.memset(counts[:], 0.0))
            start.mark(dve.memset(minus_a[:, 0:B], float(np.log(np.float32(S))) - LOG_KQ))
            start.mark(dve.memset(minus_a[:, B:G], float(np.log(np.float32(S))) - LOG_KKV))
            start.mark(dve.reduce_max(part_max[:], s, AX.X))
            dve.wait_ge(pool_did, 1)
            start.wait()
            MARKS = 4
            with dve.Fori(0, N) as i:
                step = Chain(dve, step_did, i * MARKS)
                step.mark(dve.tensor_tensor(most[:], s_max[:], minus_a[:], ALU.min))
                step.mark(dve.tensor_tensor(x[:], s, wide(minus_a[:]), ALU.min))
                step.wait()
                step.mark(dve.tensor_tensor(x[:], x[:], wide(most[:]), ALU.subtract))
                step.mark(dve.tensor_tensor(most_k[:], most[:], log_k[:], ALU.subtract))
                dve.wait_ge(exped, i + 1)
                dve.reduce_sum(part_sum[:], e[:], AX.X).then_inc(summed, 1)
                dve.wait_ge(logged, i + 1)
                dve.tensor_tensor(minus_a[:], log_sum[:], most_k[:], ALU.add).then_inc(renewed, 1)
                dve.wait_ge(renewed, i + 1)
                assert step.n == MARKS
            dve.wait_ge(renewed, N)
            start.mark(dve.tensor_tensor(x[:], s, wide(minus_a[:]), ALU.subtract))
            start.wait()
            start.mark(dve.tensor_scalar(x[:], x[:], 0.0, None, ALU.min))
            FINAL = start.n
            assert FINAL == 8
            dve.wait_ge(scored, 1)
            start.mark(dve.tensor_scalar(rest[:], score[:], -1.0, 1.0, ALU.mult, ALU.add))
            start.wait()
            start.mark(dve.tensor_tensor(keep["factor"][:].rearrange("p w b t -> p (w b) t"), score[:], rest[:], ALU.add))
            start.wait()
            start.mark(dve.tensor_scalar(keep["q_gate"][:].rearrange("p b t -> p (b t)"),
                                         keep["factor"][:, 0].rearrange("p b t -> p (b t)"),
                                         keep["gates"][:, 1:2], None, ALU.mult))
            dve.wait_ge(pe_did, 1)
            start.mark(dve.tensor_copy(score_rows[:], turn_ps[0:B * NT, 0:P]))
            assert start.n == 12
            dve.wait_ge(scores_in, 16)
            for b in range(B):
                for i in range(NT):
                    n = b * NT + i
                    own = score[:, b, i:i + 1]
                    if i:
                        start.mark(dve.tensor_scalar(hit[:, 0:i * P],
                                                     all_scores[:, b * NT:n].rearrange("p a c -> p (a c)"), own,
                                                     None, ALU.is_ge, ALU.add, accum_out=counts[:, n, 0:1]))
                    if i < NT - 1:
                        start.mark(dve.tensor_scalar(hit[:, (i + 1) * P:S],
                                                     all_scores[:, n + 1:(b + 1) * NT].rearrange("p a c -> p (a c)"), own,
                                                     None, ALU.is_gt, ALU.add, accum_out=counts[:, n, 1:2]))
                    for c, (op, half) in enumerate(((ALU.is_ge, "before"), (ALU.is_gt, "after"))):
                        start.mark(dve.scalar_tensor_tensor(hit[:, i * P:(i + 1) * P] if c else hit_tile[:],
                                                            all_scores[:, n], own, keep[half][:],
                                                            op, ALU.mult, accum_out=counts[:, n, 2 + c:3 + c]))
                    start.wait()
            start.mark(dve.reduce_sum(rank[:].rearrange("p b t -> p (b t)"), counts[:], AX.X))
            start.wait()
            start.mark(dve.tensor_scalar(far[:], rank[:], float(NQ), float(OUT_OF_RANGE), ALU.is_ge, ALU.mult))
            start.wait()
            for b in range(B):
                start.mark(dve.scalar_tensor_tensor(far[:, b], rank[:, b], float(b * NQ), far[:, b], ALU.add, ALU.add))
            start.wait()
            dve.tensor_copy(keep["place"][:], far[:]).then_inc(ranked, 1)

        @block.scalar
        def _(act):
            with act.Fori(0, N) as i:
                act.wait_ge(step_did, i * 4 + 3)
                act.activation(e[:], x[:], ACT.Exp).then_inc(exped, 1)
                act.wait_ge(added, i + 1)
                act.activation(log_sum[:], sum_ps[:, 0:G], ACT.Ln).then_inc(logged, 1)
            act.wait_ge(dve_did, 8)
            act.activation(score[:], x[:], ACT.Exp).then_inc(scored, 1)

        @block.tensor
        def _(pe):
            with pe.Fori(0, N) as i:
                pe.wait_ge(summed, i + 1)
                pe.matmul(sum_ps[:, 0:G], keep["ones"][:], part_sum[:], start=True, stop=True).then_inc(added, 1)
            pe.wait_ge(scored, 1)
            pe.transpose(turn_ps[0:B * NT, 0:P], score[:, 0:B].rearrange("p b t -> p (b t)"), keep["ident"][:]
                         ).then_inc(pe_did, 1)

        @block.gpsimd
        def _(pool):
            pool.wait_ge(dve_did, 6)
            nc.gpsimd.partition_all_reduce(s_max[:], part_max[:], P, bass.bass_isa.ReduceOp.max).then_inc(pool_did, 1)
            pool.wait_ge(ranked, 1)
            for b in range(B):
                pool.wait_ge(rows_in[b], 16)
                for i in range(NT):
                    nc.gpsimd.indirect_dma_start(
                        t["q_rows"], bass.IndirectOffsetOnAxis(keep["place"][:, b, i:i + 1], 0),
                        rows[:, b % 2, i], None, bounds_check=B * NQ - 1, oob_is_err=False).then_inc(scattered[b], 16)
            for b in range(B):
                pool.wait_ge(scattered[b], 16 * NT)

        @block.sync
        def _(sp):
            for b in range(2):
                sp.dma_start(rows[:, b], t["yn"][b].rearrange("(t p) d -> p t d", p=P)).then_inc(rows_in[b], 16)
            sp.wait_ge(dve_did, 12)
            sp.dma_start(t["scores"], score_rows[:]).then_inc(score_out, 16)
            sp.wait_ge(score_out, 16)
            sp.dma_start(all_scores[:], t["scores"].unsqueeze(0).to_broadcast([P, B * NT, P])).then_inc(scores_in, 16)
            for b in range(2, B):
                sp.wait_ge(scattered[b - 2], 16 * NT)
                sp.dma_start(rows[:, b % 2], t["yn"][b].rearrange("(t p) d -> p t d", p=P)).then_inc(rows_in[b], 16)


def heavy_attention(nc, t, keep):
    with ExitStack() as ctx:
        m = Memory(nc, ctx, "h")
        QT = NQ // P
        y_t = m.sb("y_t", [P, KT, S])
        q_rows = m.sb("q_rows", [P, QT, D])
        xq_t = m.sb("xq_t", [P, KT, NQ])
        w_qk = m.sb("w_qk", [P, 2, KT, P])
        w_v = m.sb("w_v", [P, KT, P])
        w_o = m.sb("w_o", [P, KT, D])
        part = m.sb("part", [P, 2, NQ + S], F16)
        q_stack = m.sb("q_stack", [P, 2, 2, NQ], F16)
        k_stack = m.sb("k_stack", [P, 2, 2, 2, S], F16)
        v_g = m.sb("v_g", [P, NT, P])
        factor_b = m.sb("factor_b", [P, NT])
        prob = m.sb("prob", [P, 3, S])
        prob_t = m.sb("prob_t", [P, 2, 2, NT, NQ])
        attn_t = m.sb("attn_t", [P, HP, NQ])
        neg_max = m.sb("neg_max", [P, 2, QT * 2])
        row_sum = m.sb("row_sum", [P, 2, QT * 2])
        inv = m.sb("inv", [P, QT * 2])
        inv_wide = m.sb("inv_wide", [P, QT * 2, FD])
        inv_t = m.sb("inv_t", [P, NQ])
        out_rows = m.sb("out_rows", [P, QT, D])
        score_ps = m.ps("score_ps", [P, 2, S])
        turn_ps = m.ps("turn_ps", [P, 2, 4, P])
        attn_ps = m.ps("attn_ps", [P, NQ])
        spare_ps = m.ps("spare_ps", [P, 512])
        y_in, rows_in, w_qk_in, w_v_in, wo_in, stored = (m.sem(n) for n in
                                                         ("y_in", "rows_in", "w_qk_in", "w_v_in", "wo_in", "stored"))
        stack_in = m.sem("stack_in")
        rows_turned, rows_turned_out, factor_set = m.sem("rows_turned"), m.sem("rows_turned_out"), m.sem("factor_set")
        made, v_made, high_done, low_done, v_out = (m.sem(n) for n in ("made", "v_made", "high_done", "low_done", "v_out"))
        scored, topped, exped = m.sem("scored"), m.sem("topped"), m.sem("exped")
        turn_a, turn_b, out_a, out_b = m.sem("turn_a"), m.sem("turn_b"), m.sem("out_a"), m.sem("out_b")
        inverted, widened, inv_turned, inv_out = (m.sem(n) for n in ("inverted", "widened", "inv_turned", "inv_out"))
        attended, normed, projected, proj_out = (m.sem(n) for n in ("attended", "normed", "projected", "proj_out"))
        passed = m.sem("passed")
        block = ctx.enter_context(nc.Block())
        STEPS = QT * 2
        ALL = HP * STEPS
        STACK = 2 * (2 + 2) * 16
        PARTS = 3 * HP
        FILLS = {0: ("qk", 0), 1: ("qk", 1), 2: ("qk", 2), 3: ("inverse", 0), 5: ("v", 0), 6: ("v", 1)}
        ATTEND_AT = {0: (0, 2), 1: (2, 4), 2: (4, 6), 3: (6, NT)}

        def fill_of(n):
            g, s = divmod(n, STEPS)
            if n < 0 or s not in FILLS:
                return None
            kind, c = FILLS[s]
            g += {"qk": 1, "inverse": -1, "v": 0}[kind]
            return (kind, g, c) if 0 <= g < HP else None

        @block.sync
        def _(sp):
            def load_qk(g):
                sp.dma_start(w_qk[:], t["heavy_wt"][g, 0:2].rearrange("i p k o -> p i k o")).then_inc(w_qk_in, 16)

            def load_v(g):
                sp.dma_start(w_v[:], t["heavy_wt"][g, 2]).then_inc(w_v_in, 16)

            def stack_up(b, g):
                after(sp, low_done, b * PARTS + 3 * g + 1)
                for h in range(2):
                    rows = slice(h * FD, (h + 1) * FD)
                    for half in range(2):
                        sp.dma_start(q_stack[half * FD:(half + 1) * FD, g % 2, h], part[rows, half, 0:NQ]
                                     ).then_inc(stack_in, 16)
                after(sp, low_done, b * PARTS + 3 * g + 3)
                for h in range(2):
                    rows = slice(h * FD, (h + 1) * FD)
                    for r in range(2):
                        sp.dma_start(k_stack[r * FD:(r + 1) * FD, g % 2, :, h], part[rows, :, NQ:]
                                     ).then_inc(stack_in, 16)

            sp.dma_start(w_o[:], t["L0_ffn_wo_heavy"].rearrange("(k p) o -> p k o", p=P)).then_inc(wo_in, 16)
            with sp.Fori(0, B) as b:
                sp.dma_start(q_rows[:], t["q_rows"].rearrange("(b t p) d -> b p t d", b=B, p=P)[bass.ds(b, 1)]
                             .rearrange("a p t d -> p (a t) d")).then_inc(rows_in, 16)
                load_qk(0)
                sp.dma_start(y_t[:], t["yn_t"][bass.ds(b, 1)].rearrange("a p k s -> p (a k) s")).then_inc(y_in, 16)
                load_v(0)
                stack_up(b, 0)
                for g in range(HP - 1):
                    sp.wait_ge(made, b * PARTS + 3 * g + 3)
                    load_qk(g + 1)
                    stack_up(b, g + 1)
                    sp.wait_ge(v_made, (b * HP + g + 1) * 2)
                    load_v(g + 1)
                after(sp, proj_out, (b + 1) * QT)
                sp.dma_start(t["h_rows"].rearrange("(b t p) d -> b p t d", b=B, p=P)[bass.ds(b, 1)]
                             .rearrange("a p t d -> p (a t) d"), out_rows[:]).then_inc(stored, 16)
                sp.wait_ge(stored, (b + 1) * 16)
                alone(sp, passed)

        @block.gpsimd
        def _(pool):
            prime(pool, widened)
            with pool.Fori(0, B * HP) as it:
                pool.wait_ge(inverted, it + 1)
                after(pool, inv_turned, it)
                alone(pool, passed)
                nc.gpsimd.tensor_scalar(inv_wide[:], inv[:].unsqueeze(2).to_broadcast([P, QT * 2, FD]),
                                        1.0, 1.0, ALU.mult, ALU.mult).then_inc(widened, 1)

        @block.scalar
        def _(act):
            prime(act, exped, out_a, inv_out, proj_out)
            with act.Fori(0, B) as b:
                def high(g, n, src):
                    act.wait_ge(made, b * PARTS + 3 * g + n + 1)
                    if n == 0 and g:
                        act.wait_ge(stack_in, (b * HP + g) * STACK)
                    elif n == 0:
                        after(act, scored, b * ALL)
                    act.activation(part[:, 0, n * 512:(n + 1) * 512], src, ACT.Copy).then_inc(high_done, 1)

                def expo(n):
                    g, s = divmod(n, STEPS)
                    act.wait_ge(topped, b * ALL + n + 1)
                    if n >= 3:
                        act.wait_ge(turn_b, b * ALL + n - 2)
                    act.activation(prob[:, n % 3], score_ps[:, n % 2], ACT.Exp, scale=-1.0, bias=neg_max[:, g % 2, s:s + 1],
                                   accum_out=row_sum[:, g % 2, s:s + 1]).then_inc(exped, 1)

                def inverse_out(g):
                    after(act, inv_turned, b * HP + g + 1)
                    after(act, normed, b * HP + g)
                    act.activation(inv_t[:], spare_ps[:], ACT.Copy).then_inc(inv_out, 1)

                for i in range(QT):
                    act.wait_ge(rows_turned, b * QT + i + 1)
                    act.activation(xq_t[:, :, i * P:(i + 1) * P], turn_ps[:, i % 2], ACT.Copy).then_inc(rows_turned_out, 1)
                for n in range(3):
                    high(0, n, score_ps[:, n // 2, n % 2 * 512:n % 2 * 512 + 512])
                expo(0)
                for n in range(ALL):
                    g, s = divmod(n, STEPS)
                    if n + 1 < ALL:
                        expo(n + 1)
                    if s == 0:
                        after(act, attended, b * HP + max(g - 1, 0))
                    act.wait_ge(turn_a, b * ALL + n + 1)
                    act.activation(prob_t[:, g % 2, n % 2, 0:4, s // 2 * P:s // 2 * P + P], turn_ps[:, 0],
                                   ACT.Copy).then_inc(out_a, 1)
                    f = fill_of(n - 1)
                    if f and f[0] == "qk":
                        high(f[1], f[2], spare_ps[:])
                    elif f and f[0] == "inverse":
                        inverse_out(f[1])
                inverse_out(HP - 1)
                for i in range(QT):
                    act.wait_ge(projected, b * QT + i + 1)
                    act.activation(out_rows[:, i], score_ps[:, i % 2, 0:D], ACT.Copy).then_inc(proj_out, 1)

        @block.vector
        def _(dve):
            prime(dve, v_out, out_b, normed, low_done)
            with dve.Fori(0, B) as b:
                def low(g, n, src):
                    dve.wait_ge(high_done, b * PARTS + 3 * g + n + 1)
                    cols = slice(n * 512, (n + 1) * 512)
                    dve.tensor_tensor(part[:, 1, cols], src, part[:, 0, cols], ALU.subtract).then_inc(low_done, 1)

                def least(n):
                    g, s = divmod(n, STEPS)
                    after(dve, scored, b * ALL + n + 1)
                    dve.tensor_reduce(neg_max[:, g % 2, s:s + 1], score_ps[:, n % 2], axis=AX.X, op=ALU.min
                                      ).then_inc(topped, 1)

                def invert(g):
                    after(dve, exped, b * ALL + (g + 1) * STEPS)
                    after(dve, widened, b * HP + g)
                    dve.reciprocal(inv[:], row_sum[:, g % 2]).then_inc(inverted, 1)

                def norm(g):
                    after(dve, attended, b * HP + g + 1)
                    after(dve, inv_out, b * HP + g + 1)
                    dve.tensor_tensor(attn_t[:, g], attn_ps[:], inv_t[:], ALU.mult).then_inc(normed, 1)

                after(dve, v_out, b * HP * 2)
                dve.tensor_copy(factor_b[:].unsqueeze(1), keep["factor"][:, 1, bass.ds(b, 1)]).then_inc(factor_set, 1)
                for n in range(3):
                    low(0, n, score_ps[:, n // 2, n % 2 * 512:n % 2 * 512 + 512])
                dve.wait_ge(factor_set, b + 1)
                least(0)
                least(1)
                for n in range(ALL):
                    g, s = divmod(n, STEPS)
                    if n + 2 < ALL:
                        least(n + 2)
                    if s == 0:
                        after(dve, attended, b * HP + max(g - 1, 0))
                    dve.wait_ge(turn_b, b * ALL + n + 1)
                    dve.tensor_copy(prob_t[:, g % 2, n % 2, 4:8, s // 2 * P:s // 2 * P + P], turn_ps[:, 1]
                                    ).then_inc(out_b, 1)
                    if s == 0 and g:
                        invert(g - 1)
                    f = fill_of(n - 1)
                    if f and f[0] == "qk":
                        low(f[1], f[2], spare_ps[:])
                    elif f and f[0] == "inverse":
                        norm(f[1])
                    elif f:
                        c = f[2]
                        dve.wait_ge(v_made, b * HP * 2 + 2 * g + c + 1)
                        after(dve, attended, b * HP + g)
                        dve.tensor_tensor(v_g[:, 4 * c:4 * c + 4], spare_ps[:].rearrange("p (i o) -> p i o", o=P),
                                          factor_b[:, 4 * c:4 * c + 4].unsqueeze(2).to_broadcast([P, 4, P]),
                                          ALU.mult).then_inc(v_out, 1)
                invert(HP - 1)
                norm(HP - 1)

        @block.tensor
        def _(pe):
            prime(pe, scored, inv_turned, attended)
            with pe.Fori(0, B) as b:
                def project(g, n, out):
                    w, src = (0, xq_t[:]) if n == 0 else (1, y_t[:, :, (n - 1) * 512:n * 512])
                    for k in range(KT):
                        ins = pe.matmul(out, w_qk[:, w, k], src[:, k], start=k == 0, stop=k == KT - 1)
                    ins.then_inc(made, 1)

                def emptied(f):
                    kind, g, c = f
                    if kind == "qk":
                        after(pe, low_done, b * PARTS + 3 * g + c + 1)
                    elif kind == "v":
                        after(pe, v_out, b * HP * 2 + 2 * g + c + 1)
                    else:
                        after(pe, inv_out, b * HP + g + 1)

                def fill(f):
                    kind, g, c = f
                    if kind == "qk":
                        pe.wait_ge(w_qk_in, (b * HP + g + 1) * 16)
                        project(g, c, spare_ps[:])
                    elif kind == "v":
                        pe.wait_ge(w_v_in, (b * HP + g + 1) * 16)
                        for i in range(4):
                            for k in range(KT):
                                ins = pe.matmul(spare_ps[:, i * P:(i + 1) * P],
                                                y_t[:, k, (4 * c + i) * P:(4 * c + i + 1) * P], w_v[:, k],
                                                start=k == 0, stop=k == KT - 1)
                        ins.then_inc(v_made, 1)
                    else:
                        after(pe, widened, b * HP + g + 1)
                        for q in range(QT):
                            ins = pe.transpose(spare_ps[:, q * P:(q + 1) * P],
                                               inv_wide[:, 2 * q:2 * q + 2].rearrange("p h d -> p (h d)"), keep["ident"][:])
                        ins.then_inc(inv_turned, 1)

                def score(n):
                    g, s = divmod(n, STEPS)
                    qt, h = divmod(s, 2)
                    if n >= 2:
                        after(pe, exped, b * ALL + n - 1)
                    if s == 0:
                        pe.wait_ge(stack_in, (b * HP + g + 1) * STACK)
                    for c in range(2):
                        for half in range(2):
                            ins = pe.matmul(score_ps[:, n % 2, c * 512:(c + 1) * 512],
                                            q_stack[:, g % 2, h, qt * P:(qt + 1) * P],
                                            k_stack[:, g % 2, half, h, c * 512:(c + 1) * 512],
                                            start=half == 0, stop=half == 1)
                    ins.then_inc(scored, 1)

                def attend(g, first, last):
                    if first == 0:
                        after(pe, out_a, b * ALL + (g + 1) * STEPS)
                        after(pe, out_b, b * ALL + (g + 1) * STEPS)
                        after(pe, normed, b * HP + g)
                        after(pe, v_out, b * HP * 2 + 2 * g + 2)
                    for k in range(first, last):
                        for h in range(2):
                            ins = pe.matmul(attn_ps[h * FD:(h + 1) * FD], v_g[:, k, h * FD:(h + 1) * FD],
                                            prob_t[:, g % 2, h, k], start=k == 0, stop=k == NT - 1)
                    if last == NT:
                        ins.then_inc(attended, 1)

                pe.wait_ge(rows_in, (b + 1) * 16)
                after(pe, out_a, b * ALL)
                after(pe, out_b, b * ALL)
                for i in range(QT):
                    if i >= 2:
                        pe.wait_ge(rows_turned_out, b * QT + i - 1)
                    for k in range(KT):
                        ins = pe.transpose(turn_ps[:, i % 2, k], q_rows[:, i, k * P:(k + 1) * P], keep["ident"][:])
                    ins.then_inc(rows_turned, 1)
                pe.wait_ge(y_in, (b + 1) * 16)
                pe.wait_ge(rows_turned_out, (b + 1) * QT)
                after(pe, proj_out, b * QT)
                pe.wait_ge(w_qk_in, (b * HP + 1) * 16)
                for n in range(3):
                    project(0, n, score_ps[:, n // 2, n % 2 * 512:n % 2 * 512 + 512])
                after(pe, low_done, b * PARTS + 3)
                after(pe, inv_out, b * HP)
                score(0)
                score(1)
                last = None
                for n in range(ALL):
                    g, s = divmod(n, STEPS)
                    if n + 2 < ALL:
                        score(n + 2)
                    after(pe, exped, b * ALL + n + 1)
                    for h, (sem, out) in enumerate(((turn_a, out_a), (turn_b, out_b))):
                        after(pe, out, b * ALL + n)
                        for k in range(4):
                            ins = pe.transpose(turn_ps[:, h, k], prob[:, n % 3, (4 * h + k) * P:(4 * h + k + 1) * P],
                                               keep["ident"][:])
                        ins.then_inc(sem, 1)
                    if g and s in ATTEND_AT:
                        attend(g - 1, *ATTEND_AT[s])
                    f = fill_of(n)
                    if f:
                        if last:
                            emptied(last)
                        fill(f)
                        last = f
                emptied(last)
                attend(HP - 1, 0, NT)
                fill(("inverse", HP - 1, 0))
                pe.wait_ge(wo_in, 16)
                after(pe, normed, (b + 1) * HP)
                after(pe, exped, (b + 1) * ALL)
                for i in range(QT):
                    if i >= 2:
                        after(pe, proj_out, b * QT + i - 1)
                    for k in range(HP):
                        ins = pe.matmul(score_ps[:, i % 2, 0:D], attn_t[:, k, i * P:(i + 1) * P], w_o[:, k],
                                        start=k == 0, stop=k == HP - 1)
                    ins.then_inc(projected, 1)


def combine(nc, t, keep):
    with ExitStack() as ctx:
        m = Memory(nc, ctx, "c")
        mid = m.sb("mid", [P, B, NT, D])
        routed = m.sb("routed", [P, B, NT, D])
        mid_in = [m.sem(f"mid_in{b}") for b in range(B)]
        cleared = m.sem("cleared")
        gathered = [m.sem(f"gathered{b}") for b in range(B)]
        added, stored = m.sem("added"), m.sem("stored")
        block = ctx.enter_context(nc.Block())

        @block.sync
        def _(sp):
            for b in range(B):
                sp.dma_start(mid[:, b], t["mid"][b].rearrange("(t p) d -> p t d", p=P)).then_inc(mid_in[b], 16)
            for b in range(B):
                sp.wait_ge(added, (b + 1) * NT)
                sp.dma_start(t["out"][b].rearrange("(t p) d -> p t d", p=P), mid[:, b]).then_inc(stored, 16)
            sp.wait_ge(stored, B * 16)

        @block.gpsimd
        def _(pool):
            for b in range(B):
                pool.wait_ge(cleared, b + 1)
                for i in range(NT):
                    nc.gpsimd.indirect_dma_start(
                        routed[:, b, i], None, t["h_rows"], bass.IndirectOffsetOnAxis(keep["place"][:, b, i:i + 1], 0),
                        bounds_check=B * NQ - 1, oob_is_err=False).then_inc(gathered[b], 16)

        @block.vector
        def _(dve):
            for b in range(B):
                dve.memset(routed[:, b], 0.0).then_inc(cleared, 1)
            for b in range(B):
                dve.wait_ge(mid_in[b], 16)
                dve.wait_ge(gathered[b], 16 * NT)
                for i in range(NT):
                    dve.scalar_tensor_tensor(mid[:, b, i], routed[:, b, i], keep["q_gate"][:, b, i:i + 1], mid[:, b, i],
                                             ALU.mult, ALU.add).then_inc(added, 1)


def build(nc, t, phases=9):
    def scratch(name, shape, dt=F32):
        t[name] = nc.dram_tensor(name, shape, dt, kind="Internal").ap()

    scratch("xattn_wt", [NG, 3, P, KT, P])
    scratch("xattn_wo_t", [P, KT, D])
    scratch("heavy_wt", [HP, 3, P, KT, P])
    scratch("light_wt", [3, P, KT, D])
    for name in ("x1", "yn"):
        scratch(name, [B, S, D])
    scratch("yn_t", [B, P, KT, S])
    scratch("mid", [B, S, D])
    scratch("scores", [B * NT, P])
    scratch("q_rows", [B * NQ, D])
    scratch("h_rows", [B * NQ, D])
    with ExitStack() as ctx:
        m = Memory(nc, ctx, "keep")
        keep = {
            "ident": m.sb("ident", [P, P]), "ones": m.sb("ones", [P, P]),
            "before": m.sb("before", [P, P]), "after": m.sb("after", [P, P]),
            "minus_half": m.sb("minus_half", [P, NT]), "slopes": m.sb("slopes", [P, XH]),
            "gates": m.sb("gates", [P, 2]), "route_s": m.sb("route_s", [P, 2, B, NT]),
            "factor": m.sb("factor", [P, 2, B, NT]), "q_gate": m.sb("q_gate", [P, B, NT]),
            "place": m.sb("place", [P, B, NT], I32),
        }
        prepare_weights(nc, t, keep)
        if phases >= 1:
            cross_attention(nc, t, keep, B if phases > 1 else 1)
        if phases >= 2:
            light_attention(nc, t, keep)
        if phases >= 3:
            route(nc, t, keep)
        if phases >= 4:
            heavy_attention(nc, t, keep)
        if phases >= 5:
            combine(nc, t, keep)


INPUTS = ["x", "ctx_1024", "itok_BxS_8_8191", "itok_BxS2_1_8191", "mask_BxSxS2_if1", "g_xattn", "g_ffn",
          "L0_xattn_W_q", "L0_xattn_W_k", "L0_xattn_W_v", "L0_xattn_W_o", "L0_ffn_gamma_light", "L0_ffn_wq_light",
          "L0_ffn_wkv_light", "L0_ffn_wo_light", "L0_ffn_q_routing_token", "L0_ffn_kv_routing_token",
          "L0_ffn_gamma_heavy", "L0_ffn_wq_heavy", "L0_ffn_wkv_heavy", "L0_ffn_wo_heavy"]


def kernel(**inputs):
    import concourse.bacc as bacc
    from concourse.bass_utils import run_bass_kernel_spmd

    nc = bacc.Bacc("TRN2", target_bir_lowering=False, num_devices=1)
    arrays, t = {}, {}
    for name in INPUTS:
        a = np.ascontiguousarray(inputs[name])
        arrays[f"in_{name}"] = a
        t[name] = nc.dram_tensor(f"in_{name}", a.shape, mybir.dt.from_np(a.dtype), kind="ExternalInput").ap()
    t["out"] = nc.dram_tensor("out", (B, S, D), F32, kind="ExternalOutput").ap()
    build(nc, t)
    r = run_bass_kernel_spmd(nc, [arrays], core_ids=[0])
    return r.results[0]["out"]
```

```python
from contextlib import ExitStack

import numpy as np

import concourse.bass as bass
from concourse import mybir

F32 = mybir.dt.float32
F16 = mybir.dt.float16
I32 = mybir.dt.int32
ALU = mybir.AluOpType
ACT = mybir.ActivationFunctionType
AX = mybir.AxisListType

P = 128
B, S, D = 4, 1024, 512
NT = S // P
KT = D // P
XH, XD = 16, D // 16
GH = P // XD
NG = XH // GH
FH, FD = 8, D // 8
HP = FH // 2
NQ = 512
LN_EPS = 1e-5
MASKED = 1e30
ITERS = 50
LOG_KQ = float(np.log(np.float32(min(NQ * 9.0 / 8.0, S))))
LOG_KKV = float(np.log(np.float32(min(S * 9.0 / 8.0, S))))
OUT_OF_RANGE = 1 << 20


XW_SCALE = 64.0
X_SCALE = 32.0
X_UNSCALE = 1.0 / (XW_SCALE * X_SCALE)
W_SCALE = 256.0
Y_SCALE = 256.0
UNSCALE = 1.0 / (W_SCALE * Y_SCALE)
HALVES = ((0, 0), (0, 1), (1, 0))


def slope(h):
    return float(np.float32(2.0 ** (-8.0 / XH)) ** (h + 1))


class Memory:

    def __init__(self, nc, ctx, phase):
        self.nc, self.ctx, self.phase = nc, ctx, phase

    def sb(self, name, shape, dt=F32):
        return self.ctx.enter_context(self.nc.sbuf_tensor(f"{self.phase}_{name}", shape, dt))

    def ps(self, name, shape, dt=F32):
        return self.ctx.enter_context(self.nc.psum_tensor(f"{self.phase}_{name}", shape, dt))

    def sem(self, name):
        return self.ctx.enter_context(self.nc.semaphore(f"{self.phase}_{name}"))


def prime(eng, *sems):
    for sem in sems:
        eng.sem_inc(sem, 1)


def after(eng, sem, count):
    eng.wait_ge(sem, count + 1)


def alone(eng, passed):
    eng.sem_inc(passed, 1)


class Chain:

    def __init__(self, eng, sem, base=0):
        self.eng, self.sem, self.base, self.n = eng, sem, base, 0

    def mark(self, ins):
        ins.then_inc(self.sem, 1)
        self.n += 1
        return self.base + self.n

    def wait(self):
        self.eng.wait_ge(self.sem, self.base + self.n)


def prepare_weights(nc, t, keep):
    with ExitStack() as ctx:
        m = Memory(nc, ctx, "w")
        natural = m.sb("natural", [P, 6, KT, D])
        turned = m.sb("turned", [P, 6, KT, D])
        q_scale = m.sb("q_scale", [P, KT])
        wqh = m.sb("wqh", [P, KT, D])
        gam = keep["gammas"]
        parts = turned[:].rearrange("p w k d -> p (w k d)").bitcast(F16).rearrange(
            "p (w k i d) -> p w k i d", w=6, k=KT, i=2)
        gate_in = m.sb("gate_in", [P, 2])
        gam_in = m.sb("gam_in", [P, 2, KT])
        tp = m.ps("tp", [P, 2, KT, P])
        loaded = [m.sem(f"loaded{i}") for i in range(7)]
        small_loaded = m.sem("small_loaded")
        ident_made = m.sem("ident_made")
        consts_made = m.sem("consts_made")
        scaled = m.sem("scaled")
        transposed = m.sem("transposed")
        copied, lowered = m.sem("copied"), m.sem("lowered")
        wqh_parts = m.sb("wqh_parts", [P, KT, 2, D], F16)
        stored = m.sem("stored")
        gated = m.sem("gated")
        block = ctx.enter_context(nc.Block())
        N_TURN = 6 * KT

        def lows(n):
            return n - min(max(n - 3 * KT, 0), KT)

        @block.sync
        def _(sp):
            for i, w in enumerate(("L0_xattn_W_q", "L0_xattn_W_k", "L0_xattn_W_v", "L0_xattn_W_o")):
                sp.dma_start(natural[:, i], t[w].rearrange("(o p) d -> p o d", p=P)).then_inc(loaded[i], 16)
            for i in range(2):
                sp.dma_start(natural[:, 4 + i],
                             t["L0_ffn_wkv_heavy"][i * D:(i + 1) * D, :].rearrange("(o p) d -> p o d", p=P)
                             ).then_inc(loaded[4 + i], 16)
            sp.dma_start(wqh[:], t["L0_ffn_wq_heavy"].rearrange("(k p) o -> p k o", p=P)).then_inc(loaded[6], 16)
            for i in range(3):
                sp.wait_ge(lowered, (i + 1) * KT)
                for g in range(NG):
                    sp.dma_start(t["xattn_wt"][g, i], parts[:, i, :, :, g * P:(g + 1) * P]).then_inc(stored, 16)
            sp.wait_ge(copied, 4 * KT)
            sp.dma_start(t["xattn_wo_t"], turned[:, 3]).then_inc(stored, 16)
            for hp in range(HP):
                half, at = hp // 2, (hp % 2) * 2 * P
                if hp % 2 == 0:
                    sp.wait_ge(lowered, (4 + half) * KT)
                cols = parts[:, 4 + half, :, :, at:at + 2 * P].rearrange("p k i (h s d) -> p (k i) h s d", h=2, s=2)
                for s in range(2):
                    for h in range(2):
                        sp.dma_start(t["heavy_wt"][hp, 1 + s, :, :, :, h * FD:(h + 1) * FD].rearrange("p k i d -> p (k i) d"),
                                     cols[:, :, h, s]).then_inc(stored, 16)
            sp.wait_ge(lowered, 5 * KT + 1)
            for hp in range(HP):
                sp.dma_start(t["heavy_wt"][hp, 0], wqh_parts[:, :, :, hp * P:(hp + 1) * P]).then_inc(stored, 16)
            sp.wait_ge(stored, 16 * (3 * NG + 1 + HP * 4 + HP))

        @block.gpsimd
        def _(pool):
            nc.gpsimd.memset(keep["ident"][:], 0.0).then_inc(ident_made, 1)
            pool.wait_ge(ident_made, 1)
            nc.gpsimd.affine_select(out=keep["ident"][:], in_=keep["ident"][:], compare_op=ALU.not_equal, fill=1.0,
                                    base=0, pattern=[[-1, P]], channel_multiplier=1).then_inc(ident_made, 1)
            nc.gpsimd.memset(keep["ones"][:], 1.0).then_inc(consts_made, 1)
            nc.gpsimd.memset(keep["minus_half"][:], -0.5).then_inc(consts_made, 1)
            for h in range(XH):
                nc.gpsimd.memset(keep["slopes"][:, h:h + 1], slope(h)).then_inc(consts_made, 1)
            nc.gpsimd.memset(keep["before"][:], 1.0).then_inc(consts_made, 1)
            nc.gpsimd.memset(keep["after"][:], 1.0).then_inc(consts_made, 1)
            pool.wait_ge(consts_made, XH + 4)
            nc.gpsimd.affine_select(out=keep["before"][:], in_=keep["before"][:], compare_op=ALU.is_gt, fill=0.0,
                                    base=0, pattern=[[-1, P]], channel_multiplier=1).then_inc(consts_made, 1)
            nc.gpsimd.affine_select(out=keep["after"][:], in_=keep["after"][:], compare_op=ALU.is_gt, fill=0.0,
                                    base=0, pattern=[[1, P]], channel_multiplier=-1).then_inc(consts_made, 1)

        @block.scalar
        def _(act):
            for i, n in enumerate(("g_xattn", "g_ffn")):
                act.dma_start(gate_in[:, i:i + 1], t[n].rearrange("(a n) -> a n", a=1).to_broadcast([P, 1])
                              ).then_inc(small_loaded, 16)
            for i, n in enumerate(("L0_ffn_gamma_light", "L0_ffn_gamma_heavy")):
                act.dma_start(gam_in[:, i], t[n].rearrange("(k p) -> p k", p=P),
                              allow_slow_non_contiguous=True).then_inc(small_loaded, 16)
            act.wait_ge(small_loaded, 64)
            act.activation(keep["gates"][:], gate_in[:], ACT.Tanh).then_inc(gated, 1)
            act.activation(gam[:], gam_in[:], ACT.Copy, scale=W_SCALE).then_inc(gated, 1)
            act.wait_ge(gated, 2)
            for n in range(N_TURN):
                which, kt = divmod(n, KT)
                act.wait_ge(transposed, n + 1)
                dst = turned[:, which, kt]
                if which >= 4:
                    act.activation(parts[:, which, kt, 0], tp[:, n % 2].rearrange("p o c -> p (o c)"), ACT.Copy,
                                   scale=gam[:, 1, kt:kt + 1]).then_inc(copied, 1)
                elif which < 3:
                    act.activation(parts[:, which, kt, 0], tp[:, n % 2].rearrange("p o c -> p (o c)"), ACT.Copy,
                                   scale=XW_SCALE).then_inc(copied, 1)
                else:
                    act.activation(dst, tp[:, n % 2].rearrange("p o c -> p (o c)"), ACT.Copy).then_inc(copied, 1)
            act.wait_ge(scaled, 1 + 2 * KT)
            act.activation(wqh_parts[:, :, 0], wqh[:], ACT.Copy).then_inc(copied, 1)

        @block.vector
        def _(dve):
            for o in range(KT):
                for j in range(GH):
                    ins = dve.memset(q_scale[j * XD:(j + 1) * XD, o:o + 1],
                                     -(1.0 / np.sqrt(XD)) / slope(o * GH + j))
            ins.then_inc(scaled, 1)
            dve.wait_ge(scaled, 1)
            dve.wait_ge(loaded[0], 16)
            for o in range(KT):
                dve.tensor_scalar(natural[:, 0, o], natural[:, 0, o], q_scale[:, o:o + 1], None,
                                  ALU.mult).then_inc(scaled, 1)
            dve.wait_ge(gated, 2)
            for n in range(N_TURN):
                which, kt = divmod(n, KT)
                if which == 3:
                    continue
                dve.wait_ge(copied, n + 1)
                dve.scalar_tensor_tensor(parts[:, which, kt, 1], tp[:, n % 2].rearrange("p o c -> p (o c)"),
                                         XW_SCALE if which < 3 else gam[:, 1, kt:kt + 1], parts[:, which, kt, 0],
                                         ALU.mult, ALU.subtract).then_inc(lowered, 1)
            dve.wait_ge(loaded[6], 16)
            for k in range(KT):
                dve.tensor_scalar(wqh[:, k], wqh[:, k], gam[:, 1, k:k + 1], -float(FD) ** -0.5,
                                  ALU.mult, ALU.mult).then_inc(scaled, 1)
            dve.wait_ge(copied, N_TURN + 1)
            dve.tensor_tensor(wqh_parts[:, :, 1], wqh[:], wqh_parts[:, :, 0], ALU.subtract).then_inc(lowered, 1)

        @block.tensor
        def _(pe):
            pe.wait_ge(ident_made, 2)
            pe.wait_ge(scaled, 1 + KT)
            for n in range(N_TURN):
                which, kt = divmod(n, KT)
                if which and kt == 0:
                    pe.wait_ge(loaded[which], 16)
                if n >= 2:
                    pe.wait_ge(copied, n - 1)
                if n >= 2:
                    pe.wait_ge(lowered, lows(n - 1))
                for o in range(KT):
                    ins = pe.transpose(tp[:, n % 2, o], natural[:, which, o, kt * P:(kt + 1) * P], keep["ident"][:])
                ins.then_inc(transposed, 1)




def cross_attention(nc, t, keep, batches=B):
    with ExitStack() as ctx:
        m = Memory(nc, ctx, "x")
        ctx_t = m.sb("ctx_t", [P, KT, NT, 2, P], F16)
        xn_t = m.sb("xn_t", [P, KT, NT, 2, P], F16)
        dist = m.sb("dist", [P, NT, S])
        prob = m.sb("prob", [P, 3, S])
        prob_t = m.sb("prob_t", [P, 2, GH, NT, 2 * P])
        attn_t = m.sb("attn_t", [P, NG, S])
        y_parts = attn_t[:].rearrange("p k s -> p (k s)").bitcast(F16).rearrange("p (k t i c) -> p k t i c", k=KT, t=NT, i=2)
        w_qk = m.sb("w_qk", [P, 2, KT, 2, P], F16)
        w_v = m.sb("w_v", [P, KT, 2, P], F16)
        part = m.sb("part", [P, 2, S], F16)
        q_stack = m.sb("q_stack", [P, 2, GH, S], F16)
        k_stack = m.sb("k_stack", [P, 2, GH, S], F16)
        v_g = m.sb("v_g", [P, NT, P])
        neg_max = m.sb("neg_max", [P, NT * GH])
        row_sum = m.sb("row_sum", [P, NT * GH])
        den = m.sb("den", [P, 2, GH])
        inv = m.sb("inv", [P, 2, GH])
        den_wide = m.sb("den_wide", [P, 2, GH, XD])
        den_t = m.sb("den_t", [P, 2 * P])
        stats = m.sb("stats", [P, NT, 6])
        mean_var = m.sb("mean_var", [P, NT, 2])
        small = m.sb("small", [P, 6, NT])
        route = m.sb("route", [P, 2, NT])
        pos_i = m.sb("pos_i", [P, NT], I32)
        pos_f = m.sb("pos_f", [P, NT])
        flat = prob_t[:].rearrange("p a b c d -> p (a b c d)")
        x_rows, x1_rows, xs, cs = (flat[:, i * NT * D:(i + 1) * NT * D].rearrange("p (t d) -> p t d", d=D)
                                   for i in range(4))
        mask = dist[:].bitcast(I32)
        kpos_i = prob[:, 0].bitcast(I32)
        kpos_neg = prob[:, 1]
        assert NG % 2 == 0
        wo_t = q_stack[:, 0].rearrange("p j s -> p (j s)").bitcast(F32).rearrange("p (k d) -> p k d", d=D)
        k_memory = k_stack[:, 0].rearrange("p j s -> p (j s)").bitcast(F32)
        tokens = k_memory[:, 0:2 * D].rearrange("p (w d) -> p w d", d=D)
        junk, squares = (k_memory[:, i * D:(i + 1) * D] for i in (2, 3))

        score_ps = m.ps("score_ps", [P, 2, S])
        turn_ps = m.ps("turn_ps", [P, 2, KT, P])
        attn_ps = m.ps("attn_ps", [P, 512])
        spare_ps = m.ps("spare_ps", [P, 512])

        x_in, c_in, mask_in, pos_in = m.sem("x_in"), m.sem("c_in"), m.sem("mask_in"), m.sem("pos_in")
        x_again, k_in, out_stored = m.sem("x_again"), m.sem("k_in"), m.sem("out_stored")
        q_in = [m.sem(f"q_in{c}") for c in range(2)]
        away = {way: m.sem(f"away_{way}") for way in ("k", "q0", "q1")}
        w_qk_in, w_v_in, w_o_in = m.sem("w_qk_in"), m.sem("w_v_in"), m.sem("w_o_in")
        dve_did, pool_did = m.sem("dve_did"), m.sem("pool_did")
        turned, turned_out = m.sem("turned"), m.sem("turned_out")
        qk_made, v_made = m.sem("qk_made"), m.sem("v_made")
        high_done, low_done, v_out = m.sem("high_done"), m.sem("low_done"), m.sem("v_out")
        scored, biased, exped = m.sem("scored"), m.sem("biased"), m.sem("exped")
        turn_a, turn_b, out_a, out_b = m.sem("turn_a"), m.sem("turn_b"), m.sem("out_a"), m.sem("out_b")
        den_made, inverted, widened = m.sem("den_made"), m.sem("inverted"), m.sem("widened")
        den_turned, den_out = m.sem("den_turned"), m.sem("den_out")
        attended, normed = m.sem("attended"), m.sem("normed")
        projected, x1_made, end_did = m.sem("projected"), m.sem("x1_made"), m.sem("end_did")
        var_set, var_out, square_set, square_out = (m.sem(n) for n in ("var_set", "var_out", "square_set", "square_out"))
        rows_ready, settled, y_low = m.sem("rows_ready"), m.sem("settled"), m.sem("y_low")
        x_low, squared = m.sem("x_low"), m.sem("squared")
        passed = keep["passed"]
        block = ctx.enter_context(nc.Block())

        STEPS = NT * GH
        ALL = NG * STEPS
        PER_PAIR = 2 * GH
        GP = STEPS // PER_PAIR
        PAIRS = ALL // PER_PAIR
        QK_PARTS = NG * 4
        V_PARTS = NG * 2
        STACK = 4 * 16
        DVE_BATCH = 3 * NT + 1 + 2 + 2 * NT
        END_BATCH = 5 * NT + 1

        def normed_mark(i):
            k = i + 1
            return i + 2 * min(k, NT) + 2 * max(k - 2, 0) + 1
        TURNS = 3 * NT
        WINDOWS = [("v", 0), ("v", 1), ("k", 0), ("k", 1), None, ("q", 0), ("q", 1), None]
        WINDOW_AT = (3, 6)
        ATTEND_AT = {1: (0, 3), 2: (3, 6), 5: (6, NT)}

        def window_of(n, stage):
            for w, at in enumerate(WINDOW_AT):
                first = n - stage
                if first >= 0 and first % PER_PAIR == at:
                    g, pair = divmod(first // PER_PAIR, GP)
                    kind = WINDOWS[2 * pair + w]
                    if kind and (kind[0] == "v" or g + 1 < NG):
                        return (g + (kind[0] != "v"), *kind)
            return None

        def qk_part(g, kind, c):
            return 4 * g + 2 * (kind == "q") + c

        @block.sync
        def _(sp):
            def load_qk(g):
                sp.dma_start(w_qk[:].rearrange("p w k i o -> p w (k i o)"),
                             t["xattn_wt"][g, 0:2].rearrange("w p k i o -> p w (k i o)")).then_inc(w_qk_in, 16)

            def load_v(g):
                sp.dma_start(w_v[:], t["xattn_wt"][g, 2]).then_inc(w_v_in, 16)

            def stack_up(b, g, kind, c):
                after(sp, low_done, b * QK_PARTS + qk_part(g, kind, c) + 1)
                cols = slice(0, S) if kind == "k" else slice(c * 512, (c + 1) * 512)
                stack, way, stack_in = ((k_stack, "k", k_in) if kind == "k" else (q_stack, f"q{c}", q_in[c]))
                halves = t["halves_" + way]
                sp.dma_start(halves.rearrange("i p s -> p i s"), part[:, :, cols]).then_inc(away[way], 16)
                sp.wait_ge(away[way], (b * NG + g + 1) * 16)
                for r in range(4):
                    which = r // 2 if kind == "k" else r % 2
                    sp.dma_start(stack[r * XD:(r + 1) * XD, g % 2, :, cols],
                                 halves[which].rearrange("(j p) s -> p j s", j=GH)).then_inc(stack_in, 16)

            with sp.Fori(0, batches) as b:
                after(sp, attended, b * PAIRS)
                load_qk(0)
                load_v(0)
                sp.dma_start(cs, t["ctx_1024"][bass.ds(b, 1)].rearrange("a (t p) d -> p (a t) d", p=P)).then_inc(c_in, 16)
                sp.dma_start(xs, t["x"][bass.ds(b, 1)].rearrange("a (t p) d -> p (a t) d", p=P)).then_inc(x_in, 16)
                sp.dma_start(kpos_i, t["itok_BxS2_1_8191"][bass.ds(b, 1)].to_broadcast([P, S])).then_inc(pos_in, 16)
                sp.dma_start(pos_i[:], t["itok_BxS_8_8191"][bass.ds(b, 1)].rearrange("a (t p) -> p (a t)", p=P),
                             allow_slow_non_contiguous=True).then_inc(pos_in, 16)
                sp.dma_start(mask, t["mask_BxSxS2_if1"][bass.ds(b, 1)].rearrange("a (t p) s -> p (a t) s", p=P)
                             ).then_inc(mask_in, 16)
                stack_up(b, 0, "k", 1)
                stack_up(b, 0, "q", 0)
                stack_up(b, 0, "q", 1)
                for g in range(NG):
                    if g + 1 < NG:
                        sp.wait_ge(qk_made, b * QK_PARTS + 4 * g + 4)
                        load_qk(g + 1)
                        sp.wait_ge(v_made, b * V_PARTS + 2 * g + 2)
                        load_v(g + 1)
                        stack_up(b, g + 1, "k", 1)
                        stack_up(b, g + 1, "q", 0)
                        stack_up(b, g + 1, "q", 1)
                after(sp, scored, (b + 1) * ALL - STEPS)
                sp.dma_start(wo_t, t["xattn_wo_t"]).then_inc(w_o_in, 16)
                for i, n in enumerate(("L0_ffn_q_routing_token", "L0_ffn_kv_routing_token")):
                    sp.dma_start(tokens[:, i], t[n].rearrange("(a n) -> a n", a=1).to_broadcast([P, D])
                                 ).then_inc(w_o_in, 16)
                after(sp, attended, (b + 1) * PAIRS - 1)
                sp.dma_start(x_rows, t["x"][bass.ds(b, 1)].rearrange("a (t p) d -> p (a t) d", p=P)).then_inc(x_again, 16)

        @block.gpsimd
        def _(pool):
            prime(pool, widened)
            with pool.Fori(0, batches) as b:
                def power(slot, cols, out_sem):
                    nc.gpsimd.tensor_tensor(small[:, slot + 1, cols], small[:, slot, cols], keep["minus_half"][:, cols],
                                            ALU.pow).then_inc(out_sem, 1)
                pool.wait_ge(dve_did, b * DVE_BATCH + 2 * NT + 1)
                power(0, slice(0, NT), pool_did)
                pool.wait_ge(out_stored, b * 48 + 16)
                alone(pool, settled)
                for q in range(NG * NT):
                    pool.wait_ge(exped, b * ALL + (q + 1) * GH)
                    alone(pool, passed)
                    cols = q % NT * GH
                    nc.gpsimd.tensor_scalar(den[:, q % 2], row_sum[:, cols:cols + GH], 1.0, 1.0,
                                            ALU.add, ALU.mult).then_inc(den_made, 1)
                    after(pool, den_turned, b * NG * NT + max(q - 1, 0))
                    pool.wait_ge(inverted, b * NG * NT + q + 1)
                    alone(pool, passed)
                    nc.gpsimd.tensor_scalar(den_wide[:, q % 2],
                                            inv[:, q % 2].unsqueeze(2).to_broadcast([P, GH, XD]), 1.0, 1.0,
                                            ALU.mult, ALU.mult).then_inc(widened, 1)
                for k in range(NT + 1):
                    if k < NT:
                        pool.wait_ge(var_set, b * NT + k + 1)
                        power(2, slice(k, k + 1), var_out)
                    if k:
                        pool.wait_ge(square_set, b * NT + k)
                        power(4, slice(k - 1, k), square_out)
            pool.wait_ge(out_stored, batches * 48 + 16)

        @block.scalar
        def _(act):
            prime(act, turned_out, out_a, den_out)
            act.dma_start(den_t[:], t["x"][0, 0:P, 0:2 * P]).then_inc(out_stored, 16)
            with act.Fori(0, batches) as b:
                def turn_out(first, dst):
                    for i in range(NT):
                        act.wait_ge(turned, b * TURNS + first + i + 1)
                        act.activation(dst[:, :, i, 0], turn_ps[:, i % 2], ACT.Copy, scale=X_SCALE).then_inc(turned_out, 1)

                def high(g, kind, c, src):
                    act.wait_ge(qk_made, b * QK_PARTS + qk_part(g, kind, c) + 1)
                    if kind == "q" and c == 0:
                        act.wait_ge(k_in, (b * NG + g + 1) * STACK)
                    elif kind == "k" and c == 0:
                        if g:
                            for h in range(2):
                                act.wait_ge(q_in[h], (b * NG + g) * STACK)
                        else:
                            after(act, scored, b * ALL)
                    act.activation(part[:, 0, c * 512:(c + 1) * 512], src, ACT.Copy, scale=X_UNSCALE).then_inc(high_done, 1)

                def expo(n):
                    after(act, biased, b * ALL + n + 1)
                    s = n % STEPS
                    act.activation(prob[:, n % 3], prob[:, n % 3], ACT.Exp, scale=-1.0, bias=neg_max[:, s:s + 1],
                                   accum_out=row_sum[:, s:s + 1]).then_inc(exped, 1)

                def inverse_out(pair):
                    after(act, den_turned, b * NG * NT + 2 * pair + 2)
                    after(act, normed, b * PAIRS + pair)
                    act.activation(den_t[:], spare_ps[:, 0:2 * P], ACT.Copy).then_inc(den_out, 1)

                turn_out(0, ctx_t)
                for c in range(2):
                    high(0, "k", c, score_ps[:, 0, c * 512:(c + 1) * 512])
                turn_out(NT, xn_t)
                for c in range(2):
                    high(0, "q", c, score_ps[:, 1, c * 512:(c + 1) * 512])
                expo(0)
                act.wait_ge(settled, b + 1)
                for n in range(ALL):
                    pair = n // PER_PAIR
                    if n + 1 < ALL:
                        expo(n + 1)
                    if n % PER_PAIR == 0:
                        after(act, attended, b * PAIRS + max(pair - 1, 0))
                    act.wait_ge(turn_a, b * ALL + n + 1)
                    half = n // GH % 2
                    act.activation(prob_t[:, pair % 2, n % GH, 0:4, half * P:(half + 1) * P], turn_ps[:, 0],
                                   ACT.Copy).then_inc(out_a, 1)
                    if n % PER_PAIR == 2 and pair:
                        inverse_out(pair - 1)
                    w = window_of(n, 2)
                    if w and w[1] == "v":
                        act.wait_ge(v_made, b * V_PARTS + 2 * w[0] + w[2] + 1)
                        after(act, attended, b * PAIRS + w[0] * GP)
                        act.activation(v_g[:, 4 * w[2]:4 * w[2] + 4], spare_ps[:].rearrange("p (i o) -> p i o", o=P),
                                       ACT.Copy, scale=X_UNSCALE).then_inc(v_out, 1)
                    elif w:
                        high(*w, spare_ps[:])
                inverse_out(PAIRS - 1)
                def store(name, rows):
                    act.dma_start(t[name][bass.ds(b, 1)].rearrange("a (t p) d -> p (a t) d", p=P), rows
                                  ).then_inc(out_stored, 16)

                for k in range(NT + 3):
                    if 1 <= k <= NT:
                        i = k - 1
                        act.wait_ge(end_did, b * END_BATCH + normed_mark(i))
                        act.activation(squares, x_rows[:, i], ACT.Square, accum_out=small[:, 0, i:i + 1]).then_inc(squared, 1)
                    if k < 3:
                        continue
                    i = k - 3
                    if i == NT - 3:
                        after(act, x1_made, (b + 1) * NT)
                        store("x1", x1_rows)
                    act.wait_ge(turned, b * TURNS + 2 * NT + i + 1)
                    if i == NT - 1:
                        act.wait_ge(rows_ready, (b + 1) * NT)
                        store("yn", x_rows)
                    act.activation(y_parts[:, :, i, 0], turn_ps[:, i % 2], ACT.Copy, scale=Y_SCALE).then_inc(turned_out, 1)
                after(act, y_low, (b + 1) * NT)
                act.dma_start(t["yn_t"][bass.ds(b, 1)].rearrange("a p k t i c -> p (a k) (t i c)"),
                              y_parts.rearrange("p k t i c -> p k (t i c)")).then_inc(out_stored, 16)

        @block.vector
        def _(dve):
            prime(dve, normed, biased, x1_made, out_b, low_done, y_low, x_low)
            with dve.Fori(0, batches) as b:
                done = Chain(dve, dve_did, b * DVE_BATCH)

                def low(g, kind, c, src):
                    dve.wait_ge(high_done, b * QK_PARTS + qk_part(g, kind, c) + 1)
                    cols = slice(c * 512, (c + 1) * 512)
                    dve.scalar_tensor_tensor(part[:, 1, cols], src, X_UNSCALE, part[:, 0, cols], ALU.mult, ALU.subtract
                                             ).then_inc(low_done, 1)

                def turn_low(first, dst):
                    for i in range(NT):
                        after(dve, turned_out, b * TURNS + first + i + 1)
                        dve.scalar_tensor_tensor(dst[:, :, i, 1], turn_ps[:, i % 2], X_SCALE, dst[:, :, i, 0],
                                                 ALU.mult, ALU.subtract).then_inc(x_low, 1)

                def bias(n):
                    g, s = divmod(n, STEPS)
                    qt, j = divmod(s, GH)
                    after(dve, scored, b * ALL + n + 1)
                    if n >= 3:
                        dve.wait_ge(turn_b, b * ALL + n - 2)
                    alone(dve, passed)
                    dve.tensor_tensor_reduce(out=prob[:, n % 3], in0=dist[:, qt], in1=score_ps[:, n % 2],
                                             scale=keep["slopes"][:, g * GH + j:g * GH + j + 1], scalar=3.0e38,
                                             op0=ALU.add, op1=ALU.min,
                                             accum_out=neg_max[:, s:s + 1]).then_inc(biased, 1)

                def invert(q):
                    dve.wait_ge(den_made, b * NG * NT + q + 1)
                    after(dve, widened, b * NG * NT + max(q - 1, 0))
                    dve.reciprocal(inv[:, q % 2], den[:, q % 2]).then_inc(inverted, 1)

                def norm(pair):
                    g, at = divmod(pair, GP)
                    after(dve, attended, b * PAIRS + pair + 1)
                    after(dve, den_out, b * PAIRS + pair + 1)
                    dve.tensor_tensor(attn_t[:, g, at * 2 * P:(at + 1) * 2 * P], attn_ps[:, 0:2 * P], den_t[:],
                                      ALU.mult).then_inc(normed, 1)

                turn_low(0, ctx_t)
                dve.wait_ge(x_in, (b + 1) * 16)
                for i in range(NT):
                    done.mark(dve.bn_stats(stats[:, i], xs[:, i]))
                done.wait()
                alone(dve, passed)
                for i in range(NT):
                    done.mark(dve.bn_aggr(mean_var[:, i], stats[:, i]))
                done.wait()
                done.mark(dve.tensor_scalar(small[:, 0], mean_var[:, :, 1], LN_EPS, None, ALU.add))
                dve.wait_ge(pool_did, b + 1)
                for i in range(NT):
                    done.mark(dve.tensor_scalar(xs[:, i], xs[:, i], mean_var[:, i, 0:1], small[:, 1, i:i + 1],
                                                ALU.subtract, ALU.mult))
                for c in range(2):
                    low(0, "k", c, score_ps[:, 0, c * 512:(c + 1) * 512])
                turn_low(NT, xn_t)
                dve.wait_ge(pos_in, (b + 1) * 32)
                done.mark(dve.tensor_scalar(kpos_neg, kpos_i, -1.0, None, ALU.mult))
                done.mark(dve.tensor_copy(pos_f[:], pos_i[:]))
                dve.wait_ge(mask_in, (b + 1) * 16)
                for i in range(NT):
                    done.mark(dve.tensor_scalar(dist[:, i], mask[:, i], 0.0, MASKED, ALU.is_equal, ALU.mult))
                for c in range(2):
                    low(0, "q", c, score_ps[:, 1, c * 512:(c + 1) * 512])
                done.wait()
                for i in range(NT):
                    done.mark(dve.scalar_tensor_tensor(dist[:, i], kpos_neg, pos_f[:, i:i + 1], dist[:, i],
                                                       ALU.add, ALU.add))
                done.wait()
                assert done.n == DVE_BATCH
                bias(0)
                bias(1)
                dve.wait_ge(settled, b + 1)
                for n in range(ALL):
                    pair, at = divmod(n, PER_PAIR)
                    if n + 2 < ALL:
                        bias(n + 2)
                    if at == 0:
                        after(dve, attended, b * PAIRS + max(pair - 1, 0))
                    dve.wait_ge(turn_b, b * ALL + n + 1)
                    half = n // GH % 2
                    dve.tensor_copy(prob_t[:, pair % 2, n % GH, 4:8, half * P:(half + 1) * P], turn_ps[:, 1]
                                    ).then_inc(out_b, 1)
                    if n and n % GH == 0:
                        invert(n // GH - 1)
                    if at == 6 and pair:
                        norm(pair - 1)
                    w = window_of(n, 2)
                    if w and w[1] != "v":
                        low(*w, spare_ps[:])
                invert(NG * NT - 1)
                norm(PAIRS - 1)

                end = Chain(dve, end_did, b * END_BATCH)
                dve.wait_ge(x_again, (b + 1) * 16)
                dve.wait_ge(w_o_in, (b + 1) * 48)
                for k in range(NT + 4):
                    new, mid, old, back = (i if 0 <= i < NT else None for i in (k, k - 1, k - 2, k - 4))
                    if new is not None:
                        dve.wait_ge(projected, b * NT + new + 1)
                        dve.scalar_tensor_tensor(x1_rows[:, new], score_ps[:, new % 2, 0:D], keep["gates"][:, 0:1],
                                                 x_rows[:, new], ALU.mult, ALU.add).then_inc(x1_made, 1)
                    if mid is not None:
                        dve.wait_ge(var_out, b * NT + mid + 1)
                        end.mark(dve.tensor_scalar(x_rows[:, mid], x1_rows[:, mid], mean_var[:, mid, 0:1],
                                                   small[:, 3, mid:mid + 1], ALU.subtract, ALU.mult))
                    if new is not None:
                        after(dve, x1_made, b * NT + new + 1)
                        end.mark(dve.bn_stats(stats[:, new], x1_rows[:, new]))
                    if new is not None:
                        end.wait()
                        alone(dve, passed)
                        end.mark(dve.bn_aggr(mean_var[:, new], stats[:, new]))
                    if new is not None:
                        end.wait()
                        dve.tensor_scalar(small[:, 2, new:new + 1], mean_var[:, new, 1:2], LN_EPS, None, ALU.add
                                          ).then_inc(var_set, 1)
                    if mid is not None:
                        dve.wait_ge(squared, b * NT + mid + 1)
                        dve.tensor_scalar(small[:, 4, mid:mid + 1], small[:, 0, mid:mid + 1], 1e-24, 1.0 / D,
                                          ALU.max, ALU.mult).then_inc(square_set, 1)
                    if old is not None:
                        for w in range(2):
                            end.wait()
                            alone(dve, passed)
                            end.mark(dve.tensor_tensor_reduce(out=junk, in0=x_rows[:, old], in1=tokens[:, w], scale=1.0,
                                                              scalar=0.0, op0=ALU.mult, op1=ALU.add,
                                                              accum_out=route[:, w, old:old + 1]))
                        dve.wait_ge(square_out, b * NT + old + 1)
                        dve.tensor_scalar(x_rows[:, old], x_rows[:, old], small[:, 5, old:old + 1], None, ALU.mult
                                          ).then_inc(rows_ready, 1)
                    if back is not None:
                        after(dve, turned_out, b * TURNS + 2 * NT + back + 1)
                        dve.scalar_tensor_tensor(y_parts[:, :, back, 1], turn_ps[:, back % 2], Y_SCALE,
                                                 y_parts[:, :, back, 0], ALU.mult, ALU.subtract).then_inc(y_low, 1)
                end.wait()
                end.mark(dve.tensor_copy(keep["route_s"][:, :, bass.ds(b, 1), :], route[:].unsqueeze(2)))
                assert end.n == END_BATCH

        @block.tensor
        def _(pe):
            prime(pe, scored, attended, den_turned)
            with pe.Fori(0, batches) as b:
                def turn_row(first, rows, i):
                    if i >= 2:
                        after(pe, turned_out, b * TURNS + first + i - 1)
                        if first < 2 * NT:
                            after(pe, x_low, b * 2 * NT + first + i - 1)
                    for k in range(KT):
                        ins = pe.transpose(turn_ps[:, i % 2, k], rows[:, i, k * P:(k + 1) * P], keep["ident"][:])
                    ins.then_inc(turned, 1)

                def turn_rows(first, rows):
                    for i in range(NT):
                        turn_row(first, rows, i)

                def project(g, kind, c, out, k):
                    w, src = (1, ctx_t) if kind == "k" else (0, xn_t)
                    for h, (mine, other) in enumerate(HALVES):
                        ins = pe.matmul(out.rearrange("p (t c) -> p t c", c=P), w_qk[:, w, k, mine],
                                        src[:, k, 4 * c:4 * c + 4, other],
                                        start=k == 0 and h == 0, stop=k == KT - 1 and h == 2)
                    if k == KT - 1:
                        ins.then_inc(qk_made, 1)

                def fill(w, stage):
                    g, kind, c = w
                    if stage == 0:
                        if kind == "v":
                            after(pe, low_done, b * QK_PARTS + 4 * g + 4)
                            pe.wait_ge(w_v_in, (b * NG + g + 1) * 16)
                            if c:
                                pe.wait_ge(v_out, b * V_PARTS + 2 * g + 1)
                        else:
                            pe.wait_ge(v_out, b * V_PARTS + 2 * g)
                            after(pe, low_done, b * QK_PARTS + qk_part(g, kind, c))
                            pe.wait_ge(w_qk_in, (b * NG + g + 1) * 16)
                        after(pe, den_out, b * PAIRS + done_pairs[0])
                    if kind == "v":
                        for i in range(2):
                            i += 2 * stage
                            for k in range(KT):
                                for h, (mine, other) in enumerate(HALVES):
                                    ins = pe.matmul(spare_ps[:, i * P:(i + 1) * P], ctx_t[:, k, 4 * c + i, mine],
                                                    w_v[:, k, other], start=k == 0 and h == 0,
                                                    stop=k == KT - 1 and h == 2)
                        if stage:
                            ins.then_inc(v_made, 1)
                    else:
                        for k in range(2):
                            project(g, kind, c, spare_ps[:], 2 * stage + k)

                def score(n):
                    g, s = divmod(n, STEPS)
                    qt, j = divmod(s, GH)
                    if n >= 2:
                        after(pe, biased, b * ALL + n - 1)
                    if s == 0:
                        pe.wait_ge(k_in, (b * NG + g + 1) * STACK)
                        pe.wait_ge(q_in[0], (b * NG + g + 1) * STACK)
                    if s == STEPS // 2:
                        pe.wait_ge(q_in[1], (b * NG + g + 1) * STACK)
                    for c in range(2):
                        ins = pe.matmul(score_ps[:, n % 2, c * 512:(c + 1) * 512], q_stack[:, g % 2, j, qt * P:(qt + 1) * P],
                                        k_stack[:, g % 2, j, c * 512:(c + 1) * 512], start=True, stop=True)
                    ins.then_inc(scored, 1)

                def turn_inverses(pair):
                    for q in (2 * pair, 2 * pair + 1):
                        after(pe, widened, b * NG * NT + q + 1)
                        ins = pe.transpose(spare_ps[:, (q % 2) * P:(q % 2 + 1) * P],
                                           den_wide[:, q % 2].rearrange("p h d -> p (h d)"), keep["ident"][:])
                        ins.then_inc(den_turned, 1)

                def attend(pair, first, last):
                    if first == 0:
                        after(pe, out_a, b * ALL + (pair + 1) * PER_PAIR)
                        after(pe, out_b, b * ALL + (pair + 1) * PER_PAIR)
                        after(pe, normed, b * PAIRS + pair)
                        if pair % GP == 0:
                            pe.wait_ge(v_out, b * V_PARTS + (pair // GP) * 2 + 2)
                    for k in range(first, last):
                        for j in range(GH):
                            ins = pe.matmul(attn_ps[j * XD:(j + 1) * XD, 0:2 * P], v_g[:, k, j * XD:(j + 1) * XD],
                                            prob_t[:, pair % 2, j, k], start=k == 0, stop=k == NT - 1)
                    if last == NT:
                        ins.then_inc(attended, 1)

                after(pe, turned_out, b * TURNS)
                after(pe, y_low, b * NT)
                pe.wait_ge(c_in, (b + 1) * 16)
                turn_rows(0, cs)
                after(pe, x_low, b * 2 * NT + NT)
                pe.wait_ge(w_qk_in, (b * NG + 1) * 16)
                after(pe, x1_made, b * NT)
                for c in range(2):
                    for k in range(KT):
                        project(0, "k", c, score_ps[:, 0, c * 512:(c + 1) * 512], k)
                pe.wait_ge(dve_did, b * DVE_BATCH + 3 * NT + 1)
                turn_rows(NT, xs)
                after(pe, x_low, b * 2 * NT + 2 * NT)
                for c in range(2):
                    for k in range(KT):
                        project(0, "q", c, score_ps[:, 1, c * 512:(c + 1) * 512], k)
                after(pe, low_done, b * QK_PARTS + 4)
                score(0)
                score(1)
                done_pairs = [0]
                for n in range(ALL):
                    if n + 2 < ALL:
                        score(n + 2)
                    pe.wait_ge(exped, b * ALL + n + 1)
                    for h, (sem, out) in enumerate(((turn_a, out_a), (turn_b, out_b))):
                        after(pe, out, b * ALL + n)
                        for k in range(4):
                            ins = pe.transpose(turn_ps[:, h, k], prob[:, n % 3, (4 * h + k) * P:(4 * h + k + 1) * P],
                                               keep["ident"][:])
                        ins.then_inc(sem, 1)
                    if n % PER_PAIR == 1 and n > 1:
                        pair = n // PER_PAIR - 1
                        w = window_of(n - 1, 2)
                        if w and w[1] == "v":
                            pe.wait_ge(v_out, b * V_PARTS + 2 * w[0] + w[2] + 1)
                        elif w:
                            after(pe, low_done, b * QK_PARTS + qk_part(*w) + 1)
                        turn_inverses(pair)
                        done_pairs[0] = pair + 1
                    if n > PER_PAIR and n % PER_PAIR in ATTEND_AT:
                        attend(n // PER_PAIR - 1, *ATTEND_AT[n % PER_PAIR])
                    for stage in range(2):
                        w = window_of(n, stage)
                        if w:
                            fill(w, stage)
                attend(PAIRS - 1, 0, NT)
                turn_inverses(PAIRS - 1)
                after(pe, normed, (b + 1) * PAIRS)
                after(pe, biased, (b + 1) * ALL)
                pe.wait_ge(w_o_in, (b + 1) * 48)
                for i in range(NT + 3):
                    if i == 3:
                        after(pe, out_a, (b + 1) * ALL)
                        after(pe, out_b, (b + 1) * ALL)
                    if i < NT:
                        if i >= 2:
                            after(pe, x1_made, b * NT + i - 1)
                        for k in range(KT):
                            ins = pe.matmul(score_ps[:, i % 2, 0:D], attn_t[:, k, i * P:(i + 1) * P], wo_t[:, k],
                                            start=k == 0, stop=k == KT - 1)
                        ins.then_inc(projected, 1)
                    if i >= 3:
                        pe.wait_ge(rows_ready, b * NT + i - 2)
                        if i >= 5:
                            after(pe, y_low, b * NT + i - 4)
                        turn_row(2 * NT, x_rows, i - 3)


def light_attention_and_route(nc, t, keep):
    with ExitStack() as ctx:
        m = Memory(nc, ctx, "l")
        W = D // P
        w_raw = m.sb("w_raw", [P, 2, KT, D])
        w_qkv = m.sb("w_qkv", [P, 2, 3, KT, D], F16)
        w_o = m.sb("w_o", [P, KT, D])
        y_t = m.sb("y_t", [P, 2, KT, W, 2, P], F16)
        x1 = m.sb("x1", [P, 2, W, D])
        qk_t = m.sb("qk_t", [P, 2, 2, KT, D])
        v = m.sb("v", [P, 2, W, D])
        prob = m.sb("prob", [P, 2, 2, HP, P])
        prob_t = m.sb("prob_t", [P, 2, 2, HP, P])
        attn_t = m.sb("attn_t", [P, 2, HP, P])
        top = m.sb("top", [P, 2, FH])
        total = m.sb("total", [P, 2, FH])
        inv = m.sb("inv", [P, 2, FH])
        score_ps = m.ps("score_ps", [P, 2, HP, P])
        turn_ps = m.ps("turn_ps", [P, 2, HP, P])
        attn_ps = m.ps("attn_ps", [P, HP, P])
        proj_ps = m.ps("proj_ps", [P, 2, D])
        sum_ps = m.ps("sum_ps", [P, 512])
        G = 2 * B
        s = keep["route_s"][:].rearrange("p w b t -> p (w b) t")
        log_k, minus_a, part_max, s_max = (m.sb(name, [P, G]) for name in ("log_k", "minus_a", "part_max", "s_max"))
        most, most_k, part_sum, log_sum = (m.sb(name, [P, G]) for name in ("most", "most_k", "part_sum", "log_sum"))
        x, e, score_f, rest = (m.sb(name, [P, G, NT]) for name in ("x", "e", "score_f", "rest"))
        score_rows = m.sb("score_rows", [B * NT, P])
        all_scores = m.sb("all_scores", [P, B * NT, P])
        counts = m.sb("counts", [P, B * NT, 4])
        hit = m.sb("hit", [P, S])
        hit_tile = m.sb("hit_tile", [P, P])
        rank = m.sb("rank", [P, B, NT])
        far = m.sb("far", [P, B, NT])
        CH = NT // 2
        rows = m.sb("rows", [P, 2, CH, D])
        w_scaled, w_high, w_set = m.sem("w_scaled"), m.sem("w_high"), m.sem("w_set")
        w_in, wo_in = [m.sem(f"w_in{i}") for i in range(3)], m.sem("wo_in")
        y_in = [m.sem(f"y_in{half}") for half in range(2)]
        x_in = [m.sem(f"x_in{half}") for half in range(2)]
        stored = [m.sem(f"stored{half}") for half in range(2)]
        projected, proj_out = m.sem("projected"), m.sem("proj_out")
        scored, topped, shifted, exped = m.sem("scored"), m.sem("topped"), m.sem("shifted"), m.sem("exped")
        summed, inverted, scaled = m.sem("summed"), m.sem("inverted"), m.sem("scaled")
        turned, turned_out, attended, attn_out = m.sem("turned"), m.sem("turned_out"), m.sem("attended"), m.sem("attn_out")
        out_made, result = m.sem("out_made"), m.sem("result")
        dve_did, top_parts, top_all, stepped = m.sem("dve_did"), m.sem("top_parts"), m.sem("top_all"), m.sem("stepped")
        r_exped, r_summed, r_added, r_logged = m.sem("r_exped"), m.sem("r_summed"), m.sem("r_added"), m.sem("r_logged")
        renewed, final_set, r_scored = m.sem("renewed"), m.sem("final_set"), m.sem("r_scored")
        r_turned, rows_made, score_out, scores_in = (m.sem(name) for name in ("r_turned", "rows_made", "score_out", "scores_in"))
        ranked = m.sem("ranked")
        rows_in = [m.sem(f"rows_in{c}") for c in range(2)]
        scattered = [m.sem(f"scattered{c}") for c in range(2)]
        passed = keep["passed"]
        block = ctx.enter_context(nc.Block())
        PROJ = 3 * KT
        PER_W = PROJ // W
        ALL = 2 * W
        PER_SLOT = 3
        assert 1 + PER_SLOT * ALL * (B - 2) == ITERS - 1
        MARKS = 4
        RANKS = {u: 3 for u in range(1, 11)}
        RANKS[11] = 2
        SCATTER = {4: 0, 7: 1, 10: 2, 12: 3}
        assert sum(RANKS.values()) == B * NT

        def iteration(b, w, c):
            return (b * ALL + w) * PER_SLOT + c + 1

        def wide(a):
            return a.unsqueeze(2).to_broadcast([P, G, NT])

        def bank(i):
            return i % PER_W % 2

        def batches(eng, body):
            with eng.Fori(0, B - 2) as b:
                body(b, 0)
            body(B - 2, 1)
            body(B - 1, 2)

        def rank_slot(part, w):
            return (part - 1) * ALL + w

        def heads(a):
            return a.rearrange("p a b c -> p (a b) c")

        @block.sync
        def _(sp):
            def load_y(b, half):
                sp.dma_start(y_t[:, half].rearrange("p k t i c -> p k (t i c)"),
                             t["yn_t"][bass.ds(b, 1), :, :, half * W:(half + 1) * W]
                             .rearrange("a p k t i c -> p (a k) (t i c)")).then_inc(y_in[half], 16)

            def load_x(b, half):
                sp.dma_start(x1[:, half], t["x1"][bass.ds(b, 1), half * D:(half + 1) * D]
                             .rearrange("a (t p) d -> p (a t) d", p=P)).then_inc(x_in[half], 16)

            wkv = t["L0_ffn_wkv_light"]
            raw = (t["L0_ffn_wq_light"], wkv[:, 0:D], wkv[:, D:2 * D])
            sp.dma_start(w_raw[:, 0], raw[0].rearrange("(k p) o -> p k o", p=P)).then_inc(w_in[0], 16)
            load_y(0, 0)
            for i in range(1, 3):
                if i == 2:
                    sp.wait_ge(w_set, 1)
                sp.dma_start(w_raw[:, i % 2], raw[i].rearrange("(k p) o -> p k o", p=P)).then_inc(w_in[i], 16)
            load_y(0, 1)
            load_x(0, 0)
            load_x(0, 1)
            sp.dma_start(w_o[:], t["L0_ffn_wo_light"].rearrange("(k p) o -> p k o", p=P)).then_inc(wo_in, 16)

            def load_rows(c):
                sp.dma_start(rows[:, c % 2], t["yn"][c // 2, c % 2 * CH * P:(c % 2 + 1) * CH * P]
                             .rearrange("(t p) d -> p t d", p=P)).then_inc(rows_in[c % 2], 16)

            def body(b, part):
                last, descends = part == 2, part == 0
                if not last:
                    after(sp, projected, (2 * b + 1) * PROJ)
                    load_y(b + 1, 0)
                if part == 1:
                    sp.wait_ge(rows_made, 1)
                    sp.dma_start(t["scores"], score_rows[:]).then_inc(score_out, 16)
                    sp.wait_ge(score_out, 16)
                    sp.dma_start(all_scores[:], t["scores"].unsqueeze(0).to_broadcast([P, B * NT, P])).then_inc(scores_in, 16)
                for half in range(2):
                    if part:
                        for c in {(1, 1): (2, 3), (2, 0): (4, 5), (2, 1): (6, 7)}.get((part, half), ()):
                            sp.wait_ge(scattered[c % 2], c // 2 * CH * 16)
                            load_rows(c)
                    after(sp, result, b * ALL + (half + 1) * W)
                    sp.dma_start(t["mid"][bass.ds(b, 1), half * D:(half + 1) * D]
                                 .rearrange("a (t p) d -> p (a t) d", p=P), x1[:, half]).then_inc(stored[half], 16)
                    if half == 0 and not last:
                        after(sp, projected, (2 * b + 2) * PROJ)
                        load_y(b + 1, 1)
                    if not last:
                        sp.wait_ge(stored[half], (b + 1) * 16)
                        load_x(b + 1, half)

            load_rows(0)
            load_rows(1)
            batches(sp, body)
            for half in range(2):
                sp.wait_ge(stored[half], B * 16)

        @block.gpsimd
        def _(pool):
            def scale(nw, w):
                pool.wait_ge(inverted, nw + 1)
                nc.gpsimd.tensor_tensor(heads(prob[:, w % 2]), heads(prob[:, w % 2]),
                                        inv[:, w % 2].unsqueeze(2).to_broadcast([P, FH, P]), ALU.mult
                                        ).then_inc(scaled, 1)

            def scatter(b):
                pool.wait_ge(ranked, b + 1)
                for i in range(NT):
                    c = i // CH
                    if i % CH == 0:
                        pool.wait_ge(rows_in[c], (b + 1) * 16)
                    nc.gpsimd.indirect_dma_start(
                        t["q_rows"], bass.IndirectOffsetOnAxis(keep["place"][:, b, i:i + 1], 0),
                        rows[:, c, i % CH], None, bounds_check=B * NQ - 1, oob_is_err=False).then_inc(scattered[c], 16)

            def body(b, part):
                last, descends = part == 2, part == 0
                for w in range(ALL):
                    if not (last and w == ALL - 1):
                        scale(b * ALL + w + 1, w + 1)
                    if part and rank_slot(part, w) in SCATTER:
                        scatter(SCATTER[rank_slot(part, w)])

            pool.wait_ge(top_parts, 1)
            nc.gpsimd.partition_all_reduce(s_max[:], part_max[:], P, bass.bass_isa.ReduceOp.max).then_inc(top_all, 1)
            scale(0, 0)
            batches(pool, body)
            for c in range(2):
                pool.wait_ge(scattered[c], B * CH * 16)

        @block.scalar
        def _(act):
            prime(act, proj_out, turned_out, attn_out)

            def copy_projection(n, half, i, src):
                after(act, projected, n * PROJ + i + 1)
                dst = qk_t[:, half, i // KT, i % KT] if i < 2 * KT else v[:, half, i % KT]
                act.activation(dst, proj_ps[:, src], ACT.Copy, scale=UNSCALE).then_inc(proj_out, 1)

            def exponents(j):
                act.wait_ge(stepped, j * MARKS + 3)
                act.activation(e[:], x[:], ACT.Exp).then_inc(r_exped, 1)

            def logarithms(j):
                act.wait_ge(r_added, j + 1)
                act.activation(log_sum[:], sum_ps[:, 0:G], ACT.Ln).then_inc(r_logged, 1)

            def expo(nw, w):
                after(act, shifted, nw + 1)
                act.activation(prob[:, w % 2], prob[:, w % 2], ACT.Exp, scale=float(FD) ** -0.5).then_inc(exped, 1)

            def body(b, part):
                last, descends = part == 2, part == 0
                for w in range(ALL):
                    nw, half = b * ALL + w, w // W
                    more = not (last and half)
                    n = 2 * b + half + 1
                    i = w % W * PER_W
                    if descends:
                        exponents(iteration(b, w, 0))
                    elif part == 1 and w == 0:
                        act.wait_ge(final_set, 1)
                        act.activation(score_f[:], x[:], ACT.Exp).then_inc(r_scored, 1)
                    if not (last and w == ALL - 1):
                        expo(nw + 1, w + 1)
                    if more:
                        if i == 0:
                            after(act, scored, b * ALL + half * W)
                        copy_projection(n, 1 - half, i, bank(i))
                    if descends:
                        logarithms(iteration(b, w, 0))
                    after(act, turned, nw + 1)
                    act.activation(prob_t[:, w % 2], turn_ps[:], ACT.Copy).then_inc(turned_out, 1)
                    if descends:
                        exponents(iteration(b, w, 1))
                    if more:
                        copy_projection(n, 1 - half, i + 1, bank(i + 1))
                    after(act, attended, nw + 1)
                    act.activation(attn_t[:, w % 2], attn_ps[:], ACT.Copy).then_inc(attn_out, 1)
                    if descends:
                        logarithms(iteration(b, w, 1))
                        exponents(iteration(b, w, 2))
                    if more:
                        copy_projection(n, 1 - half, i + 2, bank(i + 2))
                    if descends:
                        logarithms(iteration(b, w, 2))

            for i in range(3):
                act.wait_ge(w_scaled, (i + 1) * KT)
                act.activation(w_qkv[:, 0, i], w_raw[:, i % 2], ACT.Copy).then_inc(w_high, 1)
            exponents(0)
            for i in range(PROJ):
                copy_projection(0, 0, i, i % 2)
            logarithms(0)
            expo(0, 0)
            batches(act, body)

        @block.vector
        def _(dve):
            prime(dve, result, shifted)

            def shift(nw, w):
                after(dve, scored, nw + 1)
                dve.reduce_max(top[:, w % 2], heads(score_ps[:]), AX.X).then_inc(topped, 1)
                dve.wait_ge(topped, nw + 1)
                if w:
                    after(dve, turned, nw - 1)
                dve.tensor_tensor(heads(prob[:, w % 2]), heads(score_ps[:]),
                                  top[:, w % 2].unsqueeze(2).to_broadcast([P, FH, P]), ALU.subtract).then_inc(shifted, 1)

            def sums(nw, w):
                dve.wait_ge(exped, nw + 1)
                dve.reduce_sum(total[:, w % 2], heads(prob[:, w % 2]), AX.X).then_inc(summed, 1)
                dve.wait_ge(summed, nw + 1)
                dve.reciprocal(inv[:, w % 2], total[:, w % 2]).then_inc(inverted, 1)

            def clip(j):
                step = Chain(dve, stepped, j * MARKS)
                if not (isinstance(j, int) and j == 0):
                    dve.wait_ge(renewed, j)
                step.mark(dve.tensor_tensor(most[:], s_max[:], minus_a[:], ALU.min))
                step.mark(dve.tensor_tensor(x[:], s, wide(minus_a[:]), ALU.min))
                step.wait()
                step.mark(dve.tensor_tensor(x[:], x[:], wide(most[:]), ALU.subtract))
                step.mark(dve.tensor_tensor(most_k[:], most[:], log_k[:], ALU.subtract))
                assert step.n == MARKS

            def add_up(j):
                dve.wait_ge(r_exped, j + 1)
                dve.reduce_sum(part_sum[:], e[:], AX.X).then_inc(r_summed, 1)

            def renew(j):
                dve.wait_ge(r_logged, j + 1)
                dve.wait_ge(stepped, (j + 1) * MARKS)
                dve.tensor_tensor(minus_a[:], log_sum[:], most_k[:], ALU.add).then_inc(renewed, 1)

            own = Chain(dve, dve_did)

            def final_scores():
                dve.wait_ge(renewed, ITERS - 1)
                own.mark(dve.tensor_tensor(x[:], s, wide(minus_a[:]), ALU.subtract))
                own.wait()
                dve.tensor_scalar(x[:], x[:], 0.0, None, ALU.min).then_inc(final_set, 1)

            def factors():
                dve.wait_ge(r_scored, 1)
                own.mark(dve.tensor_scalar(rest[:], score_f[:], -1.0, 1.0, ALU.mult, ALU.add))
                own.wait()
                own.mark(dve.tensor_tensor(keep["factor"][:].rearrange("p w b t -> p (w b) t"), score_f[:], rest[:], ALU.add))
                own.wait()
                own.mark(dve.tensor_scalar(keep["q_gate"][:].rearrange("p b t -> p (b t)"),
                                           keep["factor"][:, 0].rearrange("p b t -> p (b t)"),
                                           keep["gates"][:, 1:2], None, ALU.mult))
                dve.wait_ge(r_turned, 1)
                dve.tensor_copy(score_rows[:], sum_ps[0:B * NT, P:2 * P]).then_inc(rows_made, 1)

            def rank_tile(n):
                b, i = divmod(n, NT)
                mine = score_f[:, b, i:i + 1]
                if i:
                    own.mark(dve.tensor_scalar(hit[:, 0:i * P],
                                               all_scores[:, b * NT:n].rearrange("p a c -> p (a c)"), mine,
                                               None, ALU.is_ge, ALU.add, accum_out=counts[:, n, 0:1]))
                if i < NT - 1:
                    own.mark(dve.tensor_scalar(hit[:, (i + 1) * P:S],
                                               all_scores[:, n + 1:(b + 1) * NT].rearrange("p a c -> p (a c)"), mine,
                                               None, ALU.is_gt, ALU.add, accum_out=counts[:, n, 1:2]))
                for c, (op, side) in enumerate(((ALU.is_ge, "before"), (ALU.is_gt, "after"))):
                    own.mark(dve.scalar_tensor_tensor(hit[:, i * P:(i + 1) * P] if c else hit_tile[:],
                                                      all_scores[:, n], mine, keep[side][:],
                                                      op, ALU.mult, accum_out=counts[:, n, 2 + c:3 + c]))
                own.wait()
                if i == NT - 1:
                    own.mark(dve.reduce_sum(rank[:, b], counts[:, b * NT:(b + 1) * NT], AX.X))
                    own.wait()
                    own.mark(dve.tensor_scalar(far[:, b], rank[:, b], float(NQ), float(OUT_OF_RANGE), ALU.is_ge, ALU.mult))
                    own.wait()
                    own.mark(dve.tensor_tensor(keep["row"][:, b], rank[:, b], far[:, b], ALU.add))
                    own.mark(dve.scalar_tensor_tensor(far[:, b], rank[:, b], float(b * NQ), far[:, b], ALU.add, ALU.add))
                    own.wait()
                    dve.tensor_copy(keep["place"][:, b], far[:, b]).then_inc(ranked, 1)

            def body(b, part):
                last, descends = part == 2, part == 0
                for w in range(ALL):
                    nw, half = b * ALL + w, w // W
                    if descends:
                        clip(iteration(b, w, 0))
                    elif part == 1 and w == 0:
                        final_scores()
                    if not (last and w == ALL - 1):
                        shift(nw + 1, w + 1)
                        if descends:
                            add_up(iteration(b, w, 0))
                        sums(nw + 1, w + 1)
                    if descends:
                        renew(iteration(b, w, 0))
                        clip(iteration(b, w, 1))
                        add_up(iteration(b, w, 1))
                        renew(iteration(b, w, 1))
                        clip(iteration(b, w, 2))
                        add_up(iteration(b, w, 2))
                    elif part == 1 and w == 0:
                        factors()
                    elif rank_slot(part, w) in RANKS:
                        dve.wait_ge(scores_in, 16)
                        slot = rank_slot(part, w)
                        first = sum(RANKS[u] for u in RANKS if u < slot)
                        for n in range(first, first + RANKS[slot]):
                            rank_tile(n)
                    if w % W == 0:
                        dve.wait_ge(x_in[half], (b + 1) * 16)
                    dve.wait_ge(out_made, nw + 1)
                    dve.scalar_tensor_tensor(x1[:, half, w % W], proj_ps[:, 1], keep["gates"][:, 1:2],
                                             x1[:, half, w % W], ALU.mult, ALU.add).then_inc(result, 1)
                    if descends:
                        renew(iteration(b, w, 2))

            for i in range(3):
                dve.wait_ge(w_in[i], 16)
                for k in range(KT):
                    dve.tensor_scalar(w_raw[:, i % 2, k], w_raw[:, i % 2, k], keep["gammas"][:, 0, k:k + 1], None, ALU.mult
                                      ).then_inc(w_scaled, 1)
                dve.wait_ge(w_high, i + 1)
                dve.tensor_tensor(w_qkv[:, 1, i], w_raw[:, i % 2], w_qkv[:, 0, i], ALU.subtract).then_inc(w_set, 1)
            dve.reduce_max(part_max[:], s, AX.X).then_inc(top_parts, 1)
            own.mark(dve.memset(log_k[:, 0:B], LOG_KQ))
            own.mark(dve.memset(log_k[:, B:G], LOG_KKV))
            own.mark(dve.memset(counts[:], 0.0))
            own.mark(dve.memset(minus_a[:, 0:B], float(np.log(np.float32(S))) - LOG_KQ))
            own.mark(dve.memset(minus_a[:, B:G], float(np.log(np.float32(S))) - LOG_KKV))
            own.wait()
            dve.wait_ge(top_all, 1)
            clip(0)
            add_up(0)
            renew(0)
            shift(0, 0)
            sums(0, 0)
            batches(dve, body)

        @block.tensor
        def _(pe):
            prime(pe, projected, scored, attended, turned)

            def project(n, half, i, dst):
                for k in range(KT):
                    for n_half, (a, c) in enumerate(HALVES):
                        if i < 2 * KT:
                            lhs, rhs = w_qkv[:, a, i // KT, k, (i % KT) * P:(i % KT + 1) * P], y_t[:, half, k, :, c]
                            out = proj_ps[:, dst].rearrange("p (t c) -> p t c", c=P)
                        else:
                            lhs, rhs, out = y_t[:, half, k, i % KT, a], w_qkv[:, c, 2, k], proj_ps[:, dst]
                        ins = pe.matmul(out, lhs, rhs, start=k == 0 and n_half == 0, stop=k == KT - 1 and n_half == 2)
                ins.then_inc(projected, 1)

            def all_sum(j):
                pe.wait_ge(r_summed, j + 1)
                pe.matmul(sum_ps[:, 0:G], keep["ones"][:], part_sum[:], start=True, stop=True).then_inc(r_added, 1)

            def score(n, nw, w):
                if w % W == 0:
                    after(pe, proj_out, n * PROJ + 2 * KT)
                after(pe, shifted, nw)
                cut = slice(w % W * P, (w % W + 1) * P)
                half = w // W % 2
                for h in range(FH):
                    row = (h % 2) * FD
                    ins = pe.matmul(score_ps[:, h % 2, h // 2], qk_t[row:row + FD, half, 0, h // 2, cut],
                                    qk_t[row:row + FD, half, 1, h // 2, cut], start=True, stop=True)
                ins.then_inc(scored, 1)

            def body(b, part):
                last, descends = part == 2, part == 0
                for w in range(ALL):
                    nw, half = b * ALL + w, w // W
                    more = not (last and half)
                    n = 2 * b + half + 1
                    i = w % W * PER_W
                    if not (last and w == ALL - 1):
                        score(2 * b + (w + 1) // W, nw + 1, w + 1)
                    if more:
                        if i == 0:
                            pe.wait_ge(y_in[1 - half], (b + half + 1) * 16)
                        after(pe, proj_out, n * PROJ + i)
                        project(n, 1 - half, i, bank(i))
                    if descends:
                        all_sum(iteration(b, w, 0))
                    elif part == 1 and w == 0:
                        pe.wait_ge(r_scored, 1)
                        pe.transpose(sum_ps[0:B * NT, P:2 * P], score_f[:, 0:B].rearrange("p b t -> p (b t)"),
                                     keep["ident"][:]).then_inc(r_turned, 1)
                    pe.wait_ge(scaled, nw + 1)
                    after(pe, turned_out, nw)
                    for h in range(FH):
                        ins = pe.transpose(turn_ps[:, h % 2, h // 2], prob[:, w % 2, h % 2, h // 2], keep["ident"][:])
                    ins.then_inc(turned, 1)
                    if more:
                        after(pe, result, nw)
                        project(n, 1 - half, i + 1, bank(i + 1))
                    if w % W == 0:
                        after(pe, proj_out, n * PROJ)
                    after(pe, turned_out, nw + 1)
                    after(pe, attn_out, nw)
                    for h in range(FH):
                        row = (h % 2) * FD
                        ins = pe.matmul(attn_ps[row:row + FD, h // 2], v[:, half, w % W, h * FD:(h + 1) * FD],
                                        prob_t[:, w % 2, h % 2, h // 2], start=True, stop=True)
                    ins.then_inc(attended, 1)
                    if descends:
                        all_sum(iteration(b, w, 1))
                    if more:
                        after(pe, proj_out, n * PROJ + i + 1)
                        project(n, 1 - half, i + 2, bank(i + 2))
                        after(pe, proj_out, n * PROJ + i + 2)
                    else:
                        after(pe, result, nw)
                    after(pe, attn_out, nw + 1)
                    for k in range(HP):
                        ins = pe.matmul(proj_ps[:, 1], attn_t[:, w % 2, k], w_o[:, k], start=k == 0, stop=k == HP - 1)
                    ins.then_inc(out_made, 1)
                    if descends:
                        all_sum(iteration(b, w, 2))

            pe.wait_ge(y_in[0], 16)
            for i in range(PROJ):
                if i % KT == 0:
                    pe.wait_ge(w_set, i // KT + 1)
                if i >= 2:
                    after(pe, proj_out, i - 1)
                project(0, 0, i, i % 2)
            all_sum(0)
            score(0, 0, 0)
            pe.wait_ge(wo_in, 16)
            batches(pe, body)


def heavy_attention(nc, t, keep):
    with ExitStack() as ctx:
        m = Memory(nc, ctx, "h")
        QT = NQ // P
        y_t = m.sb("y_t", [P, KT, NT, 2, P], F16)
        q_rows = m.sb("q_rows", [P, QT, D])
        xq_t = m.sb("xq_t", [P, KT, QT, 2, P], F16)
        w_qk = m.sb("w_qk", [P, 2, KT, 2, P], F16)
        w_v = m.sb("w_v", [P, KT, 2, P], F16)
        w_o = m.sb("w_o", [P, KT, D])
        part = m.sb("part", [P, 2, NQ + S], F16)
        q_stack = m.sb("q_stack", [P, 2, 2, NQ], F16)
        k_stack = m.sb("k_stack", [P, 2, 2, 2, S], F16)
        v_g = m.sb("v_g", [P, NT, P])
        factor_b = m.sb("factor_b", [P, NT])
        prob = m.sb("prob", [P, 3, S])
        prob_t = m.sb("prob_t", [P, 2, 2, NT, NQ])
        attn_t = m.sb("attn_t", [P, HP, NQ])
        neg_max = m.sb("neg_max", [P, 2, QT * 2])
        row_sum = m.sb("row_sum", [P, 2, QT * 2])
        inv = m.sb("inv", [P, QT * 2])
        inv_wide = m.sb("inv_wide", [P, QT * 2, FD])
        inv_t = m.sb("inv_t", [P, NQ])
        out_rows = m.sb("out_rows", [P, QT, D])
        mid = m.sb("mid", [P, NT, D])
        routed = m.sb("routed", [P, NT, D])
        place_b = m.sb("place_b", [P, NT], I32)
        gate_b = m.sb("gate_b", [P, NT])
        score_ps = m.ps("score_ps", [P, 2, S])
        turn_ps = m.ps("turn_ps", [P, 2, 4, P])
        attn_ps = m.ps("attn_ps", [P, NQ])
        spare_ps = m.ps("spare_ps", [P, 512])
        y_in, rows_in, w_qk_in, w_v_in, wo_in, stored = (m.sem(n) for n in
                                                         ("y_in", "rows_in", "w_qk_in", "w_v_in", "wo_in", "stored"))
        stack_in = m.sem("stack_in")
        rows_turned, rows_turned_out, factor_set = m.sem("rows_turned"), m.sem("rows_turned_out"), m.sem("factor_set")
        rows_low = m.sem("rows_low")
        made, v_made, high_done, low_done, v_out = (m.sem(n) for n in ("made", "v_made", "high_done", "low_done", "v_out"))
        scored, topped, exped = m.sem("scored"), m.sem("topped"), m.sem("exped")
        turn_a, turn_b, out_a, out_b = m.sem("turn_a"), m.sem("turn_b"), m.sem("out_a"), m.sem("out_b")
        inverted, widened, inv_turned, inv_out = (m.sem(n) for n in ("inverted", "widened", "inv_turned", "inv_out"))
        attended, normed, projected, proj_out = (m.sem(n) for n in ("attended", "normed", "projected", "proj_out"))
        combined, last_added = m.sem("combined"), m.sem("last_added")
        taken, placed, mid_in, gathered = m.sem("taken"), m.sem("placed"), m.sem("mid_in"), m.sem("gathered")
        cleared, added, out_stored = m.sem("cleared"), m.sem("added"), m.sem("out_stored")
        passed = keep["passed"]
        LC = 2
        last_in = [m.sem(f"last_in{c}") for c in range(LC)]
        block = ctx.enter_context(nc.Block())
        STEPS = QT * 2
        ALL = HP * STEPS
        STACK = 2 * (2 + 2) * 16
        PARTS = 3 * HP
        FILLS = {0: ("qk", 0), 1: ("qk", 1), 2: ("qk", 2), 3: ("inverse", 0), 5: ("v", 0), 6: ("v", 1)}
        ATTEND_AT = {0: (0, 2), 1: (2, 4), 2: (4, 6), 3: (6, NT)}

        def fill_of(n):
            g, s = divmod(n, STEPS)
            if n < 0 or s not in FILLS:
                return None
            kind, c = FILLS[s]
            g += {"qk": 1, "inverse": -1, "v": 0}[kind]
            return (kind, g, c) if 0 <= g < HP else None

        @block.sync
        def _(sp):
            def load_qk(g):
                sp.dma_start(w_qk[:].rearrange("p w k i o -> p w (k i o)"),
                             t["heavy_wt"][g, 0:2].rearrange("w p k i o -> p w (k i o)")).then_inc(w_qk_in, 16)

            def load_v(g):
                sp.dma_start(w_v[:], t["heavy_wt"][g, 2]).then_inc(w_v_in, 16)

            def stack_up(b, g):
                after(sp, low_done, b * PARTS + 3 * g + 1)
                for h in range(2):
                    rows = slice(h * FD, (h + 1) * FD)
                    for half in range(2):
                        sp.dma_start(q_stack[half * FD:(half + 1) * FD, g % 2, h], part[rows, half, 0:NQ]
                                     ).then_inc(stack_in, 16)
                after(sp, low_done, b * PARTS + 3 * g + 3)
                for h in range(2):
                    rows = slice(h * FD, (h + 1) * FD)
                    for r in range(2):
                        sp.dma_start(k_stack[r * FD:(r + 1) * FD, g % 2, :, h], part[rows, :, NQ:]
                                     ).then_inc(stack_in, 16)

            sp.dma_start(w_o[:], t["L0_ffn_wo_heavy"].rearrange("(k p) o -> p k o", p=P)).then_inc(wo_in, 16)
            with sp.Fori(0, B) as b:
                after(sp, v_made, b * HP * 2)
                sp.dma_start(q_rows[:], t["q_rows"].rearrange("(b t p) d -> b p t d", b=B, p=P)[bass.ds(b, 1)]
                             .rearrange("a p t d -> p (a t) d")).then_inc(rows_in, 16)
                load_qk(0)
                sp.dma_start(y_t[:].rearrange("p k t i c -> p (k t i c)"),
                             t["yn_t"][bass.ds(b, 1)].rearrange("a p k t i c -> p (a k t i c)")).then_inc(y_in, 16)
                load_v(0)
                stack_up(b, 0)
                for g in range(HP - 1):
                    sp.wait_ge(made, b * PARTS + 3 * g + 3)
                    load_qk(g + 1)
                    stack_up(b, g + 1)
                    after(sp, v_made, (b * HP + g + 1) * 2)
                    load_v(g + 1)
            for c in range(LC):
                sp.wait_ge(last_added, (c + 1) * NT // LC)
                cut = slice(c * NT // LC, (c + 1) * NT // LC)
                sp.dma_start(t["out"][B - 1].rearrange("(t p) d -> p t d", p=P)[:, cut], mid[:, cut]).then_inc(stored, 16)
            sp.wait_ge(stored, (B + LC) * 16)

        @block.gpsimd
        def _(pool):
            prime(pool, widened, taken, combined)

            def body(b, last):
                pool.dma_start(mid[:], t["mid"][bass.ds(b, 1)].rearrange("a (t p) d -> p (a t) d", p=P)).then_inc(mid_in, 16)
                nc.gpsimd.memset(routed[:], 0.0).then_inc(cleared, 1)
                for g in range(HP):
                    pool.wait_ge(inverted, b * HP + g + 1)
                    after(pool, inv_turned, b * HP + g)
                    alone(pool, passed)
                    nc.gpsimd.tensor_scalar(inv_wide[:], inv[:].unsqueeze(2).to_broadcast([P, QT * 2, FD]),
                                            1.0, 1.0, ALU.mult, ALU.mult).then_inc(widened, 1)
                pool.wait_ge(placed, 2 * b + 2)
                pool.wait_ge(cleared, b + 1)
                pool.wait_ge(stored, (b + 1) * 16)
                alone(pool, taken)
                for i in range(NT):
                    nc.gpsimd.indirect_dma_start(
                        routed[:, i], None, t["h_rows"], bass.IndirectOffsetOnAxis(place_b[:, i:i + 1], 0),
                        bounds_check=NQ - 1, oob_is_err=False).then_inc(last_in[i // (NT // LC)] if last else gathered, 16)
                if last:
                    return
                pool.wait_ge(mid_in, (b + 1) * 16)
                pool.wait_ge(gathered, (b + 1) * NT * 16)
                alone(pool, passed)
                nc.gpsimd.tensor_tensor(routed[:], routed[:], gate_b[:].unsqueeze(2).to_broadcast([P, NT, D]), ALU.mult
                                        ).then_inc(added, 1)
                pool.wait_ge(added, 2 * b + 1)
                nc.gpsimd.tensor_tensor(mid[:], mid[:], routed[:], ALU.add).then_inc(added, 1)
                pool.wait_ge(added, 2 * b + 2)
                alone(pool, passed)
                pool.dma_start(t["out"][bass.ds(b, 1)].rearrange("a (t p) d -> p (a t) d", p=P), mid[:]).then_inc(out_stored, 16)
                pool.wait_ge(out_stored, (b + 1) * 16)
                alone(pool, combined)

            with pool.Fori(0, B - 1) as b:
                body(b, False)
            body(B - 1, True)

        @block.scalar
        def _(act):
            prime(act, exped, out_a, inv_out, proj_out)
            with act.Fori(0, B) as b:
                def high(g, n, src):
                    act.wait_ge(made, b * PARTS + 3 * g + n + 1)
                    if n == 0 and g:
                        act.wait_ge(stack_in, (b * HP + g) * STACK)
                    elif n == 0:
                        after(act, scored, b * ALL)
                    act.activation(part[:, 0, n * 512:(n + 1) * 512], src, ACT.Copy, scale=UNSCALE).then_inc(high_done, 1)

                def expo(n):
                    g, s = divmod(n, STEPS)
                    act.wait_ge(topped, b * ALL + n + 1)
                    if n >= 3:
                        act.wait_ge(turn_b, b * ALL + n - 2)
                    act.activation(prob[:, n % 3], score_ps[:, n % 2], ACT.Exp, scale=-1.0, bias=neg_max[:, g % 2, s:s + 1],
                                   accum_out=row_sum[:, g % 2, s:s + 1]).then_inc(exped, 1)

                def inverse_out(g):
                    after(act, inv_turned, b * HP + g + 1)
                    after(act, normed, b * HP + g)
                    act.activation(inv_t[:], spare_ps[:], ACT.Copy).then_inc(inv_out, 1)

                for i in range(QT):
                    act.wait_ge(rows_turned, b * QT + i + 1)
                    act.activation(xq_t[:, :, i, 0], turn_ps[:, i % 2], ACT.Copy, scale=Y_SCALE).then_inc(rows_turned_out, 1)
                for n in range(3):
                    high(0, n, score_ps[:, n // 2, n % 2 * 512:n % 2 * 512 + 512])
                expo(0)
                for n in range(ALL):
                    g, s = divmod(n, STEPS)
                    f = fill_of(n - 1)
                    if f and f[0] == "qk":
                        high(f[1], f[2], spare_ps[:])
                    elif f and f[0] == "inverse":
                        inverse_out(f[1])
                    if n + 1 < ALL:
                        expo(n + 1)
                    if s == 0:
                        after(act, attended, b * HP + max(g - 1, 0))
                    act.wait_ge(turn_a, b * ALL + n + 1)
                    act.activation(prob_t[:, g % 2, n % 2, 0:4, s // 2 * P:s // 2 * P + P], turn_ps[:, 0],
                                   ACT.Copy).then_inc(out_a, 1)
                inverse_out(HP - 1)
                after(act, taken, b)
                for i in range(QT):
                    act.wait_ge(projected, b * QT + i + 1)
                    act.activation(out_rows[:, i], score_ps[:, i % 2, 0:D], ACT.Copy).then_inc(proj_out, 1)
                after(act, proj_out, (b + 1) * QT)
                after(act, combined, b)
                act.dma_start(t["h_rows"].rearrange("(t p) d -> p t d", p=P), out_rows[:]).then_inc(stored, 16)

        @block.vector
        def _(dve):
            prime(dve, v_out, out_b, normed, low_done)
            with dve.Fori(0, B) as b:
                def low(g, n, src):
                    dve.wait_ge(high_done, b * PARTS + 3 * g + n + 1)
                    cols = slice(n * 512, (n + 1) * 512)
                    dve.scalar_tensor_tensor(part[:, 1, cols], src, UNSCALE, part[:, 0, cols], ALU.mult, ALU.subtract
                                             ).then_inc(low_done, 1)

                def least(n):
                    g, s = divmod(n, STEPS)
                    after(dve, scored, b * ALL + n + 1)
                    dve.tensor_reduce(neg_max[:, g % 2, s:s + 1], score_ps[:, n % 2], axis=AX.X, op=ALU.min
                                      ).then_inc(topped, 1)

                def invert(g):
                    after(dve, exped, b * ALL + (g + 1) * STEPS)
                    after(dve, widened, b * HP + g)
                    dve.reciprocal(inv[:], row_sum[:, g % 2]).then_inc(inverted, 1)

                def norm(g):
                    after(dve, attended, b * HP + g + 1)
                    after(dve, inv_out, b * HP + g + 1)
                    dve.tensor_tensor(attn_t[:, g], attn_ps[:], inv_t[:], ALU.mult).then_inc(normed, 1)

                def empty(n):
                    f = fill_of(n)
                    if f and f[0] == "qk":
                        low(f[1], f[2], spare_ps[:])
                    elif f and f[0] == "inverse":
                        norm(f[1])
                    elif f:
                        c = f[2]
                        after(dve, v_made, b * HP * 2 + 2 * g + c + 1)
                        after(dve, attended, b * HP + g)
                        dve.scalar_tensor_tensor(v_g[:, 4 * c:4 * c + 4], spare_ps[:].rearrange("p (i o) -> p i o", o=P),
                                                 UNSCALE, factor_b[:, 4 * c:4 * c + 4].unsqueeze(2).to_broadcast([P, 4, P]),
                                                 ALU.mult, ALU.mult).then_inc(v_out, 1)

                after(dve, v_out, b * HP * 2)
                dve.tensor_copy(factor_b[:].unsqueeze(1), keep["factor"][:, 1, bass.ds(b, 1)]).then_inc(factor_set, 1)
                for i in range(QT):
                    dve.wait_ge(rows_turned_out, b * QT + i + 1)
                    dve.scalar_tensor_tensor(xq_t[:, :, i, 1], turn_ps[:, i % 2], Y_SCALE, xq_t[:, :, i, 0],
                                             ALU.mult, ALU.subtract).then_inc(rows_low, 1)
                for n in range(3):
                    low(0, n, score_ps[:, n // 2, n % 2 * 512:n % 2 * 512 + 512])
                dve.wait_ge(factor_set, b + 1)
                least(0)
                least(1)
                for n in range(ALL):
                    g, s = divmod(n, STEPS)
                    empty(n - 1)
                    if n + 2 < ALL:
                        least(n + 2)
                    if s == 0:
                        after(dve, attended, b * HP + max(g - 1, 0))
                    dve.wait_ge(turn_b, b * ALL + n + 1)
                    dve.tensor_copy(prob_t[:, g % 2, n % 2, 4:8, s // 2 * P:s // 2 * P + P], turn_ps[:, 1]
                                    ).then_inc(out_b, 1)
                    if s == 0 and g:
                        invert(g - 1)
                empty(ALL - 1)
                invert(HP - 1)
                norm(HP - 1)
                after(dve, combined, b)
                dve.tensor_copy(place_b[:].unsqueeze(1), keep["row"][:, bass.ds(b, 1)]).then_inc(placed, 1)
                dve.tensor_copy(gate_b[:].unsqueeze(1), keep["q_gate"][:, bass.ds(b, 1)]).then_inc(placed, 1)
            dve.wait_ge(placed, 2 * B)
            dve.wait_ge(mid_in, B * 16)
            for c in range(LC):
                dve.wait_ge(last_in[c], NT // LC * 16)
                for i in range(c * NT // LC, (c + 1) * NT // LC):
                    dve.scalar_tensor_tensor(mid[:, i], routed[:, i], gate_b[:, i:i + 1], mid[:, i],
                                             ALU.mult, ALU.add).then_inc(last_added, 1)

        @block.tensor
        def _(pe):
            prime(pe, scored, inv_turned, attended, v_made)
            with pe.Fori(0, B) as b:
                def project(g, n, out):
                    w, src = (0, xq_t[:]) if n == 0 else (1, y_t[:, :, (n - 1) * 4:n * 4])
                    for k in range(KT):
                        for h, (a, c) in enumerate(HALVES):
                            ins = pe.matmul(out.rearrange("p (t c) -> p t c", c=P), w_qk[:, w, k, a], src[:, k, :, c],
                                            start=k == 0 and h == 0, stop=k == KT - 1 and h == 2)
                    ins.then_inc(made, 1)

                def emptied(f):
                    kind, g, c = f
                    if kind == "qk":
                        after(pe, low_done, b * PARTS + 3 * g + c + 1)
                    elif kind == "v":
                        after(pe, v_out, b * HP * 2 + 2 * g + c + 1)
                    else:
                        after(pe, inv_out, b * HP + g + 1)

                def fill(f):
                    kind, g, c = f
                    if kind == "qk":
                        pe.wait_ge(w_qk_in, (b * HP + g + 1) * 16)
                        project(g, c, spare_ps[:])
                    elif kind == "v":
                        pe.wait_ge(w_v_in, (b * HP + g + 1) * 16)
                        for i in range(4):
                            for k in range(KT):
                                for h, (a, e) in enumerate(HALVES):
                                    ins = pe.matmul(spare_ps[:, i * P:(i + 1) * P], y_t[:, k, 4 * c + i, a], w_v[:, k, e],
                                                    start=k == 0 and h == 0, stop=k == KT - 1 and h == 2)
                        ins.then_inc(v_made, 1)
                    else:
                        after(pe, widened, b * HP + g + 1)
                        for q in range(QT):
                            ins = pe.transpose(spare_ps[:, q * P:(q + 1) * P],
                                               inv_wide[:, 2 * q:2 * q + 2].rearrange("p h d -> p (h d)"), keep["ident"][:])
                        ins.then_inc(inv_turned, 1)

                def score(n):
                    g, s = divmod(n, STEPS)
                    qt, h = divmod(s, 2)
                    if n >= 2:
                        after(pe, exped, b * ALL + n - 1)
                    if s == 0:
                        pe.wait_ge(stack_in, (b * HP + g + 1) * STACK)
                    for c in range(2):
                        for half in range(2):
                            ins = pe.matmul(score_ps[:, n % 2, c * 512:(c + 1) * 512],
                                            q_stack[:, g % 2, h, qt * P:(qt + 1) * P],
                                            k_stack[:, g % 2, half, h, c * 512:(c + 1) * 512],
                                            start=half == 0, stop=half == 1)
                    ins.then_inc(scored, 1)

                def attend(g, first, last):
                    if first == 0:
                        after(pe, out_a, b * ALL + (g + 1) * STEPS)
                        after(pe, out_b, b * ALL + (g + 1) * STEPS)
                        after(pe, normed, b * HP + g)
                        after(pe, v_out, b * HP * 2 + 2 * g + 2)
                    for k in range(first, last):
                        for h in range(2):
                            ins = pe.matmul(attn_ps[h * FD:(h + 1) * FD], v_g[:, k, h * FD:(h + 1) * FD],
                                            prob_t[:, g % 2, h, k], start=k == 0, stop=k == NT - 1)
                    if last == NT:
                        ins.then_inc(attended, 1)

                pe.wait_ge(rows_in, (b + 1) * 16)
                after(pe, out_a, b * ALL)
                after(pe, out_b, b * ALL)
                for i in range(QT):
                    if i >= 2:
                        pe.wait_ge(rows_low, b * QT + i - 1)
                    for k in range(KT):
                        ins = pe.transpose(turn_ps[:, i % 2, k], q_rows[:, i, k * P:(k + 1) * P], keep["ident"][:])
                    ins.then_inc(rows_turned, 1)
                pe.wait_ge(y_in, (b + 1) * 16)
                pe.wait_ge(rows_low, (b + 1) * QT)
                after(pe, proj_out, b * QT)
                pe.wait_ge(w_qk_in, (b * HP + 1) * 16)
                for n in range(3):
                    project(0, n, score_ps[:, n // 2, n % 2 * 512:n % 2 * 512 + 512])
                after(pe, low_done, b * PARTS + 3)
                after(pe, inv_out, b * HP)
                score(0)
                score(1)
                last = None
                for n in range(ALL):
                    g, s = divmod(n, STEPS)
                    if n + 2 < ALL:
                        score(n + 2)
                    after(pe, exped, b * ALL + n + 1)
                    for h, (sem, out) in enumerate(((turn_a, out_a), (turn_b, out_b))):
                        after(pe, out, b * ALL + n)
                        for k in range(4):
                            ins = pe.transpose(turn_ps[:, h, k], prob[:, n % 3, (4 * h + k) * P:(4 * h + k + 1) * P],
                                               keep["ident"][:])
                        ins.then_inc(sem, 1)
                    if g and s in ATTEND_AT:
                        attend(g - 1, *ATTEND_AT[s])
                    f = fill_of(n)
                    if f:
                        if last:
                            emptied(last)
                        fill(f)
                        last = f
                emptied(last)
                attend(HP - 1, 0, NT)
                fill(("inverse", HP - 1, 0))
                pe.wait_ge(wo_in, 16)
                after(pe, normed, (b + 1) * HP)
                after(pe, exped, (b + 1) * ALL)
                for i in range(QT):
                    if i >= 2:
                        after(pe, proj_out, b * QT + i - 1)
                    for k in range(HP):
                        ins = pe.matmul(score_ps[:, i % 2, 0:D], attn_t[:, k, i * P:(i + 1) * P], w_o[:, k],
                                        start=k == 0, stop=k == HP - 1)
                    ins.then_inc(projected, 1)


def build(nc, t, phases=9):
    def scratch(name, shape, dt=F32):
        t[name] = nc.dram_tensor(name, shape, dt, kind="Internal").ap()

    scratch("xattn_wt", [NG, 3, P, KT, 2, P], F16)
    scratch("xattn_wo_t", [P, KT, D])
    scratch("heavy_wt", [HP, 3, P, KT, 2, P], F16)
    for name in ("x1", "yn"):
        scratch(name, [B, S, D])
    scratch("yn_t", [B, P, KT, NT, 2, P], F16)
    for way, width in (("k", S), ("q0", S // 2), ("q1", S // 2)):
        scratch(f"halves_{way}", [2, P, width], F16)
    scratch("mid", [B, S, D])
    scratch("scores", [B * NT, P])
    scratch("q_rows", [B * NQ, D])
    scratch("h_rows", [NQ, D])
    with ExitStack() as ctx:
        m = Memory(nc, ctx, "keep")
        keep = {
            "passed": m.sem("passed"), "ident": m.sb("ident", [P, P]), "ones": m.sb("ones", [P, P]),
            "before": m.sb("before", [P, P]), "after": m.sb("after", [P, P]),
            "minus_half": m.sb("minus_half", [P, NT]), "slopes": m.sb("slopes", [P, XH]),
            "gates": m.sb("gates", [P, 2]), "gammas": m.sb("gammas", [P, 2, KT]), "route_s": m.sb("route_s", [P, 2, B, NT]),
            "factor": m.sb("factor", [P, 2, B, NT]), "q_gate": m.sb("q_gate", [P, B, NT]),
            "place": m.sb("place", [P, B, NT], I32),
        }
        prepare_weights(nc, t, keep)
        if phases >= 1:
            cross_attention(nc, t, keep, B if phases > 1 else 1)
        keep["row"] = m.sb("row", [P, B, NT])
        if phases >= 2:
            light_attention_and_route(nc, t, keep)
        if phases >= 3:
            heavy_attention(nc, t, keep)


INPUTS = ["x", "ctx_1024", "itok_BxS_8_8191", "itok_BxS2_1_8191", "mask_BxSxS2_if1", "g_xattn", "g_ffn",
          "L0_xattn_W_q", "L0_xattn_W_k", "L0_xattn_W_v", "L0_xattn_W_o", "L0_ffn_gamma_light", "L0_ffn_wq_light",
          "L0_ffn_wkv_light", "L0_ffn_wo_light", "L0_ffn_q_routing_token", "L0_ffn_kv_routing_token",
          "L0_ffn_gamma_heavy", "L0_ffn_wq_heavy", "L0_ffn_wkv_heavy", "L0_ffn_wo_heavy"]


def kernel(**inputs):
    import concourse.bacc as bacc
    from concourse.bass_utils import run_bass_kernel_spmd

    nc = bacc.Bacc("TRN2", target_bir_lowering=False, num_devices=1)
    arrays, t = {}, {}
    for name in INPUTS:
        a = np.ascontiguousarray(inputs[name])
        arrays[f"in_{name}"] = a
        t[name] = nc.dram_tensor(f"in_{name}", a.shape, mybir.dt.from_np(a.dtype), kind="ExternalInput").ap()
    t["out"] = nc.dram_tensor("out", (B, S, D), F32, kind="ExternalOutput").ap()
    build(nc, t)
    r = run_bass_kernel_spmd(nc, [arrays], core_ids=[0])
    return r.results[0]["out"]
```
